# Optimizing a Trainium2 kernel written in Bass

```python
import numpy as np
import jax
import jax.numpy as jnp

def _softmax(x, axis=-1):
    return jax.nn.softmax(x, axis=axis)

def _gelu(x):
    return jax.nn.gelu(x, approximate=True)

def _silu(x):
    return jax.nn.silu(x)

def _sigmoid(x):
    return jax.nn.sigmoid(x)

def _layernorm(x, axis=-1, eps=1e-05):
    m = jnp.mean(x, axis=axis, keepdims=True)
    v = jnp.var(x, axis=axis, keepdims=True)
    return (x - m) / jnp.sqrt(v + eps)

def _scatter_add(tgt, idx, src, axis=0):
    return tgt.at[idx].add(src)

def _segment_sum(src, seg, n):
    return jax.ops.segment_sum(src, seg, n)
kernel_name = 'mk_gnn_preln_d4_gnn_r32_fdc2c3'

def setup_inputs(seed: int=0):
    np.random.seed(seed)
    _w = jnp.asarray

    def _rec_inputs():
        import jax
        import jax.numpy as jnp
        _gk = jax.random.key(seed)
        x = -0.000202 + 1 * jax.random.normal(jax.random.fold_in(_gk, 1), (3125, 128), jnp.float32)
        src = jax.random.randint(jax.random.fold_in(_gk, 2), (50000,), 0, 3125, jnp.int32)
        dst = jax.random.randint(jax.random.fold_in(_gk, 3), (50000,), 0, 3125, jnp.int32)
        _o = jnp.argsort(dst, stable=True)
        src = src[_o]
        dst = dst[_o]
        edge_type_3 = jax.random.randint(jax.random.fold_in(_gk, 13), (50000,), 0, 3, jnp.int32)
        node_type_3 = jax.random.randint(jax.random.fold_in(_gk, 14), (3125,), 0, 3, jnp.int32)
        return (x, src, dst, edge_type_3, node_type_3)
    x, src, dst, edge_type_3, node_type_3 = _rec_inputs()

    def _L0_gnn_setup():
        import jax, jax.numpy as jnp
        import numpy as np
        N_NODES = 50000
        N_EDGES = 25000
        D_FEAT = 128
        HIDDEN = 128
        BN_EPS = 1e-05

        def _gcn_conv(h, row, col, norm, W, b, n_nodes):
            m = norm[:, None] * (h @ W)[row]
            return jax.ops.segment_sum(m, col, num_segments=n_nodes) + b
        key = jax.random.key(seed)
        ks = jax.random.split(key, 12)
        s_in = 1.0 / np.sqrt(D_FEAT)
        s_h = 1.0 / np.sqrt(HIDDEN)
        return {'x': jax.random.normal(ks[0], (N_NODES, D_FEAT), dtype=jnp.float32), 'edge_index': jax.random.randint(ks[1], (2, N_EDGES), 0, N_NODES, dtype=jnp.int64), 'W_enc': jax.random.uniform(ks[2], (D_FEAT, HIDDEN), jnp.float32, -s_in, s_in), 'b_enc': jax.random.uniform(ks[3], (HIDDEN,), jnp.float32, -s_in, s_in), 'bn_gamma': 1.0 + 0.1 * jax.random.normal(ks[4], (HIDDEN,), jnp.float32), 'bn_beta': 0.1 * jax.random.normal(ks[5], (HIDDEN,), jnp.float32), 'bn_mean': 0.1 * jax.random.normal(ks[6], (HIDDEN,), jnp.float32), 'bn_var': jnp.ones((HIDDEN,), jnp.float32), 'W1': jax.random.uniform(ks[7], (HIDDEN, HIDDEN), jnp.float32, -s_h, s_h), 'b1': jnp.zeros((HIDDEN,), jnp.float32), 'W2': jax.random.uniform(ks[8], (HIDDEN, HIDDEN), jnp.float32, -s_h, s_h), 'b2': jnp.zeros((HIDDEN,), jnp.float32)}
    _L0_gnn_all = _L0_gnn_setup()
    _L0_gnn_in = {k: v for k, v in _L0_gnn_all.items() if k in ('W_enc', 'b_enc', 'bn_gamma', 'bn_beta', 'bn_mean', 'bn_var', 'W1', 'b1', 'W2', 'b2')}
    del _L0_gnn_all

    def _L1_gnn_setup():
        import jax, jax.numpy as jnp
        import numpy as np
        N_NODES = 3125
        N_EDGES = 18750
        H = 128
        NUM_STEPS = 5
        key = jax.random.key(seed)
        ks = jax.random.split(key, 8)
        s = 0.05
        return {'x': jax.random.normal(ks[0], (N_NODES, H), dtype=jnp.float32), 'edge_index': jax.random.randint(ks[1], (2, N_EDGES), 0, N_NODES, dtype=jnp.int64), 'W_msg': jax.random.normal(ks[2], (H, H), dtype=jnp.float32) * s, 'b_msg': jax.random.normal(ks[3], (H,), dtype=jnp.float32) * s, 'W_ih': jax.random.normal(ks[4], (3 * H, H), dtype=jnp.float32) * s, 'W_hh': jax.random.normal(ks[5], (3 * H, H), dtype=jnp.float32) * s, 'b_ih': jax.random.normal(ks[6], (3 * H,), dtype=jnp.float32) * s, 'b_hh': jax.random.normal(ks[7], (3 * H,), dtype=jnp.float32) * s}
    _L1_gnn_all = _L1_gnn_setup()
    _L1_gnn_in = {k: v for k, v in _L1_gnn_all.items() if k in ('W_msg', 'b_msg', 'W_ih', 'W_hh', 'b_ih', 'b_hh')}
    del _L1_gnn_all

    def _L2_gnn_setup():
        import jax, jax.numpy as jnp
        import numpy as np
        N_NODES = 3125

        def _deg_inv_sqrt(idx, n):
            deg = jax.ops.segment_sum(jnp.ones(idx.shape, jnp.float32), idx, num_segments=n)
            deg = jnp.clip(deg, 1.0)
            return jax.lax.rsqrt(deg)

        def _graph_conv(h, W, b, src, dst, out_norm, in_norm, n):
            h = h * out_norm[:, None]
            h = h @ W
            msg = jnp.take(h, src, axis=0)
            agg = jax.ops.segment_sum(msg, dst, num_segments=n)
            return jax.nn.relu(agg * in_norm[:, None] + b)
        key = jax.random.key(seed)
        ks = jax.random.split(key, 5)
        E = 50000
        return {'features': jax.random.normal(ks[0], (N_NODES, 128), jnp.float32), 'src': jax.random.randint(ks[1], (E,), 0, N_NODES, jnp.int32), 'dst': jax.random.randint(ks[2], (E,), 0, N_NODES, jnp.int32), 'W1': jax.random.normal(ks[3], (128, 128), jnp.float32) * (1.0 / np.sqrt(128)), 'b1': jnp.zeros((128,), jnp.float32), 'W2': jax.random.normal(ks[4], (128, 128), jnp.float32) * (1.0 / np.sqrt(128)), 'b2': jnp.zeros((128,), jnp.float32)}
    _L2_gnn_all = _L2_gnn_setup()
    _L2_gnn_in = {k: v for k, v in _L2_gnn_all.items() if k in ('W1', 'b1', 'W2', 'b2')}
    del _L2_gnn_all

    def _L3_gnn_setup():
        import jax, jax.numpy as jnp
        import numpy as np
        N_NODES = 50000
        N_EDGES = 25000
        D = 128
        T = 3
        NODE_IN = D + T * D
        key = jax.random.key(seed)
        ks = jax.random.split(key, 8)
        scale = 0.05
        return {'node_feature': jax.random.normal(ks[0], (N_NODES, D), jnp.float32), 'W_e': jax.random.normal(ks[1], (T, D, D), jnp.float32) * scale, 'b_e': jnp.zeros((T, D), jnp.float32), 'W_n': jax.random.normal(ks[2], (T, D, NODE_IN), jnp.float32) * scale, 'b_n': jnp.zeros((T, D), jnp.float32), 'edge_src': jax.random.randint(ks[3], (N_EDGES,), 0, N_NODES, jnp.int32), 'edge_dst': jax.random.randint(ks[4], (N_EDGES,), 0, N_NODES, jnp.int32), 'edge_type': jax.random.randint(ks[5], (N_EDGES,), 0, T, jnp.int32), 'node_type': jax.random.randint(ks[6], (N_NODES,), 0, T, jnp.int32)}
    _L3_gnn_all = _L3_gnn_setup()
    _L3_gnn_in = {k: v for k, v in _L3_gnn_all.items() if k in ('W_e', 'b_e', 'W_n', 'b_n')}
    del _L3_gnn_all
    return {'x': x, 'src': src, 'dst': dst, 'edge_type_3': edge_type_3, 'node_type_3': node_type_3, 'L0_gnn_W_enc': _L0_gnn_in['W_enc'], 'L0_gnn_b_enc': _L0_gnn_in['b_enc'], 'L0_gnn_bn_gamma': _L0_gnn_in['bn_gamma'], 'L0_gnn_bn_beta': _L0_gnn_in['bn_beta'], 'L0_gnn_bn_mean': _L0_gnn_in['bn_mean'], 'L0_gnn_bn_var': _L0_gnn_in['bn_var'], 'L0_gnn_W1': _L0_gnn_in['W1'], 'L0_gnn_b1': _L0_gnn_in['b1'], 'L0_gnn_W2': _L0_gnn_in['W2'], 'L0_gnn_b2': _L0_gnn_in['b2'], 'L1_gnn_W_msg': _L1_gnn_in['W_msg'], 'L1_gnn_b_msg': _L1_gnn_in['b_msg'], 'L1_gnn_W_ih': _L1_gnn_in['W_ih'], 'L1_gnn_W_hh': _L1_gnn_in['W_hh'], 'L1_gnn_b_ih': _L1_gnn_in['b_ih'], 'L1_gnn_b_hh': _L1_gnn_in['b_hh'], 'L2_gnn_W1': _L2_gnn_in['W1'], 'L2_gnn_b1': _L2_gnn_in['b1'], 'L2_gnn_W2': _L2_gnn_in['W2'], 'L2_gnn_b2': _L2_gnn_in['b2'], 'L3_gnn_W_e': _L3_gnn_in['W_e'], 'L3_gnn_b_e': _L3_gnn_in['b_e'], 'L3_gnn_W_n': _L3_gnn_in['W_n'], 'L3_gnn_b_n': _L3_gnn_in['b_n']}

def reference(x, src, dst, edge_type_3, node_type_3, L0_gnn_W_enc, L0_gnn_b_enc, L0_gnn_bn_gamma, L0_gnn_bn_beta, L0_gnn_bn_mean, L0_gnn_bn_var, L0_gnn_W1, L0_gnn_b1, L0_gnn_W2, L0_gnn_b2, L1_gnn_W_msg, L1_gnn_b_msg, L1_gnn_W_ih, L1_gnn_W_hh, L1_gnn_b_ih, L1_gnn_b_hh, L2_gnn_W1, L2_gnn_b1, L2_gnn_W2, L2_gnn_b2, L3_gnn_W_e, L3_gnn_b_e, L3_gnn_W_n, L3_gnn_b_n):
    import jax
    import jax.numpy as jnp

    def _L0_gnn_ref(x, edge_index, W_enc, b_enc, bn_gamma, bn_beta, bn_mean, bn_var, W1, b1, W2, b2):
        import jax, jax.numpy as jnp
        import numpy as np
        N_NODES = 50000
        N_EDGES = 25000
        D_FEAT = 128
        HIDDEN = 128
        BN_EPS = 1e-05

        def _gcn_conv(h, row, col, norm, W, b, n_nodes):
            m = norm[:, None] * (h @ W)[row]
            return jax.ops.segment_sum(m, col, num_segments=n_nodes) + b
        n = x.shape[0]
        loops = jnp.arange(n, dtype=edge_index.dtype)
        row = jnp.concatenate([edge_index[0], loops])
        col = jnp.concatenate([edge_index[1], loops])
        deg = jax.ops.segment_sum(jnp.ones(row.shape[0], jnp.float32), col, num_segments=n)
        dis = jnp.where(deg > 0, jax.lax.rsqrt(jnp.maximum(deg, 1.0)), 0.0)
        norm = dis[row] * dis[col]
        h = jax.nn.relu(x @ W_enc + b_enc)
        h = (h - bn_mean) * jax.lax.rsqrt(bn_var + BN_EPS) * bn_gamma + bn_beta
        h = _gcn_conv(h, row, col, norm, W1, b1, n)
        h = jax.nn.relu(h)
        h = _gcn_conv(h, row, col, norm, W2, b2, n)
        return h

    def _L1_gnn_ref(x, edge_index, W_msg, b_msg, W_ih, W_hh, b_ih, b_hh):
        import jax, jax.numpy as jnp
        import numpy as np
        N_NODES = 3125
        N_EDGES = 18750
        H = 128
        NUM_STEPS = 5
        num_nodes = x.shape[0]
        row, col = (edge_index[0], edge_index[1])

        def step(h, _):
            messages = h[col] @ W_msg.T + b_msg
            agg = jax.ops.segment_sum(messages, row, num_segments=num_nodes)
            gi = agg @ W_ih.T + b_ih
            gh = h @ W_hh.T + b_hh
            i_r, i_z, i_n = jnp.split(gi, 3, axis=-1)
            h_r, h_z, h_n = jnp.split(gh, 3, axis=-1)
            r = jax.nn.sigmoid(i_r + h_r)
            z = jax.nn.sigmoid(i_z + h_z)
            n = jnp.tanh(i_n + r * h_n)
            h_new = (1.0 - z) * n + z * h
            return (h_new, None)
        h, _ = jax.lax.scan(step, x, None, length=NUM_STEPS)
        return h

    def _L2_gnn_ref(features, src, dst, W1, b1, W2, b2):
        import jax, jax.numpy as jnp
        import numpy as np
        N_NODES = 3125

        def _deg_inv_sqrt(idx, n):
            deg = jax.ops.segment_sum(jnp.ones(idx.shape, jnp.float32), idx, num_segments=n)
            deg = jnp.clip(deg, 1.0)
            return jax.lax.rsqrt(deg)

        def _graph_conv(h, W, b, src, dst, out_norm, in_norm, n):
            h = h * out_norm[:, None]
            h = h @ W
            msg = jnp.take(h, src, axis=0)
            agg = jax.ops.segment_sum(msg, dst, num_segments=n)
            return jax.nn.relu(agg * in_norm[:, None] + b)
        n = features.shape[0]
        out_norm = _deg_inv_sqrt(src, n)
        in_norm = _deg_inv_sqrt(dst, n)
        h = _graph_conv(features, W1, b1, src, dst, out_norm, in_norm, n)
        h = _graph_conv(h, W2, b2, src, dst, out_norm, in_norm, n)
        return h

    def _L3_gnn_ref(node_feature, W_e, b_e, W_n, b_n, edge_src, edge_dst, edge_type, node_type):
        import jax, jax.numpy as jnp
        import numpy as np
        N_NODES = 50000
        N_EDGES = 25000
        D = 128
        T = 3
        NODE_IN = D + T * D
        N, Din = node_feature.shape
        n_types = W_e.shape[0]
        out_dim = W_e.shape[1]
        src = node_feature[edge_src]
        parts = [jax.nn.relu(node_feature)]
        for t in range(n_types):
            msg = jax.nn.relu(src @ W_e[t].T + b_e[t])
            msg = jnp.where((edge_type == t)[:, None], msg, jnp.zeros((), msg.dtype))
            parts.append(jax.ops.segment_sum(msg, edge_dst, num_segments=N))
        agg = jnp.concatenate(parts, axis=1)
        updated = jnp.zeros((N, out_dim), node_feature.dtype)
        for t in range(n_types):
            o = agg @ W_n[t].T + b_n[t]
            updated = jnp.where((node_type == t)[:, None], o, updated)
        return updated + node_feature
    edge_index = jnp.stack([src, dst])
    h = jnp.maximum(_layernorm(x, axis=-1), 0.0)
    x = x + _L0_gnn_ref(h, edge_index, L0_gnn_W_enc, L0_gnn_b_enc, L0_gnn_bn_gamma, L0_gnn_bn_beta, L0_gnn_bn_mean, L0_gnn_bn_var, L0_gnn_W1, L0_gnn_b1, L0_gnn_W2, L0_gnn_b2)
    h = jnp.maximum(_layernorm(x, axis=-1), 0.0)
    x = x + _L1_gnn_ref(h, edge_index, L1_gnn_W_msg, L1_gnn_b_msg, L1_gnn_W_ih, L1_gnn_W_hh, L1_gnn_b_ih, L1_gnn_b_hh)
    h = jnp.maximum(_layernorm(x, axis=-1), 0.0)
    x = x + _L2_gnn_ref(h, src, dst, L2_gnn_W1, L2_gnn_b1, L2_gnn_W2, L2_gnn_b2)
    h = jnp.maximum(_layernorm(x, axis=-1), 0.0)
    x = x + _L3_gnn_ref(h, L3_gnn_W_e, L3_gnn_b_e, L3_gnn_W_n, L3_gnn_b_n, src, dst, edge_type_3, node_type_3)
    return x

_drawn_inputs = setup_inputs


def setup_inputs(seed=0):
    import zlib

    import numpy as np

    out = dict(_drawn_inputs(seed))
    spreads = {'L0_gnn_bn_var': (1.0, 0.6),
     'L0_gnn_b1': (0.0, 0.1),
     'L0_gnn_b2': (0.0, 0.1),
     'L2_gnn_b1': (0.0, 0.1),
     'L2_gnn_b2': (0.0, 0.1),
     'L3_gnn_b_e': (0.0, 0.1),
     'L3_gnn_b_n': (0.0, 0.1)}
    factors = {'L0_gnn_b_enc': 3.836, 'L0_gnn_bn_gamma': 2.758}
    for name, (base, spread) in spreads.items():
        noise = np.random.default_rng([zlib.crc32(name.encode()), seed]).standard_normal(out[name].shape)
        drawn = base * np.exp(spread * noise) if base else spread * noise
        out[name] = jnp.asarray(drawn.astype(out[name].dtype))
    for name, factor in factors.items():
        out[name] = (out[name] * factor).astype(out[name].dtype)
    return out
```

```python
from contextlib import ExitStack

import concourse.bass as bass
from concourse import mybir

F32 = mybir.dt.float32
BF16 = mybir.dt.bfloat16
F16 = mybir.dt.float16
I32 = mybir.dt.int32
ALU = mybir.AluOpType
ACT = mybir.ActivationFunctionType
AX = mybir.AxisListType.X

P = 128
N = 3125
E = 50000
D = 128
TN = 125
NT = N // TN
GT = 5
NG = NT // GT
GN = GT * TN
H0, H1 = 3 * TN, 2 * TN
AG0 = 512 - H0
NCH = -(-E // P)
LEAD = 4
NCP = 400
WIN = 25
GP = 15632
SPLITS = 3
EPS = 1e-5
STEPS = 5
TYPES = 3

DEG_IN, CONV0, CONV1, DEG_OUT, GRU0 = 0, 1, 2, 3, 4
CONV2 = GRU0 + STEPS
CONV3 = CONV2 + 1
TYPE0 = CONV3 + 1
FEAT = {CONV0: 0, CONV1: 1, CONV2: 2 + STEPS, CONV3: 3 + STEPS}
FEAT_GRU0 = 2
FEAT_TYPE0 = 4 + STEPS
(V_BENC, V_GAMMA, V_BETA, V_MEAN, V_VAR, V_B01, V_B02, V_BMSG, V_BIR, V_BIZ, V_BIN, V_BHR, V_BHZ, V_BHN,
 V_B21, V_B22, V_BR, V_BZ, V_SCALE, V_SHIFT, V_STD, V_EPS) = range(22)
NV = 16
W_ENC, W_01, W_02, W_MSG, W_IR, W_IZ, W_IN, W_HR, W_HZ, W_HN, W_21, W_22, W_E, W_N = 0, 1, 2, 3, 4, 5, 6, 7, 8, 9, 10, 11, 12, 15


def gnn_kernel(nc, x, src, dst, etype, ntype, vecs, wts, be, bn, out):
    with ExitStack() as ctx:
        def sb(name, shape, dt):
            return ctx.enter_context(nc.sbuf_tensor(name, shape, dt))

        def sem(name):
            return ctx.enter_context(nc.semaphore(name))

        xs = nc.dram_tensor("x_between", (N, D), F32, kind="Internal").ap()
        aggd = nc.dram_tensor("typed_sums", (TYPES, P, N), F32, kind="Internal").ap()
        degd = nc.dram_tensor("degrees", (2, N), F32, kind="Internal").ap()
        normd = nc.dram_tensor("norms", (3, N), F32, kind="Internal").ap()
        hrows = nc.dram_tensor("feature_rows", (N, SPLITS * D), BF16, kind="Internal").ap()
        hrows16 = nc.dram_tensor("feature_rows16", (N, 2 * D), F16, kind="Internal").ap()
        keyd = nc.dram_tensor("edge_keys", (5, P, NCP), F32, kind="Internal").ap()
        idxd = nc.dram_tensor("edge_rows", (2, P, NCP), I32, kind="Internal").ap()

        adj = sb("counts", [P, NG * GP], BF16)
        H = sb("H", [P, NT * SPLITS * D], BF16)
        hT = sb("hT", [P, N], F32)
        A, B, C, DB, X = (sb(f"buf{c}", [P, 640], F32) for c in "ABCDX")
        W = sb("W", [P, 7, D], F32)
        rec = sb("rec", [P, 3, NT, NT], BF16)
        identf = sb("identf", [P, P], F32)
        identb = sb("identb", [P, P], BF16)
        ones = sb("ones", [P, P], BF16)
        zeros = sb("zeros", [P, P], BF16)
        iota1 = sb("iota1", [P, P], BF16)
        iotat = sb("iotat", [P, NT], F32)
        beb = sb("beb", [P, TYPES, D], F32)
        vec = sb("vec", [P, 22], F32)
        stats = sb("stats", [P, GT, 6], F32)
        mv = sb("mv", [P, GT, 2], F32)
        rstd = sb("rstd", [P, GT], F32)
        occs = sb("occs", [P, 4], F32)
        flag = sb("flag", [P, 1], I32)

        def place(base, at, shape, dt):
            size = 1
            for s in shape:
                size *= s
            elems = size * (2 if dt in (F32, I32) else 1)
            ap = base[:, at // 2:at // 2 + elems]
            if dt != BF16:
                ap = ap.bitcast(dt)
            if len(shape) == 2:
                ap = ap.rearrange("p (a b) -> p a b", b=shape[1])
            if len(shape) == 3:
                ap = ap.rearrange("p (a b c) -> p a b c", b=shape[1], c=shape[2])
            return ap

        raw = place(adj, 0, (3, 4, P), I32)
        rawf = place(adj, 6144, (3, 4, P), F32)
        ef = place(adj, 12288, (3, NCP), F32)
        qi = place(adj, 17088, (2, NCP), I32)
        qf = place(adj, 20288, (2, NCP), F32)
        val = place(adj, 26688, (3, NCP), BF16)
        stile = place(adj, 29088, (NCP,), BF16)
        V = place(adj, 29888, (4 * NT, NCP), BF16)
        M = place(adj, 29888 + 3 * NT * NCP * 2, (NT, NCP), BF16)
        U = place(adj, 109888, (4, NCP), BF16)
        tri = place(adj, 113088, (P,), BF16)
        ct = place(adj, 113344, (4, NT), BF16)
        gsel = place(adj, 113600, (NT, NCP), F32)
        oslot = place(adj, 113600, (2, WIN, P), BF16)
        gsum = place(adj, 0, (NCP,), I32)
        gslot = place(adj, 1600, (NCP,), I32)
        slot1 = place(adj, 3200, (NCP,), F32)
        slotb = place(adj, 6400, (2, WIN * 4), BF16)
        qrem = place(adj, 23488, (2, NCP), F32)
        onesf = place(adj, 130000, (P,), F32)
        keyf = place(H, 0, (5, NCP), F32)
        idxi = place(H, 8000, (2, NCP), I32)
        idxf = place(H, 11200, (NCP,), F32)
        H16 = place(H, 0, (NT * 2 * D,), F16)
        WN = place(adj, 0, (4, TYPES * D), F32)
        bnb = place(adj, 6144, (TYPES * D,), F32)
        part = place(adj, 8192, (TYPES, GN), F32)
        tmp = place(adj, 16384, (2, TYPES * D), F32)
        ntf = place(adj, 20480, (NT,), F32)
        nti = place(adj, 20608, (NT,), I32)
        mask = place(adj, 20736, (TYPES, NT), F32)

        AG, D0, D1, D2 = (ctx.enter_context(nc.psum_tensor(n, [P, 1024], F32)) for n in ("AG", "D0", "D1", "D2"))

        def nodes(ps):
            return ps[:, AG0:AG0 + GN]

        def half(ap, h):
            return ap[:, 0:H0] if h == 0 else ap[:, H0:GN]

        def tiles(ap, rows=P):
            return ap[0:rows, 0:640].rearrange("p (t n) -> p t n", t=GT)

        def group(ap, g):
            return ap[:, g * GN:(g + 1) * GN]

        def ohring(r):
            return (B, C)[r][:].bitcast(BF16).rearrange("p (i n) -> p i n", n=P)

        dups = DB[:, 0:NT * GT * 4].bitcast(BF16).rearrange("p (j i d) -> p j i d", j=NT, d=4)

        s_pown = sem("s_pown")
        sl_seen = sem("sl_seen")
        s_slotb = sem("s_slotb")
        s_aggf = sem("s_aggf")
        s_pmsg = sem("s_pmsg")
        s_msg = sem("s_msg")
        s_prz = sem("s_prz")
        s_sig = sem("s_sig")
        s_pn = sem("s_pn")
        s_const = sem("s_const")
        s_par = sem("s_par")
        s_w = sem("s_w")
        s_vec = sem("s_vec")
        s_vstd = sem("s_vstd")
        s_rawm = sem("s_rawm")
        s_raw = sem("s_raw")
        s_rawf = sem("s_rawf")
        s_eT = sem("s_eT")
        s_ef = sem("s_ef")
        s_own = sem("s_own")
        s_M = sem("s_M")
        s_ctm = sem("s_ctm")
        s_ct = sem("s_ct")
        s_G = sem("s_G")
        s_gsel = sem("s_gsel")
        s_V = sem("s_V")
        s_osl = sem("s_osl")
        s_rmm = sem("s_rmm")
        s_rec = sem("s_rec")
        s_occ = sem("s_occ")
        s_om = sem("s_om")
        s_omm = sem("s_omm")
        s_flag = sem("s_flag")
        s_kp = sem("s_kp")
        s_key = sem("s_key")
        s_dup = sem("s_dup")
        s_oh = sem("s_oh")
        s_blk = sem("s_blk")
        s_cnt = sem("s_cnt")
        s_xl = sem("s_xl")
        s_xst = sem("s_xst")
        s_xT = sem("s_xT")
        s_xsum = sem("s_xsum")
        s_bn = sem("s_bn")
        s_mv = sem("s_mv")
        s_std = sem("s_std")
        s_rstd = sem("s_rstd")
        s_norm = sem("s_norm")
        s_hTm = sem("s_hTm")
        s_h = sem("s_h")
        s_enc = sem("s_enc")
        s_encr = sem("s_encr")
        s_bnh = sem("s_bnh")
        s_nbl = sem("s_nbl")
        s_pre = sem("s_pre")
        s_nm = sem("s_nm")
        s_ebias = sem("s_ebias")
        s_erelu = sem("s_erelu")
        s_hi = sem("s_hi")
        s_r1 = sem("s_r1")
        s_mid = sem("s_mid")
        s_feat = sem("s_feat")
        s_agg = sem("s_agg")
        s_aggu = sem("s_aggu")
        s_act = sem("s_act")
        s_degst = sem("s_degst")
        s_degl = sem("s_degl")
        s_degf = sem("s_degf")
        s_degs = sem("s_degs")
        s_norms = sem("s_norms")
        s_nst = sem("s_nst")
        s_gmsg = sem("s_gmsg")
        s_gm = sem("s_gm")
        s_grz = sem("s_grz")
        s_gsg = sem("s_gsg")
        s_gn = sem("s_gn")
        s_gown = sem("s_gown")
        s_gpre = sem("s_gpre")
        s_gtanh = sem("s_gtanh")
        s_hnew = sem("s_hnew")
        s_tst = sem("s_tst")
        s_lw = sem("s_lw")
        s_lx = sem("s_lx")
        s_lnt = sem("s_lnt")
        s_lo = sem("s_lo")
        s_lh = sem("s_lh")
        s_lown = sem("s_lown")
        s_lt = sem("s_lt")
        s_ly = sem("s_ly")
        s_out = sem("s_out")
        sl_rows = sem("sl_rows")
        sl_load = sem("sl_load")
        sl_iota = sem("sl_iota")
        sl_idx = sem("sl_idx")
        sl_g = [sem("sl_g0"), sem("sl_g1")]
        sl_oh = sem("sl_oh")
        sl_used = sem("sl_used")

        block = ctx.enter_context(nc.Block())

        SL = NCH + 1
        BLD = NG * NT

        def arena(g):
            b = g * GP * 2
            return dict(key=place(adj, b, (NCP,), F32), idx=place(adj, b + 1600, (NCP,), I32),
                        iota=place(adj, b + 3200, (GN,), F32), oh=place(adj, b + 5728, (2, 640), BF16),
                        rows=place(adj, b + 8320, (2, SPLITS * D), BF16), col=place(adj, b + 10240, (2, 8), I32))

        def run_steps(eng, q, step, prepare=None):
            for g in range(NG):
                if prepare:
                    prepare(g)
                r0 = (q * BLD + g * NT) % 2
                with eng.Fori(0, NT // 2) as i:
                    for r in range(2):
                        step(g * NT + 2 * i + r, (r0 + r) % 2, 2 * i + r, g)
                step(g * NT + NT - 1, r0, NT - 1, g)

        def conv_no(p):
            return (CONV0, CONV1, CONV2, CONV3).index(p)

        def mid_of(hp, g):
            return (0, 1, 7, 8, 9, 10, 11).index(hp) * NG + g

        def key_of(kind, t):
            return {"deg_in": 0, "deg_out": 1, "conv": 0, "gru": 1, "type": 2 + t}[kind]

        def builds_before(kind, p):
            return {"deg_in": 1, "deg_out": 2, "gru": 2}.get(kind) or (1 if kind == "conv" and p < DEG_OUT else 3 if kind == "conv" else 4 + p - TYPE0)

        def norm_used(k):
            q, g = divmod(k, NG)
            return {0: (s_pre, g + 1), 1: (s_aggu, CONV0 * NG + g + 1), 2: (s_pre, NG + g + 1),
                    3: (s_aggu, CONV1 * NG + g + 1), 9: (s_pre, 2 * NG + g + 1), 10: (s_aggu, CONV2 * NG + g + 1),
                    11: (s_pre, 3 * NG + g + 1), 12: (s_aggu, CONV3 * NG + g + 1)}[q]

        NORM_OF = {0: 0, 1: NG, 2: 2 * NG, 3: 3 * NG, "gru": 4 * NG, 9: 9 * NG, 10: 10 * NG, 11: 11 * NG, 12: 12 * NG}
        PRE_NORM = [0, 2, 9, 11]
        CONV_NORM = {CONV0: 1, CONV1: 3, CONV2: 10, CONV3: 12}

        @block.sync
        def _(sp):
            full = 3 * P * P
            sp.wait_ge(s_rawm, 1)
            for k, a in enumerate((src, dst, etype)):
                sp.dma_start(raw[:, k, 0:3, :], a[0:full].rearrange("(b c p) -> c b p", b=3, p=P)).then_inc(s_raw, 16)
                rows = (E - full) // P
                sp.dma_start(raw[0:rows, k, 3, :], a[full:full + rows * P].rearrange("(c p) -> c p", p=P)).then_inc(s_raw, 16)
                sp.dma_start(raw[rows:rows + 1, k, 3, 0:E - full - rows * P],
                             a[full + rows * P:E].rearrange("(c p) -> c p", c=1)).then_inc(s_raw, 16)
            sp.dma_start(vec[:, 0:NV], vecs).then_inc(s_par, 16)
            sp.dma_start(beb[:], be.rearrange("(a t) d -> a t d", a=1).to_broadcast([P, TYPES, D])).then_inc(s_par, 16)
            sp.dma_start(W[:, 0:3, :], wts[:, 0:3, :]).then_inc(s_w, 16)

            def load_x(n):
                q, g = divmod(n, NG)
                if n:
                    sp.wait_ge(s_norm, n)
                if n > NG:
                    sp.wait_ge(s_xst, 16 * (n - NG))
                if n == 2 * NG:
                    sp.wait_ge(s_pmsg, STEPS * NG)
                srcx = x if q < 2 else xs
                sp.dma_start(tiles(X, TN), srcx[g * GN:(g + 1) * GN, :].rearrange("(t p) d -> p t d", p=TN)).then_inc(s_xl, 16)

            def store_x(n):
                g = n % NG
                sp.wait_ge(s_xsum, n - NG + 1)
                sp.dma_start(xs[g * GN:(g + 1) * GN, :].rearrange("(t p) d -> p t d", p=TN), tiles(X, TN)).then_inc(s_xst, 16)

            for n in range(NG):
                load_x(n)

            sp.wait_ge(s_kp, 1)
            sp.dma_start(keyd.rearrange("k p c -> p k c"), keyf).then_inc(s_key, 16)
            sp.dma_start(idxd.rearrange("k p c -> p k c"), idxi).then_inc(s_key, 16)
            sp.wait_ge(s_key, 32)

            sp.wait_ge(s_flag, 1)
            fast = sp.value_load(flag[0:1, 0:1], min_val=0, max_val=1)

            def slow_loads(kind, p, hp, g, t=0):
                with sp.If(fast == 0):
                    a = arena(g)
                    sp.wait_ge(s_cnt, 2 + BLD * builds_before(kind, p))
                    if kind[:3] != "deg" and g == 0:
                        sp.wait_ge(s_feat, hp * NG + NG)
                        if kind == "gru":
                            sp.dma_start(hrows16.rearrange("(t p) d -> p t d", p=TN),
                                         H16[0:TN].rearrange("p (t d) -> p t d", t=NT)).then_inc(sl_rows, 16)
                        else:
                            sp.dma_start(hrows.rearrange("(t p) d -> p t d", p=TN),
                                         H[0:TN].rearrange("p (t d) -> p t d", t=NT)).then_inc(sl_rows, 16)
                    if not (kind == "deg_in" and g == 0):
                        sp.wait_ge(s_agg, p * NG + g)
                    sp.dma_start(a["key"], keyd[key_of(kind, t)]).then_inc(sl_load, 16)
                    sp.dma_start(a["idx"], idxd[1 if kind == "gru" else 0]).then_inc(sl_load, 16)
                with sp.Else():
                    sp.nop()
                sp.nop()

            def degrees(kind, p, d):
                for g in range(NG):
                    slow_loads(kind, p, 0, g)
                    sp.wait_ge(s_aggu, p * NG + g + 1)
                    sp.dma_start(degd[d:d + 1, g * GN:(g + 1) * GN], A[0:1, 0:GN]).then_inc(s_degst, 16)
                    sp.wait_ge(s_degst, 16 * (d * NG + g + 1))
                sp.dma_start(A[0:TN, 0:NT], degd[d, :].rearrange("(t p) -> p t", p=TN), allow_slow_non_contiguous=True).then_inc(s_degl, 16)
                sp.wait_ge(s_norms, d + 1)
                if d == 0:
                    sp.dma_start(normd[0, :].rearrange("(t p) -> p t", p=TN), A[0:TN, 128:128 + NT], allow_slow_non_contiguous=True).then_inc(s_nst, 16)
                sp.dma_start(normd[1 + d, :].rearrange("(t p) -> p t", p=TN), A[0:TN, 192:192 + NT], allow_slow_non_contiguous=True).then_inc(s_nst, 16)
                sp.wait_ge(s_nst, 32 + 16 * d)

            def load_norm(k, row, g, after):
                a = degd[1:2] if row == "deg" else normd[row:row + 1]
                sp.wait_ge(*after)
                sp.dma_start(DB[:, 0:GN], a[:, g * GN:(g + 1) * GN].to_broadcast([P, GN])).then_inc(s_nbl, 16)

            degrees("deg_in", DEG_IN, 0)
            def conv_norms(table, first, builds, n):
                for q, row, p, hp in table:
                    last = p in (CONV1, CONV3)
                    for g in range(NG + 1):
                        if g < NG:
                            if p is not None:
                                slow_loads("conv", p, hp, g)
                            k = q * NG + g
                            load_norm(k, row, g, norm_used(k - 1) if k > first * NG else (s_cnt, 2 + BLD * builds))
                        if last and g:
                            load_x(n + g - 1)
                            store_x(n + g - 1)

            conv_norms(((0, 0, None, None), (1, 0, CONV0, 0), (2, 0, None, None), (3, 0, CONV1, 1)), 0, 1, NG)
            degrees("deg_out", DEG_OUT, 1)
            sp.wait_ge(s_hi, 2 * NG)
            sp.wait_ge(s_xsum, NG)
            sp.dma_start(W[:, 0:7, :], wts[:, W_MSG:W_MSG + 7, :]).then_inc(s_w, 16)

            def gru_sp(s):
                for g in range(NG):
                    slow_loads("gru", GRU0 + s, FEAT_GRU0 + s, g)
                    load_norm(None, "deg", g, (s_msg, s * NG + g) if not (isinstance(s, int) and s == 0 and g == 0) else (s_cnt, 2 + 2 * BLD))

            gru_sp(0)
            with sp.Fori(1, STEPS) as s:
                gru_sp(s)
            for n in range(2 * NG, 3 * NG):
                load_x(n)
                store_x(n)
            sp.wait_ge(s_hnew, STEPS * NG)
            sp.dma_start(W[:, 0:2, :], wts[:, W_21:W_21 + 2, :]).then_inc(s_w, 16)
            conv_norms(((9, 2, None, None), (10, 1, CONV2, 7), (11, 2, None, None), (12, 1, CONV3, 8)), 9, 3, 3 * NG)
            sp.wait_ge(s_feat, FEAT_TYPE0 * NG)
            sp.dma_start(W[:, 0:3, :], wts[:, W_E:W_E + 3, :]).then_inc(s_w, 16)
            for t in range(TYPES):
                for g in range(NG):
                    slow_loads("type", TYPE0 + t, FEAT_TYPE0 + t, g, t)
                    buf = (A, B)[g % 2]
                    sp.wait_ge(s_aggu, (TYPE0 + t) * NG + g + 1)
                    sp.dma_start(group(aggd[t], g), buf[:, 0:GN]).then_inc(s_tst, 16)
            sp.wait_ge(s_agg, (TYPE0 + TYPES) * NG)
            sp.wait_ge(s_tst, 16 * TYPES * NG)
            sp.dma_start(WN, wts[:, W_N:W_N + 12, :].rearrange("p (a b) d -> p a (b d)", a=4)).then_inc(s_lw, 16)
            sp.dma_start(bnb, bn.rearrange("(a t) d -> a (t d)", a=1).to_broadcast([P, TYPES * D])).then_inc(s_lw, 16)
            sp.dma_start(nti[0:TN], ntype.rearrange("(t p) -> p t", p=TN), allow_slow_non_contiguous=True).then_inc(s_lw, 16)
            for g in range(NG):
                if g:
                    sp.wait_ge(s_lo, GT * g)
                    sp.wait_ge(s_out, 16 * g)
                for t in range(TYPES):
                    sp.dma_start(part[:, t, :], group(aggd[t], g)).then_inc(s_lx, 16)
                sp.wait_ge(s_xst, 16 * 3 * NG)
                sp.wait_ge(s_norm, 4 * NG)
                sp.dma_start(tiles(X, TN), xs[g * GN:(g + 1) * GN, :].rearrange("(t p) d -> p t d", p=TN)).then_inc(s_lx, 16)
                sp.wait_ge(s_ly, g + 1)
                sp.dma_start(out[g * GN:(g + 1) * GN, :].rearrange("(t p) d -> p t d", p=TN), tiles(X, TN)).then_inc(s_out, 16)
            sp.wait_ge(s_out, 16 * NG)

        @block.gpsimd
        def _(pool):
            pool.memset(identf[:], 0.0).then_inc(s_pown, 1)
            pool.memset(tri, 1.0).then_inc(s_pown, 1)
            pool.memset(U, 1.0).then_inc(s_pown, 1)
            pool.memset(ones[:], 1.0).then_inc(s_pown, 1)
            pool.memset(zeros[:], 0.0).then_inc(s_pown, 1)
            pool.wait_ge(s_pown, 5)
            pool.affine_select(out=identf[:], in_=identf[:], compare_op=ALU.not_equal, fill=1.0, base=0,
                               pattern=[[-1, P]], channel_multiplier=1).then_inc(s_pown, 1)
            pool.affine_select(out=tri, in_=tri, compare_op=ALU.is_gt, fill=0.0, base=0,
                               pattern=[[1, P]], channel_multiplier=-1).then_inc(s_pown, 1)
            pool.affine_select(out=U, in_=U, compare_op=ALU.is_gt, fill=0.0, base=0,
                               pattern=[[-P, 4], [1, NCP]], channel_multiplier=-1).then_inc(s_pown, 1)
            pool.iota(iota1[:], [[1, P]], base=1, channel_multiplier=0, allow_small_or_imprecise_dtypes=True).then_inc(s_pown, 1)
            pool.iota(iotat[:], [[1, NT]], base=0, channel_multiplier=0, allow_small_or_imprecise_dtypes=True).then_inc(s_pown, 1)
            pool.memset(vec[:, V_EPS:V_EPS + 1], EPS).then_inc(s_pown, 1)
            pool.wait_ge(s_pown, 11)
            pool.tensor_copy(identb[:], identf[:]).then_inc(s_const, 1)

            pool.wait_ge(s_ef, 3)
            pool.tensor_copy(keyf[:, 0, :], ef[:, 1, :]).then_inc(s_pown, 1)
            pool.tensor_copy(keyf[:, 1, :], ef[:, 0, :]).then_inc(s_pown, 1)
            for t in range(TYPES):
                pool.tensor_scalar(keyf[:, 2 + t, :], ef[:, 2, :], float(t), None, ALU.is_equal).then_inc(s_pown, 1)
            pool.tensor_scalar(idxf, ef[:, 1, :], 1.0, None, ALU.add).then_inc(s_pown, 1)
            pool.wait_ge(s_pown, 17)
            for t in range(TYPES):
                pool.tensor_tensor(keyf[:, 2 + t, :], keyf[:, 2 + t, :], idxf, ALU.mult).then_inc(s_pown, 1)
            pool.wait_ge(s_pown, 20)
            for t in range(TYPES):
                pool.tensor_scalar(keyf[:, 2 + t, :], keyf[:, 2 + t, :], -1.0, None, ALU.add).then_inc(s_pown, 1)
            for k in range(2):
                pool.tensor_scalar(idxi[:, k, :], ef[:, k, :], 0.0, None, ALU.max).then_inc(s_pown, 1)
            pool.wait_ge(s_pown, 25)
            pool.nop().then_inc(s_kp, 1)

            pool.wait_ge(s_flag, 1)
            fast = pool.value_load(flag[0:1, 0:1], min_val=0, max_val=1)

            def slow_gathers(kind, p, hp, g):
                with pool.If(fast == 0):
                    a = arena(g)
                    n = p * NG + g
                    pool.wait_ge(sl_load, 32 * (n + 1))
                    pool.sem_inc(sl_seen, 1)
                    pool.iota(a["iota"], [[1, GN]], base=g * GN, channel_multiplier=0,
                              allow_small_or_imprecise_dtypes=True).then_inc(sl_iota, 1)
                    if kind[:3] != "deg":
                        m = hp * NG + g
                        pool.wait_ge(sl_rows, 16 * (hp + 1))
                        pool.sem_inc(sl_seen, 1)
                        with pool.Fori(0, SL // 2) as i:
                            for r in range(2):
                                pool.wait_ge(sl_used, n * SL + 2 * i + r + 1)
                                pool.tensor_copy(a["col"][:, r, 0:1], a["idx"][:, bass.ds(LEAD + 2 * i + r, 1)]).then_inc(sl_idx, 1)
                                pool.wait_ge(sl_idx, m * SL + 2 * i + r + 1)
                                pool.sem_inc(sl_seen, 1)
                                if kind == "gru":
                                    to, table = a["rows"][:, r, 0:2 * D].bitcast(F16), hrows16
                                else:
                                    to, table = a["rows"][:, r, :], hrows
                                pool.indirect_dma_start(out=to, out_offset=None, in_=table,
                                                        in_offset=bass.IndirectOffsetOnAxis(ap=a["col"][:, r, 0:1], axis=0)
                                                        ).then_inc(sl_g[r], 16)
                with pool.Else():
                    pool.nop()
                pool.nop()

            for g in range(NG):
                slow_gathers("deg_in", DEG_IN, 0, g)
            for p, hp in ((CONV0, 0), (CONV1, 1)):
                for g in range(NG):
                    slow_gathers("conv", p, hp, g)
            for g in range(NG):
                slow_gathers("deg_out", DEG_OUT, 0, g)
            with pool.Fori(0, STEPS) as s:
                for g in range(NG):
                    slow_gathers("gru", GRU0 + s, FEAT_GRU0 + s, g)
            for p, hp in ((CONV2, 7), (CONV3, 8)):
                for g in range(NG):
                    slow_gathers("conv", p, hp, g)
            for t in range(TYPES):
                for g in range(NG):
                    slow_gathers("type", TYPE0 + t, FEAT_TYPE0 + t, g)

        @block.tensor
        def _(pe):
            pe.sem_inc(s_blk, 2)
            pe.sem_inc(sl_used, 2)
            pe.wait_ge(s_const, 1)
            pe.wait_ge(s_rawf, 1)
            for k in range(3):
                for b in range(4):
                    mm = pe.transpose((D0, D0, D1)[k][:, 512 * (k % 2) + P * b:512 * (k % 2) + P * (b + 1)], rawf[:, k, b, :], identf[:])
                mm.then_inc(s_eT, 1)
            pe.wait_ge(s_M, NT)
            for b in range(4):
                cols = min(P, NCP - P * b)
                for sh in range(NT):
                    mm = pe.matmul(D1[0:cols, 512 + NT * b + sh:513 + NT * b + sh], M[:, sh, P * b:P * b + cols], ones[:, 0:1], start=True, stop=True)
            mm.then_inc(s_ctm, 1)
            pe.wait_ge(s_ct, 2)
            ring = [AG[:, 0:NCP], AG[:, 512:512 + NCP], D2[:, 0:NCP], D2[:, 512:512 + NCP]]

            def places_before(sh, r, wait):
                pe.wait_ge(s_gsel, wait)
                for b in range(4):
                    k = min(P, NCP - P * b)
                    pe.matmul(ring[r][:, P * b:NCP], ct[0:k, b, bass.ds(sh, 1)].to_broadcast([k, P]),
                              U[0:k, b, P * b:NCP], start=(b == 0), stop=False, skip_group_check=True)
                mm = pe.matmul(ring[r], tri, M[:, bass.ds(sh, 1), :], start=False, stop=True, skip_group_check=True)
                mm.then_inc(s_G, 1)

            with pe.Fori(0, NT // 4) as i:
                for r in range(4):
                    places_before(4 * i + r, r, 4 * i + r + 1)
            places_before(NT - 1, 0, NT)
            pe.wait_ge(s_V, 3)

            def records(b, r, w):
                pe.wait_ge(s_osl, b + 1)
                pe.wait_ge(s_rec, 2 * b + 2)
                for j in range(WIN):
                    mm = pe.matmul(D0[:, 512 * r:512 * r + 4 * NT], oslot[:, r, j, :], V[:, :, bass.ds(w + j, 1)],
                                   start=(j == 0), stop=(j == WIN - 1))
                mm.then_inc(s_rmm, 1)

            with pe.Fori(0, NT // 2) as i:
                for r in range(2):
                    records(2 * i + r, r, (i * 250 + 125 * r) // 8)
            records(NT - 1, 0, (NT - 1) * 125 // 8)
            pe.wait_ge(s_om, 1)
            pe.matmul(D1[:, 0:2], onesf, occs[:, 0:2], start=True, stop=True).then_inc(s_omm, 1)

            def ln_back(n):
                pe.wait_ge(s_norm, n + 1)
                if n:
                    pe.wait_ge(s_h, n)
                for i in range(GT):
                    mm = pe.transpose(D1[:, P * i:P * i + TN], tiles(C, TN)[:, i, :], identf[0:TN, 0:TN])
                mm.then_inc(s_hTm, 1)

            def ln_in(n):
                g = n % NG
                if n // NG == 2:
                    pe.wait_ge(s_hnew, STEPS * NG)
                else:
                    pe.wait_ge(s_act, n + 1)
                if n > NG:
                    pe.wait_ge(s_xsum, n - NG)
                for i in range(GT):
                    mm = pe.transpose(D0[0:TN, P * i:P * (i + 1)], group(hT, g)[:, TN * i:TN * (i + 1)], identf[:])
                mm.then_inc(s_xT, 1)

            def dense(ps, w, act, start=True, stop=True):
                for h in range(2):
                    mm = pe.matmul(half(nodes(ps), h), W[:, w, :], half(act, h), start=start, stop=stop)
                return mm

            pe.wait_ge(s_w, 16)
            for n in range(NG):
                ln_back(n)
                pe.wait_ge(s_h, n + 1)
                if n:
                    pe.wait_ge(s_encr, n)
                dense(D2, 0, group(hT, n)).then_inc(s_enc, 1)

            pe.wait_ge(s_flag, 1)
            fast = pe.value_load(flag[0:1, 0:1], min_val=0, max_val=1)

            def build(q):
                def step(t, r, j, g):
                    pe.wait_ge(s_oh, q * BLD + t + 1)
                    pe.wait_ge(s_cnt, q * BLD + t + 1)
                    oh = ohring(r)
                    for i in range(GT):
                        mm = pe.matmul((D1, D2)[r][0:TN, P * i:P * i + TN], oh[:, i, 0:TN], oh[:, GT + i, 0:TN], start=True, stop=True)
                    mm.then_inc(s_blk, 1)
                if q < 3:
                    pe.wait_ge(s_h, NG * (q + 1))
                else:
                    pe.wait_ge(s_feat, NG * (FEAT_TYPE0 + q - 2))
                if q == 0:
                    pe.wait_ge(s_encr, NG)
                run_steps(pe, q, step)

            def agg(kind, p, hp, g):
                S = 2 if kind == "gru" else SPLITS
                n = p * NG + g
                if kind[:3] != "deg":
                    pe.wait_ge(s_feat, hp * NG + NG)
                if not (kind == "deg_in" and g == 0):
                    pe.wait_ge(s_aggu, n)
                Hs = H16 if kind == "gru" else H[:]

                def feature(j, k):
                    if kind[:3] == "deg":
                        return ones[0:TN, :]
                    if isinstance(j, int):
                        return Hs[0:TN, (j * S + k) * D:(j * S + k + 1) * D]
                    return Hs[0:TN, bass.ds((j * S + k) * D, D)]

                pe.wait_ge(s_cnt, 2 + BLD * builds_before(kind, p))
                with pe.If(fast == 1):
                    ks = 1 if kind[:3] == "deg" else S

                    def tile(j):
                        for k in range(ks):
                            for h in range(2):
                                at, size = (0, H0) if h == 0 else (H0, H1)
                                mm = pe.matmul(half(nodes(AG), h), feature(j, k), adj[0:TN, bass.ds(g * GP + j * GN + at, size)],
                                               start=(isinstance(j, int) and j == 0 and k == 0), stop=(isinstance(j, int) and j == NT - 1 and k == ks - 1),
                                               skip_group_check=True)
                        return mm

                    tile(0)
                    with pe.Fori(0, 5) as i:
                        for r in range(4):
                            tile(i * 4 + 1 + r)
                    for j in range(21, NT):
                        mm = tile(j)
                    mm.then_inc(s_aggf, 1)
                with pe.Else():
                    a = arena(g)
                    for h in range(2):
                        pe.matmul(half(nodes(AG), h), zeros[:], iota1[:, 0:1].to_broadcast([P, (H0, H1)[h]]), start=True, stop=False, skip_group_check=True)
                    with pe.Fori(0, SL // 2) as i:
                        for r in range(2):
                            pe.wait_ge(sl_oh, n * SL + 2 * i + r + 1)
                            if kind[:3] != "deg":
                                pe.wait_ge(sl_g[r], 16 * ((hp * NG + g) * (SL // 2) + i + 1))
                            for k in range(1 if kind[:3] == "deg" else S):
                                rows = a["rows"][:, r, k * D:(k + 1) * D]
                                if kind == "gru":
                                    rows = rows.bitcast(F16)
                                for h in range(2):
                                    mm = pe.matmul(half(nodes(AG), h), ones[:] if kind[:3] == "deg" else rows, half(a["oh"][:, r, :], h),
                                                   start=False, stop=False, skip_group_check=True)
                            mm.then_inc(sl_used, 1)
                    for h in range(2):
                        mm = pe.matmul(half(nodes(AG), h), zeros[:], iota1[:, 0:1].to_broadcast([P, (H0, H1)[h]]), start=False, stop=True, skip_group_check=True)
                    mm.then_inc(s_aggf, 1)
                if kind == "conv" and isinstance(p, int) and p < DEG_OUT:
                    for i in range(GT):
                        for k in range(SPLITS):
                            mm = pe.matmul(nodes(AG)[:, TN * i:TN * (i + 1)], feature(g * GT + i, k), identb[0:TN, 0:TN],
                                           start=False, stop=(k == SPLITS - 1), skip_group_check=True)
                    mm.then_inc(s_agg, 1)
                else:
                    pe.wait_ge(s_aggf, n + 1)
                    pe.nop().then_inc(s_agg, 1)

            def nm(kind, hp, g, w=0, first=0):
                ps = (D0, D1)[g % 2]
                m = hp * NG + g
                if kind == "conv":
                    pe.wait_ge(s_pre, first + g + 1)
                elif kind == "type":
                    pe.wait_ge(s_h, 4 * NG)
                if not (isinstance(hp, int) and m < 2):
                    pe.wait_ge(s_feat, m - 1)
                for i in range(GT):
                    at = TN * i
                    if kind == "gru":
                        mm = pe.transpose(ps[0:TN, P * i:P * (i + 1)], group(hT, g)[:, at:at + TN], identf[:])
                    else:
                        act = C[:, at:at + TN] if kind == "conv" else group(hT, g)[:, at:at + TN]
                        mm = pe.matmul(ps[0:TN, P * i:P * (i + 1)], act, W[:, w, :], start=True, stop=True)
                mm.then_inc(s_nm, 1)

            build(0)
            for g in range(NG):
                agg("deg_in", DEG_IN, 0, g)
            for g in range(NG):
                nm("conv", 0, g, 1, 0)
            for g in range(NG):
                agg("conv", CONV0, 0, g)
            for g in range(NG):
                nm("conv", 1, g, 2, NG)
            for g in range(NG + 1):
                if g < NG:
                    agg("conv", CONV1, 1, g)
                if g:
                    ln_in(NG + g - 1)
                    ln_back(NG + g - 1)
            build(1)
            for g in range(NG):
                agg("deg_out", DEG_OUT, 0, g)
            pe.wait_ge(s_w, 32)
            pe.wait_ge(s_h, 2 * NG)
            for g in range(NG):
                nm("gru", FEAT_GRU0, g)

            def gates(s, g):
                n = s * NG + g
                h = group(hT, g)
                pe.wait_ge(s_aggu, GRU0 * NG + n + 1)
                if not (isinstance(s, int) and s == 0 and g == 0):
                    pe.wait_ge(s_hnew, n)
                dense(D0, 0, X).then_inc(s_pmsg, 1)
                pe.wait_ge(s_msg, n + 1)
                dense(D1, 1, B, True, False)
                dense(D1, 4, h, False, True)
                dense(D2, 2, B, True, False)
                dense(D2, 5, h, False, True).then_inc(s_prz, 1)
                pe.wait_ge(s_sig, 2 * n + 1)
                dense(D1, 6, h)
                dense(D0, 3, B).then_inc(s_pn, 1)

            def gru_pe(s):
                for g in range(NG + 1):
                    if g < NG:
                        agg("gru", GRU0 + s, FEAT_GRU0 + s, g)
                    if g:
                        gates(s, g - 1)
                pe.wait_ge(s_hnew, s * NG + NG)

            gru_pe(0)
            with pe.Fori(1, STEPS) as s:
                for g in range(NG):
                    nm("gru", FEAT_GRU0 + s, g)
                gru_pe(s)
            for n in range(2 * NG, 3 * NG):
                ln_in(n)
                ln_back(n)
            build(2)
            pe.wait_ge(s_w, 48)
            for g in range(NG):
                nm("conv", 7, g, 0, 2 * NG)
            for g in range(NG):
                agg("conv", CONV2, 7, g)
            for g in range(NG):
                nm("conv", 8, g, 1, 3 * NG)
            for g in range(NG + 1):
                if g < NG:
                    agg("conv", CONV3, 8, g)
                if g:
                    ln_in(3 * NG + g - 1)
                    ln_back(3 * NG + g - 1)
            pe.wait_ge(s_w, 64)
            for t in range(TYPES):
                for g in range(NG):
                    nm("type", FEAT_TYPE0 + t, g, t)
                build(3 + t)
                for g in range(NG):
                    agg("type", TYPE0 + t, FEAT_TYPE0 + t, g)
            pe.wait_ge(s_lw, 48)
            banks = [D1[0:TN, 0:384], D1[0:TN, 512:896], D2[0:TN, 0:384], D2[0:TN, 512:896]]
            for g in range(NG):
                pe.wait_ge(s_lx, 64 * (g + 1))
                if g:
                    pe.wait_ge(s_ly, g)
                for i in range(GT):
                    n = g * GT + i
                    at = TN * i
                    h = group(hT, g)[:, at:at + TN]
                    pe.transpose(D0[0:TN, P * i:P * (i + 1)], h, identf[:])
                    if n >= 4:
                        pe.wait_ge(s_lt, n - 3)
                    pe.matmul(banks[n % 4], h, WN[:, 0, :], start=True, stop=False)
                    for t in range(TYPES):
                        mm = pe.matmul(banks[n % 4], part[:, t, at:at + TN], WN[:, 1 + t, :], start=False, stop=(t == TYPES - 1))
                    mm.then_inc(s_lo, 1)

        @block.vector
        def _(dve):
            own = [0]

            def mine(ins):
                own[0] += 1
                ins.then_inc(s_own, 1)
                dve.wait_ge(s_own, own[0])

            dve.sem_inc(s_gsel, 4)
            dve.memset(raw[:, :, 3, :], -1).then_inc(s_rawm, 1)
            dve.memset(ef[:, :, 0:LEAD], -1.0)
            dve.wait_ge(s_raw, 16 * 9)
            dve.wait_ge(s_rawm, 1)
            dve.tensor_copy(rawf.rearrange("p a b c -> p (a b c)"), raw.rearrange("p a b c -> p (a b c)")).then_inc(s_rawf, 1)
            for k in range(3):
                dve.wait_ge(s_eT, k + 1)
                dve.tensor_copy(ef[:, k, LEAD:NCP], (D0, D0, D1)[k][:, 512 * (k % 2):512 * (k % 2) + NCP - LEAD]).then_inc(s_ef, 1)
            dve.wait_ge(s_ef, 3)
            mine(dve.tensor_scalar(qi, ef[:, 0:2, :], 1.0 / TN, 0.5 / TN - 0.5, ALU.mult, ALU.add))
            mine(dve.tensor_copy(qf, qi))
            dve.tensor_copy(stile, qf[:, 0, :])
            mine(dve.scalar_tensor_tensor(out=qrem, in0=qf, scalar=-float(TN), in1=ef[:, 0:2, :], op0=ALU.mult, op1=ALU.add))
            for sh in range(NT):
                dve.tensor_scalar(M[:, sh, :], stile, float(sh), None, ALU.is_equal).then_inc(s_M, 1)
            dve.tensor_scalar(val[:, 0:2, :], qrem, 1.0, None, ALU.add)
            mine(dve.tensor_scalar(val[:, 2, :], ef[:, 2, :], 1.0, None, ALU.add))
            for k in range(3):
                dve.tensor_tensor(V[:, NT * k:NT * (k + 1), :], M, val[:, k:k + 1, :].to_broadcast([P, NT, NCP]), ALU.mult).then_inc(s_V, 1)

            def select(sh, r, v):
                dve.wait_ge(s_G, v)
                dve.scalar_tensor_tensor(out=gsel[:, bass.ds(sh, 1), :].rearrange("p a c -> p (a c)"), in0=stile, scalar=iotat[:, bass.ds(sh, 1)],
                                         in1=(AG, AG, D2, D2)[r][:, 512 * (r % 2):512 * (r % 2) + NCP],
                                         op0=ALU.is_equal, op1=ALU.mult).then_inc(s_gsel, 1)

            dve.wait_ge(s_const, 1)
            with dve.Fori(0, NT // 4) as i:
                for r in range(4):
                    select(4 * i + r, r, 4 * i + r + 1)
            select(NT - 1, 0, NT)
            dve.wait_ge(s_gsel, NT + 4)
            mine(dve.tensor_reduce(slot1, gsel.rearrange("p a c -> p c a"), AX, ALU.add))
            mine(dve.tensor_copy(gsum, slot1))
            mine(dve.tensor_scalar(gslot, gsum, P - 1, None, ALU.bitwise_and))
            mine(dve.tensor_scalar(slot1, gslot, 1.0, None, ALU.add))

            def slots(b, r, w):
                dve.wait_ge(s_rmm, b + 1)
                dve.scalar_tensor_tensor(out=slotb[:, r, :].rearrange("p (c d) -> p c d", d=4),
                                         in0=qf[:, 1, bass.ds(w, WIN)].unsqueeze(2).to_broadcast([P, WIN, 4]), scalar=iotat[:, bass.ds(b, 1)],
                                         in1=slot1[:, bass.ds(w, WIN)].unsqueeze(2).to_broadcast([P, WIN, 4]),
                                         op0=ALU.is_equal, op1=ALU.mult).then_inc(s_slotb, 1)
                dve.wait_ge(s_slotb, b + 1)
                dve.tensor_tensor(oslot[:, r, :, :].rearrange("p c (v d) -> p c v d", d=4),
                                  iota1[:].rearrange("p (v d) -> p v d", d=4).unsqueeze(1).to_broadcast([P, WIN, P // 4, 4]),
                                  slotb[:, r, :].rearrange("p (c d) -> p c d", d=4).unsqueeze(2).to_broadcast([P, WIN, P // 4, 4]),
                                  ALU.is_equal).then_inc(s_osl, 1)

            dve.sem_inc(s_rmm, 2)
            with dve.Fori(0, NT // 2) as i:
                for r in range(2):
                    slots(2 * i + r, r, (i * 250 + 125 * r) // 8)
            slots(NT - 1, 0, (NT - 1) * 125 // 8)
            dve.wait_ge(s_rec, 4 + 2 * NT)
            occ = B[:, 0:NT * NT]
            mine(dve.tensor_reduce(occs[:, 2:3], occ, AX, ALU.max))
            mine(dve.tensor_reduce(occs[:, 1:2], occ, AX, ALU.add))
            mine(dve.memset(onesf, 1.0))
            dve.tensor_scalar(occs[:, 0:1], occs[:, 2:3], 1.5, None, ALU.is_gt).then_inc(s_om, 1)
            dve.wait_ge(s_omm, 1)
            mine(dve.tensor_copy(occs[:, 2:4], D1[:, 0:2]))
            mine(dve.tensor_scalar(occs[:, 0:1], occs[:, 2:3], 0.5, None, ALU.is_lt))
            mine(dve.tensor_scalar(occs[:, 1:2], occs[:, 3:4], float(E), None, ALU.is_equal))
            dve.tensor_tensor(flag[:], occs[:, 0:1], occs[:, 1:2], ALU.mult).then_inc(s_flag, 1)

            dve.wait_ge(s_par, 32)
            dve.wait_ge(s_vstd, 1)
            v = lambda k: vec[:, k:k + 1]
            mine(dve.reciprocal(v(V_STD), v(V_STD)))
            mine(dve.tensor_tensor(v(V_SCALE), v(V_GAMMA), v(V_STD), ALU.mult))
            mine(dve.tensor_tensor(v(V_SHIFT), v(V_MEAN), v(V_SCALE), ALU.mult))
            mine(dve.tensor_tensor(v(V_SHIFT), v(V_BETA), v(V_SHIFT), ALU.subtract))
            dve.tensor_tensor(v(V_BR), v(V_BIR), v(V_BHR), ALU.add)
            dve.tensor_tensor(v(V_BZ), v(V_BIZ), v(V_BHZ), ALU.add).then_inc(s_vec, 1)

            def ln(n):
                xt = tiles(X, TN)
                dve.wait_ge(s_xl, 16 * (n + 1))
                if n >= NG:
                    dve.wait_ge(s_xT, n - NG + 1)
                    dve.tensor_tensor(xt, xt, tiles(D0, TN), ALU.add).then_inc(s_xsum, 1)
                    dve.wait_ge(s_xsum, n - NG + 1)
                for i in range(GT):
                    st = dve.bn_stats(stats[0:TN, i, :], xt[:, i, :])
                st.then_inc(s_bn, 1)
                dve.wait_ge(s_bn, n + 1)
                for i in range(GT):
                    st = dve.bn_aggr(mv[0:TN, i, :], stats[0:TN, i, :])
                st.then_inc(s_mv, 1)
                dve.wait_ge(s_std, n + 1)
                mine(dve.reciprocal(rstd[0:TN, :], rstd[0:TN, :]))
                if n:
                    dve.wait_ge(s_hTm, n)
                for i in range(GT):
                    st = dve.tensor_scalar(tiles(C, TN)[:, i, :], xt[:, i, :], mv[0:TN, i, 0:1], rstd[0:TN, i:i + 1], ALU.subtract, ALU.mult)
                st.then_inc(s_norm, 1)

            dve.wait_ge(s_vec, 1)
            for n in range(NG + 1):
                if n < NG:
                    ln(n)
                if n:
                    dve.wait_ge(s_encr, n)
                    dve.tensor_scalar(group(hT, n - 1), (A, B)[(n - 1) % 2][:, 0:GN], v(V_SCALE), v(V_SHIFT), ALU.mult, ALU.add).then_inc(s_bnh, 1)

            fast = dve.value_load(flag[0:1, 0:1], min_val=0, max_val=1)

            def build(q, swapped=False, t=None):
                if t is not None:
                    dve.wait_ge(s_xst, 16 * 3 * NG)
                    rect = X[:, 0:320].bitcast(BF16)[:, 0:NT * NT].rearrange("p (i j) -> p i j", j=NT)
                    mine(dve.scalar_tensor_tensor(out=rect, in0=rec[:, 2, :, :], scalar=float(t + 1), in1=rec[:, 1, :, :],
                                                  op0=ALU.is_equal, op1=ALU.mult))

                if q == 1 or q == 2:
                    dve.wait_ge(s_hTm, NG * (q + 1))
                if q > 2:
                    dve.wait_ge(s_erelu, NG * (q - 2))

                def prepare(g):
                    dup = dups
                    if q or g:
                        dve.wait_ge(s_oh, q * BLD + g * NT)
                    if q and g == 0:
                        dve.wait_ge(s_blk, q * BLD + 2)
                    for kind in range(2):
                        k = kind if not swapped else 1 - kind
                        r = rec[:, k, GT * g:GT * (g + 1), :].rearrange("p i j -> p j i") if not swapped else rec[:, k, :, GT * g:GT * (g + 1)]
                        o = dup[:, :, GT * kind:GT * (kind + 1), :]
                        if t is not None and k == 1:
                            r = rect[:, GT * g:GT * (g + 1), :].rearrange("p i j -> p j i")
                        ins = dve.tensor_copy(o, r.unsqueeze(3).to_broadcast([P, NT, GT, 4]))
                    ins.then_inc(s_dup, 1)
                    dve.wait_ge(s_dup, q * NG + g + 1)

                def step(t, r, j, g):
                    dve.wait_ge(s_blk, q * BLD + t + 1)
                    dve.tensor_tensor(ohring(r).rearrange("p i (v d) -> p i v d", d=4),
                                      iota1[:].rearrange("p (v d) -> p v d", d=4).unsqueeze(1).to_broadcast([P, 2 * GT, P // 4, 4]),
                                      dups[:, bass.ds(j, 1), :, :].rearrange("p a i d -> p (a i) d").unsqueeze(2).to_broadcast([P, 2 * GT, P // 4, 4]),
                                      ALU.is_equal).then_inc(s_oh, 1)
                run_steps(dve, q, step, prepare)

            def slow_hots(kind, p, g):
                with dve.If(fast == 0):
                    a = arena(g)
                    n = p * NG + g
                    dve.wait_ge(sl_load, 32 * (n + 1))
                    dve.wait_ge(sl_iota, n + 1)
                    dve.sem_inc(sl_seen, 1)
                    with dve.Fori(0, SL // 2) as i:
                        for r in range(2):
                            dve.wait_ge(sl_used, n * SL + 2 * i + r + 1)
                            dve.tensor_scalar(a["oh"][:, r, 0:GN], a["iota"], a["key"][:, bass.ds(LEAD + 2 * i + r, 1)], None, ALU.is_equal).then_inc(sl_oh, 1)
                with dve.Else():
                    dve.nop()
                dve.nop()

            def degrees(kind, p, d):
                for g in range(NG):
                    slow_hots(kind, p, g)
                    dve.wait_ge(s_agg, p * NG + g + 1)
                    if g:
                        dve.wait_ge(s_degst, 16 * (d * NG + g))
                    elif d:
                        dve.wait_ge(s_act, 2 * NG)
                    dve.tensor_copy(A[:, 0:GN], nodes(AG)).then_inc(s_aggu, 1)
                dve.wait_ge(s_degl, 16 * (d + 1))
                deg = A[0:TN, 0:NT]
                if d == 0:
                    mine(dve.tensor_scalar(A[0:TN, 128:128 + NT], deg, 1.0, None, ALU.add))
                dve.tensor_scalar(A[0:TN, 192:192 + NT], deg, 1.0, None, ALU.max).then_inc(s_degf, 1)
                dve.wait_ge(s_degs, d + 1)
                if d == 0:
                    mine(dve.reciprocal(A[0:TN, 128:128 + NT], A[0:TN, 128:128 + NT]))
                dve.reciprocal(A[0:TN, 192:192 + NT], A[0:TN, 192:192 + NT]).then_inc(s_norms, 1)

            def pre(j, g):
                k = PRE_NORM[j] * NG + g
                dve.wait_ge(s_nbl, 16 * (k + 1))
                if j == 2:
                    dve.wait_ge(s_h, 3 * NG)
                elif j:
                    dve.wait_ge(s_act, NG * j)
                if j * NG + g:
                    dve.wait_ge(s_nm, (0, 1, 7, 8)[j] * NG + g)
                if g == 0 and j in (0, 2):
                    dve.wait_ge(s_blk, 2 + BLD * (j + 1))
                dve.tensor_tensor(C[:, 0:GN], group(hT, g), DB[:, 0:GN], ALU.mult).then_inc(s_pre, 1)

            def split3(hp, g, src):
                m = hp * NG + g
                Ht = H[0:TN, :].rearrange("p (t k d) -> p t k d", k=SPLITS, d=D)[:, GT * g:GT * (g + 1)]
                dve.wait_ge(s_hi, m + 1)
                dve.tensor_tensor(tiles(A, TN), src, Ht[:, :, 0, :], ALU.subtract).then_inc(s_r1, 1)
                dve.wait_ge(s_mid, mid_of(hp, g) + 1)
                dve.tensor_tensor(Ht[:, :, 2, :], tiles(A, TN), Ht[:, :, 1, :], ALU.subtract).then_inc(s_feat, 1)

            def split2(hp, g):
                m = hp * NG + g
                Ht = H16[0:TN].rearrange("p (t k d) -> p t k d", k=2, d=D)[:, GT * g:GT * (g + 1)]
                dve.wait_ge(s_hi, m + 1)
                dve.tensor_tensor(Ht[:, :, 1, :], tiles((D0, D1)[g % 2], TN), Ht[:, :, 0, :], ALU.subtract).then_inc(s_feat, 1)

            def conv(p, g):
                slow_hots("conv", p, g)
                dve.wait_ge(s_agg, p * NG + g + 1)
                dve.wait_ge(s_nbl, 16 * (CONV_NORM[p] * NG + g + 1))
                if conv_no(p) * NG + g:
                    dve.wait_ge(s_act, conv_no(p) * NG + g)
                dve.tensor_tensor(A[:, 0:GN], nodes(AG), DB[:, 0:GN], ALU.mult).then_inc(s_aggu, 1)

            dve.wait_ge(s_bnh, NG)
            build(0)
            degrees("deg_in", DEG_IN, 0)
            for g in range(NG):
                pre(0, g)
                split3(0, g, tiles((D0, D1)[g % 2], TN))
            for g in range(NG):
                conv(CONV0, g)
            for g in range(NG):
                pre(1, g)
                split3(1, g, tiles((D0, D1)[g % 2], TN))
            for g in range(NG + 1):
                if g < NG:
                    conv(CONV1, g)
                if g:
                    ln(NG + g - 1)
            build(1, swapped=True)
            degrees("deg_out", DEG_OUT, 1)
            for g in range(NG):
                split2(FEAT_GRU0, g)

            def gru(s, g):
                n = s * NG + g
                h = group(hT, g)
                b = B[:, 0:GN]
                a = A[:, 0:GN]
                dve.wait_ge(s_pmsg, n + 1)
                dve.wait_ge(s_nbl, 16 * (4 * NG + n + 1))
                dve.scalar_tensor_tensor(out=b, in0=DB[:, 0:GN], scalar=v(V_BMSG), in1=nodes(D0), op0=ALU.mult, op1=ALU.add).then_inc(s_msg, 1)
                dve.wait_ge(s_pn, n + 1)
                dve.wait_ge(s_sig, 2 * n + 2)
                dve.scalar_tensor_tensor(out=a, in0=nodes(D1), scalar=v(V_BHN), in1=a, op0=ALU.add, op1=ALU.mult).then_inc(s_gown, 1)
                dve.wait_ge(s_gown, 3 * n + 1)
                dve.tensor_tensor(a, a, nodes(D0), ALU.add).then_inc(s_gpre, 1)
                dve.wait_ge(s_gtanh, n + 1)
                dve.tensor_tensor(b, h, a, ALU.subtract).then_inc(s_gown, 1)
                dve.wait_ge(s_gown, 3 * n + 2)
                dve.tensor_tensor(b, b, C[:, 0:GN], ALU.mult).then_inc(s_gown, 1)
                dve.wait_ge(s_gown, 3 * n + 3)
                dve.tensor_tensor(h, a, b, ALU.add).then_inc(s_hnew, 1)

            def gru_dve(s):
                for g in range(NG + 1):
                    if g < NG:
                        slow_hots("gru", GRU0 + s, g)
                    if g:
                        gru(s, g - 1)

            gru_dve(0)
            with dve.Fori(1, STEPS) as s:
                for g in range(NG):
                    split2(FEAT_GRU0 + s, g)
                gru_dve(s)
            for n in range(2 * NG, 3 * NG):
                ln(n)
            build(2)
            for g in range(NG):
                pre(2, g)
                split3(7, g, tiles((D0, D1)[g % 2], TN))
            for g in range(NG):
                conv(CONV2, g)
            for g in range(NG):
                pre(3, g)
                split3(8, g, tiles((D0, D1)[g % 2], TN))
            for g in range(NG + 1):
                if g < NG:
                    conv(CONV3, g)
                if g:
                    ln(3 * NG + g - 1)
            for t in range(TYPES):
                for g in range(NG):
                    m = (FEAT_TYPE0 + t) * NG + g
                    dve.wait_ge(s_nm, m + 1)
                    if t * NG + g:
                        dve.wait_ge(s_erelu, t * NG + g)
                    if t and g == 0:
                        dve.wait_ge(s_tst, 16 * t * NG)
                        dve.wait_ge(s_blk, 2 + BLD * (3 + t))
                    dve.tensor_tensor(tiles(C, TN), tiles((D0, D1)[g % 2], TN), beb[0:TN, t:t + 1, :].to_broadcast([TN, GT, D]), ALU.add).then_inc(s_ebias, 1)
                    split3(FEAT_TYPE0 + t, g, tiles(B, TN))
                build(3 + t, t=t)
                for g in range(NG):
                    slow_hots("type", TYPE0 + t, g)

            dve.wait_ge(s_lw, 48)
            mine(dve.tensor_copy(ntf[0:TN], nti[0:TN]))
            for t in range(TYPES):
                mine(dve.tensor_scalar(mask[0:TN, t, :], ntf[0:TN], float(t), None, ALU.is_equal))
            for g in range(NG):
                dve.wait_ge(s_lx, 64 * (g + 1))
                for i in range(GT):
                    n = g * GT + i
                    y = tmp[0:TN, n % 2, :]
                    xt = tiles(X, TN)[:, i, :]
                    dve.wait_ge(s_lo, n + 1)
                    dve.tensor_tensor(y, (D1, D1, D2, D2)[n % 4][0:TN, 512 * (n % 2):512 * (n % 2) + TYPES * D], bnb[0:TN], ALU.add).then_inc(s_lt, 1)
                    dve.wait_ge(s_lt, n + 1)
                    for t in range(TYPES):
                        mine(dve.scalar_tensor_tensor(out=xt, in0=y[:, D * t:D * (t + 1)], scalar=mask[0:TN, t, n:n + 1], in1=xt, op0=ALU.mult, op1=ALU.add))
                dve.tensor_tensor(tiles(X, TN), tiles(X, TN), tiles(D0, TN), ALU.add).then_inc(s_ly, 1)

        @block.scalar
        def _(act):
            act.sem_inc(s_rec, 4)
            act.sem_inc(s_cnt, 2)
            v = lambda k: vec[:, k:k + 1]
            act.wait_ge(s_par, 32)
            act.wait_ge(s_const, 1)
            act.activation(v(V_STD), v(V_VAR), ACT.Sqrt, bias=v(V_EPS)).then_inc(s_vstd, 1)
            act.wait_ge(s_ctm, 1)
            act.copy(ct[:, 0:3, :], D1[:, 512:512 + 3 * NT].rearrange("p (a b) -> p a b", a=3)).then_inc(s_ct, 1)
            act.copy(ct[0:NCP - 3 * P, 3, :], D1[0:NCP - 3 * P, 512 + 3 * NT:512 + 4 * NT]).then_inc(s_ct, 1)

            def take(b, r):
                act.wait_ge(s_rmm, b + 3)
                act.copy(rec[:, :, bass.ds(b, 1), :].rearrange("p k a s -> p k (a s)"), D0[:, 512 * r:512 * r + 3 * NT].rearrange("p (k s) -> p k s", k=3)).then_inc(s_rec, 1)
                act.copy(B[:, bass.ds(b * NT, NT)], D0[:, 512 * r + 3 * NT:512 * r + 4 * NT]).then_inc(s_rec, 1)

            with act.Fori(0, NT // 2) as i:
                for r in range(2):
                    take(2 * i + r, r)
            take(NT - 1, 0)

            def ln_std(n):
                act.wait_ge(s_mv, n + 1)
                act.activation(rstd[0:TN, :], mv[0:TN, :, 1], ACT.Sqrt, bias=vec[0:TN, V_EPS:V_EPS + 1]).then_inc(s_std, 1)

            def ln_h(n):
                act.wait_ge(s_hTm, n + 1)
                act.activation(group(hT, n % NG).rearrange("p (t n) -> p t n", t=GT), tiles(D1)[:, :, 0:TN], ACT.Relu).then_inc(s_h, 1)

            act.wait_ge(s_flag, 1)
            for n in range(NG):
                ln_std(n)
                ln_h(n)
                act.wait_ge(s_enc, n + 1)
                if n > 1:
                    act.wait_ge(s_bnh, n - 1)
                act.activation((A, B)[n % 2][:, 0:GN], nodes(D2), ACT.Relu, bias=v(V_BENC)).then_inc(s_encr, 1)

            def build(q):
                if q == 0:
                    act.wait_ge(s_kp, 1)

                def step(t, r, j, g):
                    act.wait_ge(s_blk, q * BLD + t + 3)
                    act.copy(adj[0:TN, bass.ds(g * GP + j * GN, GN)].rearrange("p (i n) -> p i n", i=GT), tiles((D1, D2)[r], TN)[:, :, 0:TN]).then_inc(s_cnt, 1)
                run_steps(act, q, step)

            def hi3(hp, g, src):
                m = hp * NG + g
                act.wait_ge(s_nm, m + 1)
                Ht = H[0:TN, :].rearrange("p (t k d) -> p t k d", k=SPLITS, d=D)[:, GT * g:GT * (g + 1)]
                act.copy(Ht[:, :, 0, :], src).then_inc(s_hi, 1)
                act.wait_ge(s_r1, mid_of(hp, g) + 1)
                act.copy(Ht[:, :, 1, :], tiles(A, TN)).then_inc(s_mid, 1)

            def hi2(hp, g):
                m = hp * NG + g
                act.wait_ge(s_nm, m + 1)
                Ht = H16[0:TN].rearrange("p (t k d) -> p t k d", k=2, d=D)[:, GT * g:GT * (g + 1)]
                act.copy(Ht[:, :, 0, :], tiles((D0, D1)[g % 2], TN)).then_inc(s_hi, 1)

            def conv(p, g, bias, relu):
                act.wait_ge(s_aggu, p * NG + g + 1)
                act.activation(group(hT, g), A[:, 0:GN], ACT.Relu if relu else ACT.Identity, bias=v(bias)).then_inc(s_act, 1)

            def norms(d):
                act.wait_ge(s_degf, d + 1)
                if d == 0:
                    act.activation(A[0:TN, 128:128 + NT], A[0:TN, 128:128 + NT], ACT.Sqrt)
                act.activation(A[0:TN, 192:192 + NT], A[0:TN, 192:192 + NT], ACT.Sqrt).then_inc(s_degs, 1)

            build(0)
            norms(0)
            for g in range(NG):
                hi3(0, g, tiles((D0, D1)[g % 2], TN))
            for g in range(NG):
                conv(CONV0, g, V_B01, True)
            for g in range(NG):
                hi3(1, g, tiles((D0, D1)[g % 2], TN))
            for g in range(NG + 1):
                if g < NG:
                    conv(CONV1, g, V_B02, False)
                if g:
                    ln_std(NG + g - 1)
                    ln_h(NG + g - 1)
            build(1)
            norms(1)
            for g in range(NG):
                hi2(FEAT_GRU0, g)

            def gru(s, g):
                n = s * NG + g
                act.wait_ge(s_prz, n + 1)
                act.activation(A[:, 0:GN], nodes(D1), ACT.Sigmoid, bias=v(V_BR)).then_inc(s_sig, 1)
                act.activation(C[:, 0:GN], nodes(D2), ACT.Sigmoid, bias=v(V_BZ)).then_inc(s_sig, 1)
                act.wait_ge(s_gpre, n + 1)
                act.activation(A[:, 0:GN], A[:, 0:GN], ACT.Tanh, bias=v(V_BIN)).then_inc(s_gtanh, 1)

            def gru_act(s):
                for g in range(NG + 1):
                    if g < NG:
                        p = GRU0 + s
                        act.wait_ge(s_agg, p * NG + g + 1)
                        if isinstance(s, int) and s == 0 and g == 0:
                            act.wait_ge(s_xst, 16 * NG)
                            act.wait_ge(s_norm, 2 * NG)
                        else:
                            act.wait_ge(s_pmsg, s * NG + g)
                        act.copy(X[:, 0:GN], nodes(AG)).then_inc(s_aggu, 1)
                    if g:
                        gru(s, g - 1)

            gru_act(0)
            with act.Fori(1, STEPS) as s:
                for g in range(NG):
                    hi2(FEAT_GRU0 + s, g)
                gru_act(s)
            for n in range(2 * NG, 3 * NG):
                ln_std(n)
                ln_h(n)
            build(2)
            for g in range(NG):
                hi3(7, g, tiles((D0, D1)[g % 2], TN))
            for g in range(NG):
                conv(CONV2, g, V_B21, True)
            for g in range(NG):
                hi3(8, g, tiles((D0, D1)[g % 2], TN))
            for g in range(NG + 1):
                if g < NG:
                    conv(CONV3, g, V_B22, True)
                if g:
                    ln_std(3 * NG + g - 1)
                    ln_h(3 * NG + g - 1)
            for t in range(TYPES):
                for g in range(NG):
                    act.wait_ge(s_ebias, t * NG + g + 1)
                    if t * NG + g:
                        act.wait_ge(s_r1, mid_of(FEAT_TYPE0 + t, g))
                    if t:
                        act.wait_ge(s_tst, 16 * t * NG)
                    act.activation(tiles(B, TN), tiles(C, TN), ACT.Relu).then_inc(s_erelu, 1)
                    act.wait_ge(s_erelu, t * NG + g + 1)
                    hi3(FEAT_TYPE0 + t, g, tiles(B, TN))
                build(3 + t)
                for g in range(NG):
                    p = TYPE0 + t
                    act.wait_ge(s_agg, p * NG + g + 1)
                    k = t * NG + g
                    if k:
                        act.wait_ge(s_tst, 16 * k)
                    act.copy((A, B)[g % 2][:, 0:GN], nodes(AG)).then_inc(s_aggu, 1)


_VECS = ("L0_gnn_b_enc", "L0_gnn_bn_gamma", "L0_gnn_bn_beta", "L0_gnn_bn_mean", "L0_gnn_bn_var", "L0_gnn_b1", "L0_gnn_b2", "L1_gnn_b_msg")


def kernel(**inputs):
    import numpy as np
    import concourse.bacc as bacc
    from concourse.bass_utils import run_bass_kernel_spmd

    a = {k: np.asarray(v) for k, v in inputs.items()}
    vecs = [a[k] for k in _VECS] + list(a["L1_gnn_b_ih"].reshape(3, D)) + list(a["L1_gnn_b_hh"].reshape(3, D)) + [a["L2_gnn_b1"], a["L2_gnn_b2"]]
    ih, hh = a["L1_gnn_W_ih"].reshape(3, D, D), a["L1_gnn_W_hh"].reshape(3, D, D)
    wts = [a["L0_gnn_W_enc"], a["L0_gnn_W1"], a["L0_gnn_W2"], a["L1_gnn_W_msg"].T, *(w.T for w in ih), *(w.T for w in hh),
           a["L2_gnn_W1"], a["L2_gnn_W2"], *(w.T for w in a["L3_gnn_W_e"])]
    wn = a["L3_gnn_W_n"].reshape(3, D, 4, D)
    wts += [wn[t, :, k, :].T for k in range(4) for t in range(3)]
    arrays = {
        "in_x": a["x"], "in_src": a["src"], "in_dst": a["dst"], "in_edge_type": a["edge_type_3"], "in_node_type": a["node_type_3"],
        "in_vecs": np.stack(vecs, 1), "in_weights": np.stack(wts, 1), "in_b_e": a["L3_gnn_b_e"], "in_b_n": a["L3_gnn_b_n"],
    }
    arrays = {k: np.ascontiguousarray(v) for k, v in arrays.items()}
    nc = bacc.Bacc("TRN2", target_bir_lowering=False, num_devices=1)
    args = [nc.dram_tensor(k, v.shape, mybir.dt.from_np(v.dtype), kind="ExternalInput").ap() for k, v in arrays.items()]
    args.append(nc.dram_tensor("out_x", (N, D), F32, kind="ExternalOutput").ap())
    gnn_kernel(nc, *args)
    r = run_bass_kernel_spmd(nc, [arrays], core_ids=[0])
    return r.results[0]["out_x"]
```

```python
from contextlib import ExitStack

import concourse.bass as bass
from concourse import mybir

F32 = mybir.dt.float32
BF16 = mybir.dt.bfloat16
F16 = mybir.dt.float16
I32 = mybir.dt.int32
ALU = mybir.AluOpType
ACT = mybir.ActivationFunctionType
AX = mybir.AxisListType.X

P = 128
N = 3125
E = 50000
D = 128
TN = 125
NT = N // TN
GT = 5
NG = NT // GT
GN = GT * TN
H0, H1 = 3 * TN, 2 * TN
AG0 = 512 - H0
NCH = -(-E // P)
LEAD = 4
NCP = 400
WIN = 25
GP = 15632
SPLITS = 3
EPS = 1e-5
STEPS = 5
TYPES = 3

DEG_IN, CONV0, CONV1, DEG_OUT, GRU0 = 0, 1, 2, 3, 4
CONV2 = GRU0 + STEPS
CONV3 = CONV2 + 1
TYPE0 = CONV3 + 1
FEAT = {CONV0: 0, CONV1: 1, CONV2: 2 + STEPS, CONV3: 3 + STEPS}
FEAT_GRU0 = 2
FEAT_TYPE0 = 4 + STEPS
(V_BENC, V_GAMMA, V_BETA, V_MEAN, V_VAR, V_B01, V_B02, V_BMSG, V_BIR, V_BIZ, V_BIN, V_BHR, V_BHZ, V_BHN,
 V_B21, V_B22, V_BR, V_BZ, V_SCALE, V_SHIFT, V_STD, V_EPS) = range(22)
NV = 16
W_ENC, W_01, W_02, W_MSG, W_IR, W_IZ, W_IN, W_HR, W_HZ, W_HN, W_21, W_22, W_E, W_N = 0, 1, 2, 3, 4, 5, 6, 7, 8, 9, 10, 11, 12, 15


def gnn_kernel(nc, x, src, dst, etype, ntype, vecs, wts, be, bn, out):
    with ExitStack() as ctx:
        def sb(name, shape, dt):
            return ctx.enter_context(nc.sbuf_tensor(name, shape, dt))

        def sem(name):
            return ctx.enter_context(nc.semaphore(name))

        xs = nc.dram_tensor("x_between", (N, D), F32, kind="Internal").ap()
        aggd = nc.dram_tensor("typed_sums", (TYPES, P, N), F32, kind="Internal").ap()
        degd = nc.dram_tensor("degrees", (2, N), F32, kind="Internal").ap()
        normd = nc.dram_tensor("norms", (3, N), F32, kind="Internal").ap()
        hrows = nc.dram_tensor("feature_rows", (N, SPLITS * D), BF16, kind="Internal").ap()
        hrows16 = nc.dram_tensor("feature_rows16", (N, 2 * D), F16, kind="Internal").ap()
        keyd = nc.dram_tensor("edge_keys", (5, P, NCP), F32, kind="Internal").ap()
        idxd = nc.dram_tensor("edge_rows", (2, P, NCP), I32, kind="Internal").ap()

        adj = sb("counts", [P, NG * GP], BF16)
        H = sb("H", [P, NT * SPLITS * D], BF16)
        hT = sb("hT", [P, N], F32)
        A, B, C, DB, F, X = (sb(f"buf{c}", [P, 640], F32) for c in "ABCDFX")
        W = sb("W", [P, 7, D], F32)
        rec = sb("rec", [P, 3, NT, NT], BF16)
        identf = sb("identf", [P, P], F32)
        identb = sb("identb", [P, P], BF16)
        ones = sb("ones", [P, P], BF16)
        zeros = sb("zeros", [P, P], BF16)
        iota1 = sb("iota1", [P, P], BF16)
        iotat = sb("iotat", [P, NT], F32)
        vec = sb("vec", [P, 22], F32)
        stats = sb("stats", [P, GT, 6], F32)
        mv = sb("mv", [P, GT, 2], F32)
        rstd = sb("rstd", [P, GT], F32)
        occs = sb("occs", [P, 4], F32)
        flag = sb("flag", [P, 1], I32)

        def place(base, at, shape, dt):
            size = 1
            for s in shape:
                size *= s
            elems = size * (2 if dt in (F32, I32) else 1)
            ap = base[:, at // 2:at // 2 + elems]
            if dt != BF16:
                ap = ap.bitcast(dt)
            if len(shape) == 2:
                ap = ap.rearrange("p (a b) -> p a b", b=shape[1])
            if len(shape) == 3:
                ap = ap.rearrange("p (a b c) -> p a b c", b=shape[1], c=shape[2])
            return ap

        raw = place(adj, 0, (3, 4, P), I32)
        rawf = place(adj, 6144, (3, 4, P), F32)
        ef = place(adj, 12288, (3, NCP), F32)
        qi = place(adj, 17088, (2, NCP), I32)
        qf = place(adj, 20288, (2, NCP), F32)
        val = place(adj, 26688, (3, NCP), BF16)
        stile = place(adj, 29088, (NCP,), BF16)
        V = place(adj, 29888, (4 * NT, NCP), BF16)
        M = place(adj, 29888 + 3 * NT * NCP * 2, (NT, NCP), BF16)
        U = place(adj, 109888, (4, NCP), BF16)
        tri = place(adj, 113088, (P,), BF16)
        ct = place(adj, 113344, (4, NT), BF16)
        gsel = place(adj, 113600, (NT, NCP), F32)
        oslot = place(adj, 113600, (2, WIN, P), BF16)
        gsum = place(adj, 0, (NCP,), I32)
        gslot = place(adj, 1600, (NCP,), I32)
        slot1 = place(adj, 3200, (NCP,), F32)
        slotb = place(adj, 6400, (2, WIN * 4), BF16)
        qrem = place(adj, 23488, (2, NCP), F32)
        onesf = place(adj, 130000, (P,), F32)
        keyf = place(H, 0, (5, NCP), F32)
        idxi = place(H, 8000, (2, NCP), I32)
        idxf = place(H, 11200, (NCP,), F32)
        H16 = place(H, 0, (NT * 2 * D,), F16)
        beb = W[:, 3:3 + TYPES, :]
        WN = place(adj, 0, (4, TYPES * D), F32)
        bnb = place(adj, 6144, (TYPES * D,), F32)
        part = place(adj, 8192, (TYPES, GN), F32)
        tmp = place(adj, 16384, (2, TYPES * D), F32)
        ntf = place(adj, 20480, (NT,), F32)
        nti = place(adj, 20608, (NT,), I32)
        mask = place(adj, 20736, (TYPES, NT), F32)

        AG, D0, D1, D2 = (ctx.enter_context(nc.psum_tensor(n, [P, 1024], F32)) for n in ("AG", "D0", "D1", "D2"))

        def nodes(ps):
            return ps[:, AG0:AG0 + GN]

        def half(ap, h):
            return ap[:, 0:H0] if h == 0 else ap[:, H0:GN]

        def tiles(ap, rows=P):
            return ap[0:rows, 0:640].rearrange("p (t n) -> p t n", t=GT)

        def group(ap, g):
            return ap[:, g * GN:(g + 1) * GN]

        def ohring(q, g, r):
            if r == 0 and q == 2 and g < NG - 1:
                return place(H, 2 * NT * 2 * D, (2 * GT, P), BF16)
            types = (q, g) >= (3, NG - 1)
            return (X if types and r == 0 else B if r == 0 else F)[:].bitcast(BF16).rearrange("p (i n) -> p i n", n=P)

        def dup_of(q, g):
            if q == 2 and g < NG - 1:
                return place(H, 2 * NT * 2 * D + 4 * 640, (NT, 2 * GT * 4), BF16).rearrange("p j (i d) -> p j i d", d=4)
            if q == 0 or (q, g) >= (3, NG - 1):
                flat = DB[:, 0:NT * GT * 4]
            else:
                flat = W[:, 3:7, :].rearrange("p a b -> p (a b)")[:, 0:NT * GT * 4]
            return flat.bitcast(BF16).rearrange("p (j i d) -> p j i d", j=NT, d=4)

        s_pown = sem("s_pown")
        sl_seen = sem("sl_seen")
        s_slotb = sem("s_slotb")
        s_aggf = sem("s_aggf")
        s_pmsg = sem("s_pmsg")
        s_msg = sem("s_msg")
        s_prz = sem("s_prz")
        s_sig = sem("s_sig")
        s_pn = sem("s_pn")
        s_const = sem("s_const")
        s_par = sem("s_par")
        s_w = sem("s_w")
        s_vec = sem("s_vec")
        s_vstd = sem("s_vstd")
        s_rawm = sem("s_rawm")
        s_raw = sem("s_raw")
        s_rawf = sem("s_rawf")
        s_eT = sem("s_eT")
        s_ef = sem("s_ef")
        s_own = sem("s_own")
        s_M = sem("s_M")
        s_ctm = sem("s_ctm")
        s_ct = sem("s_ct")
        s_G = sem("s_G")
        s_gsel = sem("s_gsel")
        s_V = sem("s_V")
        s_osl = sem("s_osl")
        s_rmm = sem("s_rmm")
        s_rec = sem("s_rec")
        s_occ = sem("s_occ")
        s_om = sem("s_om")
        s_omm = sem("s_omm")
        s_flag = sem("s_flag")
        s_kp = sem("s_kp")
        s_key = sem("s_key")
        s_dup = sem("s_dup")
        s_oh = sem("s_oh")
        s_blk = sem("s_blk")
        s_cnt = sem("s_cnt")
        s_xl = sem("s_xl")
        s_xst = sem("s_xst")
        s_xT = sem("s_xT")
        s_xsum = sem("s_xsum")
        s_bn = sem("s_bn")
        s_mv = sem("s_mv")
        s_std = sem("s_std")
        s_rstd = sem("s_rstd")
        s_norm = sem("s_norm")
        s_hTm = sem("s_hTm")
        s_h = sem("s_h")
        s_enc = sem("s_enc")
        s_encr = sem("s_encr")
        s_bnh = sem("s_bnh")
        s_nb = sem("s_nb")
        s_nb2 = sem("s_nb2")
        s_pre = sem("s_pre")
        s_nm = sem("s_nm")
        s_ebias = sem("s_ebias")
        s_erelu = sem("s_erelu")
        s_hi = sem("s_hi")
        s_r1 = sem("s_r1")
        s_mid = sem("s_mid")
        s_feat = sem("s_feat")
        s_agg = sem("s_agg")
        s_aggu = sem("s_aggu")
        s_act = sem("s_act")
        s_degst = sem("s_degst")
        s_degl = sem("s_degl")
        s_degf = sem("s_degf")
        s_degs = sem("s_degs")
        s_norms = sem("s_norms")
        s_nst = sem("s_nst")
        s_gmsg = sem("s_gmsg")
        s_gm = sem("s_gm")
        s_grz = sem("s_grz")
        s_gsg = sem("s_gsg")
        s_gn = sem("s_gn")
        s_gown = sem("s_gown")
        s_gpre = sem("s_gpre")
        s_gtanh = sem("s_gtanh")
        s_hnew = sem("s_hnew")
        s_tst = sem("s_tst")
        s_lw = sem("s_lw")
        s_lx = sem("s_lx")
        s_lnt = sem("s_lnt")
        s_lo = sem("s_lo")
        s_lh = sem("s_lh")
        s_lown = sem("s_lown")
        s_lt = sem("s_lt")
        s_ly = sem("s_ly")
        s_out = sem("s_out")
        sl_rows = sem("sl_rows")
        sl_load = sem("sl_load")
        sl_iota = sem("sl_iota")
        sl_idx = sem("sl_idx")
        sl_g = [[sem(f"sl_g{g}{r}") for r in range(2)] for g in range(NG)]
        sl_oh = sem("sl_oh")
        sl_used = sem("sl_used")

        block = ctx.enter_context(nc.Block())

        SL = NCH + 1
        BLD = NG * NT

        def arena(g):
            b = g * GP * 2
            return dict(key=place(adj, b, (NCP,), F32), idx=place(adj, b + 1600, (NCP,), I32),
                        iota=place(adj, b + 3200, (GN,), F32), oh=place(adj, b + 5728, (2, 640), BF16),
                        rows=place(adj, b + 8320, (2, SPLITS * D), BF16), col=place(adj, b + 10240, (2, 8), I32))

        def along(kind, p, g):
            if kind == "deg_in":
                return (0, g + 1) if g + 1 < NG else None
            if not isinstance(p, int) or kind == "conv" and p in (CONV0,):
                return None
            if g == 0:
                q = {DEG_OUT: 1, CONV2: 2, TYPE0: 3, TYPE0 + 1: 4, TYPE0 + 2: 5}.get(p)
                return None if q is None else (q, NG - 1)
            q = {CONV1: 1, GRU0 + STEPS - 1: 2, CONV3: 3, TYPE0: 4, TYPE0 + 1: 5}.get(p)
            return None if q is None else (q, g - 1)

        def parity(q, g, j):
            return (q * BLD + g * NT + j) % 2

        def blocks(q, g, j_parity):
            return (D2, 2) if q == 2 and g < NG - 1 else ((D2, D1)[j_parity], 1)

        def steps(eng, what, step, first=0, last=NT):
            q, g = what
            n = (last - first) // 2
            with eng.Fori(0, n) as i:
                for r in range(2):
                    step(q, g, first + 2 * i + r, parity(q, g, first + r))
            for j in range(first + 2 * n, last):
                step(q, g, j, parity(q, g, j))

        def weave(eng, todo, at_tile):
            todo = sorted(todo, key=lambda e: e[0])
            first = max([2] + [int(at) + 1 for at, _ in todo])
            first = min(first + first % 2, NT - 1)

            def before(j):
                while todo and todo[0][0] <= j:
                    todo.pop(0)[1]()
            for j in range(first):
                before(j)
                if at_tile:
                    at_tile(j, j % 2)
            if at_tile and first < NT - 1:
                with eng.Fori(0, (NT - 1 - first) // 2) as i:
                    for r in range(2):
                        at_tile(first + 2 * i + r, r)
            before(NT)
            if at_tile:
                at_tile(NT - 1, 0)

        def along_step(what, step):
            return (lambda j, r: step(*what, j, parity(*what, r))) if what else None

        def accumulator(kind, p, g):
            if kind == "gru" and not (isinstance(p, int) and p == GRU0 + STEPS - 1):
                return ((AG, D2)[g % 2], 2)
            if kind[:3] == "deg" or kind == "type" or kind == "conv" and p in (CONV0, CONV2):
                return ((AG, D0)[g % 2], 2)
            return (AG, 1)

        def cnt_of(kind, p, g):
            return 2 + BLD * (builds_before(kind, p) - 1) + (g + 1) * NT

        NM_AT = (-9, 0, 4, 8, 13)
        NM_AT_GRU = (-9, 0, 5, 10, 18)

        def conv_no(p):
            return (CONV0, CONV1, CONV2, CONV3).index(p)

        def mid_of(hp, g):
            return (0, 1, 7, 8, 9, 10, 11).index(hp) * NG + g

        def key_of(kind, t):
            return {"deg_in": 0, "deg_out": 1, "conv": 0, "gru": 1, "type": 2 + t}[kind]

        def builds_before(kind, p):
            return {"deg_in": 1, "deg_out": 2, "gru": 2}.get(kind) or (1 if kind == "conv" and p < DEG_OUT else 3 if kind == "conv" else 4 + p - TYPE0)

        NB = {"pre0": 0, CONV0: 3, CONV1: 8, "gru": 13, "pre2": 38, CONV2: 41, CONV3: 46}
        NB2 = {"pre0": 0, CONV0: 2, "pre2": 7, CONV2: 9}

        @block.sync
        def _(sp):
            full = 3 * P * P
            sp.wait_ge(s_rawm, 1)
            for k, a in enumerate((src, dst, etype)):
                sp.dma_start(raw[:, k, 0:3, :], a[0:full].rearrange("(b c p) -> c b p", b=3, p=P)).then_inc(s_raw, 16)
                rows = (E - full) // P
                sp.dma_start(raw[0:rows, k, 3, :], a[full:full + rows * P].rearrange("(c p) -> c p", p=P)).then_inc(s_raw, 16)
                sp.dma_start(raw[rows:rows + 1, k, 3, 0:E - full - rows * P],
                             a[full + rows * P:E].rearrange("(c p) -> c p", c=1)).then_inc(s_raw, 16)
            sp.dma_start(vec[:, 0:NV], vecs).then_inc(s_par, 16)
            sp.dma_start(W[:, 0:3, :], wts[:, 0:3, :]).then_inc(s_w, 16)

            def load_x(n):
                q, g = divmod(n, NG)
                if n:
                    sp.wait_ge(s_norm, n)
                if n > NG:
                    sp.wait_ge(s_xst, 16 * (n - NG))
                if n == 2 * NG:
                    sp.wait_ge(s_pmsg, STEPS * NG)
                srcx = x if q < 2 else xs
                sp.dma_start(tiles(X, TN), srcx[g * GN:(g + 1) * GN, :].rearrange("(t p) d -> p t d", p=TN)).then_inc(s_xl, 16)

            def store_x(n):
                g = n % NG
                sp.wait_ge(s_xsum, n - NG + 1)
                sp.dma_start(xs[g * GN:(g + 1) * GN, :].rearrange("(t p) d -> p t d", p=TN), tiles(X, TN)).then_inc(s_xst, 16)

            for n in range(NG):
                load_x(n)

            sp.wait_ge(s_kp, 1)
            sp.dma_start(keyd.rearrange("k p c -> p k c"), keyf).then_inc(s_key, 16)
            sp.dma_start(idxd.rearrange("k p c -> p k c"), idxi).then_inc(s_key, 16)
            sp.wait_ge(s_key, 32)

            sp.wait_ge(s_flag, 1)
            fast = sp.value_load(flag[0:1, 0:1], min_val=0, max_val=1)

            def slow_loads(kind, p, hp, g, t=0):
                with sp.If(fast == 0):
                    a = arena(g)
                    sp.wait_ge(s_cnt, cnt_of(kind, p, g))
                    if kind[:3] != "deg" and g == 0:
                        sp.wait_ge(s_feat, hp * NG + NG)
                        if kind == "gru":
                            sp.dma_start(hrows16.rearrange("(t p) d -> p t d", p=TN),
                                         H16[0:TN].rearrange("p (t d) -> p t d", t=NT)).then_inc(sl_rows, 16)
                        else:
                            sp.dma_start(hrows.rearrange("(t p) d -> p t d", p=TN),
                                         H[0:TN].rearrange("p (t d) -> p t d", t=NT)).then_inc(sl_rows, 16)
                    if not (kind == "deg_in" and g == 0):
                        sp.wait_ge(s_agg, p * NG + g)
                    sp.dma_start(a["key"], keyd[key_of(kind, t)]).then_inc(sl_load, 16)
                    sp.dma_start(a["idx"], idxd[1 if kind == "gru" else 0]).then_inc(sl_load, 16)
                with sp.Else():
                    sp.nop()
                sp.nop()

            def degrees(kind, p, d):
                for g in range(NG):
                    slow_loads(kind, p, 0, g)
                    if d and g == 0:
                        store_x(2 * NG - 1)
                    if d and g == 1:
                        sp.wait_ge(s_oh, 2 * BLD)
                        sp.dma_start(W[:, 0:7, :], wts[:, W_MSG:W_MSG + 7, :]).then_inc(s_w, 16)
                    sp.wait_ge(s_aggu, p * NG + g + 1)
                    sp.dma_start(degd[d:d + 1, g * GN:(g + 1) * GN], A[0:1, 0:GN]).then_inc(s_degst, 16)
                    sp.wait_ge(s_degst, 16 * (d * NG + g + 1))
                sp.dma_start(A[0:TN, 0:NT], degd[d, :].rearrange("(t p) -> p t", p=TN), allow_slow_non_contiguous=True).then_inc(s_degl, 16)
                sp.wait_ge(s_norms, d + 1)
                if d == 0:
                    sp.dma_start(normd[0, :].rearrange("(t p) -> p t", p=TN), A[0:TN, 128:128 + NT], allow_slow_non_contiguous=True).then_inc(s_nst, 16)
                sp.dma_start(normd[1 + d, :].rearrange("(t p) -> p t", p=TN), A[0:TN, 192:192 + NT], allow_slow_non_contiguous=True).then_inc(s_nst, 16)
                sp.wait_ge(s_nst, 32 + 16 * d)

            def load_norm(row, g, after, buf=DB):
                a = degd[1:2] if row == "deg" else normd[row:row + 1]
                sp.wait_ge(*after)
                sp.dma_start(buf[:, 0:GN], a[:, g * GN:(g + 1) * GN].to_broadcast([P, GN])).then_inc(s_nb if buf is DB else s_nb2, 16)

            def norms_before(row, done, free, free2, buf2):
                for g in range(NG):
                    load_norm(row, g, (free, free2)[g] if g < 2 else (s_pre, done + g - 1), (DB, buf2)[g % 2])

            def conv_norms(p, hp, done=None, row2=None, free2=None, n=None):
                for g in range(NG):
                    slow_loads("conv", p, hp, g)
                    load_norm(0 if p < DEG_OUT else 1, g, (s_pre, done) if g == 0 and done else (s_aggu, p * NG + g))
                    if row2 is not None:
                        load_norm(row2, g, (s_pre, done + g) if g or free2 is None else free2, C)
                    if n is not None and g:
                        store_x(n + g - 1)
                        load_x(n + g)

            degrees("deg_in", DEG_IN, 0)
            norms_before(0, 0, (s_cnt, 2 + BLD), (s_h, NG), C)
            conv_norms(CONV0, 0, NG, 0)
            load_x(NG)
            conv_norms(CONV1, 1, n=NG)
            degrees("deg_out", DEG_OUT, 1)

            def gru_sp(s):
                for g in range(NG):
                    slow_loads("gru", GRU0 + s, FEAT_GRU0 + s, g)
                    load_norm("deg", g, (s_msg, s * NG + g) if not (isinstance(s, int) and s == 0 and g == 0) else (s_aggu, CONV1 * NG + NG))

            gru_sp(0)
            with sp.Fori(1, STEPS - 1) as s:
                gru_sp(s)
            gru_sp(STEPS - 1)
            load_x(2 * NG)
            sp.wait_ge(s_hnew, STEPS * NG)
            sp.dma_start(W[:, 0:2, :], wts[:, W_21:W_21 + 2, :]).then_inc(s_w, 16)
            for g in range(NG):
                store_x(2 * NG + g)
                if g < 2:
                    load_norm(2, g, ((s_msg, STEPS * NG), (s_hnew, STEPS * NG))[g], (DB, B)[g])
                else:
                    load_norm(2, g, (s_pre, 2 * NG + g - 1), (DB, B)[g % 2])
                if g + 1 < NG:
                    load_x(2 * NG + g + 1)
            conv_norms(CONV2, 7, 3 * NG, 2, (s_hTm, 3 * NG))
            load_x(3 * NG)
            conv_norms(CONV3, 8, n=3 * NG)
            store_x(4 * NG - 1)
            sp.wait_ge(s_feat, FEAT_TYPE0 * NG)
            sp.dma_start(W[:, 0:3, :], wts[:, W_E:W_E + 3, :]).then_inc(s_w, 16)
            sp.wait_ge(s_oh, 3 * BLD + (NG - 1) * NT)
            sp.dma_start(beb, be.rearrange("(a t) d -> a t d", a=1).to_broadcast([P, TYPES, D])).then_inc(s_w, 16)
            for t in range(TYPES):
                for g in range(NG):
                    slow_loads("type", TYPE0 + t, FEAT_TYPE0 + t, g, t)
                    buf = (A, B)[g % 2]
                    sp.wait_ge(s_aggu, (TYPE0 + t) * NG + g + 1)
                    sp.dma_start(group(aggd[t], g), buf[:, 0:GN]).then_inc(s_tst, 16)
            sp.wait_ge(s_agg, (TYPE0 + TYPES) * NG)
            sp.wait_ge(s_tst, 16 * TYPES * NG)
            sp.dma_start(WN, wts[:, W_N:W_N + 12, :].rearrange("p (a b) d -> p a (b d)", a=4)).then_inc(s_lw, 16)
            sp.dma_start(bnb, bn.rearrange("(a t) d -> a (t d)", a=1).to_broadcast([P, TYPES * D])).then_inc(s_lw, 16)
            sp.dma_start(nti[0:TN], ntype.rearrange("(t p) -> p t", p=TN), allow_slow_non_contiguous=True).then_inc(s_lw, 16)
            for g in range(NG):
                if g:
                    sp.wait_ge(s_lo, GT * g)
                    sp.wait_ge(s_out, 16 * g)
                for t in range(TYPES):
                    sp.dma_start(part[:, t, :], group(aggd[t], g)).then_inc(s_lx, 16)
                sp.wait_ge(s_xst, 16 * 3 * NG)
                sp.wait_ge(s_norm, 4 * NG)
                sp.dma_start(tiles(X, TN), xs[g * GN:(g + 1) * GN, :].rearrange("(t p) d -> p t d", p=TN)).then_inc(s_lx, 16)
                sp.wait_ge(s_ly, g + 1)
                sp.dma_start(out[g * GN:(g + 1) * GN, :].rearrange("(t p) d -> p t d", p=TN), tiles(X, TN)).then_inc(s_out, 16)
            sp.wait_ge(s_out, 16 * NG)

        @block.gpsimd
        def _(pool):
            pool.memset(identf[:], 0.0).then_inc(s_pown, 1)
            pool.memset(tri, 1.0).then_inc(s_pown, 1)
            pool.memset(U, 1.0).then_inc(s_pown, 1)
            pool.memset(ones[:], 1.0).then_inc(s_pown, 1)
            pool.memset(zeros[:], 0.0).then_inc(s_pown, 1)
            pool.wait_ge(s_pown, 5)
            pool.affine_select(out=identf[:], in_=identf[:], compare_op=ALU.not_equal, fill=1.0, base=0,
                               pattern=[[-1, P]], channel_multiplier=1).then_inc(s_pown, 1)
            pool.affine_select(out=tri, in_=tri, compare_op=ALU.is_gt, fill=0.0, base=0,
                               pattern=[[1, P]], channel_multiplier=-1).then_inc(s_pown, 1)
            pool.affine_select(out=U, in_=U, compare_op=ALU.is_gt, fill=0.0, base=0,
                               pattern=[[-P, 4], [1, NCP]], channel_multiplier=-1).then_inc(s_pown, 1)
            pool.iota(iota1[:], [[1, P]], base=1, channel_multiplier=0, allow_small_or_imprecise_dtypes=True).then_inc(s_pown, 1)
            pool.iota(iotat[:], [[1, NT]], base=0, channel_multiplier=0, allow_small_or_imprecise_dtypes=True).then_inc(s_pown, 1)
            pool.memset(vec[:, V_EPS:V_EPS + 1], EPS).then_inc(s_pown, 1)
            pool.wait_ge(s_pown, 11)
            pool.tensor_copy(identb[:], identf[:]).then_inc(s_const, 1)

            pool.wait_ge(s_ef, 3)
            pool.tensor_copy(keyf[:, 0, :], ef[:, 1, :]).then_inc(s_pown, 1)
            pool.tensor_copy(keyf[:, 1, :], ef[:, 0, :]).then_inc(s_pown, 1)
            for t in range(TYPES):
                pool.tensor_scalar(keyf[:, 2 + t, :], ef[:, 2, :], float(t), None, ALU.is_equal).then_inc(s_pown, 1)
            pool.tensor_scalar(idxf, ef[:, 1, :], 1.0, None, ALU.add).then_inc(s_pown, 1)
            pool.wait_ge(s_pown, 17)
            for t in range(TYPES):
                pool.tensor_tensor(keyf[:, 2 + t, :], keyf[:, 2 + t, :], idxf, ALU.mult).then_inc(s_pown, 1)
            pool.wait_ge(s_pown, 20)
            for t in range(TYPES):
                pool.tensor_scalar(keyf[:, 2 + t, :], keyf[:, 2 + t, :], -1.0, None, ALU.add).then_inc(s_pown, 1)
            for k in range(2):
                pool.tensor_scalar(idxi[:, k, :], ef[:, k, :], 0.0, None, ALU.max).then_inc(s_pown, 1)
            pool.wait_ge(s_pown, 25)
            pool.nop().then_inc(s_kp, 1)

            pool.wait_ge(s_flag, 1)
            fast = pool.value_load(flag[0:1, 0:1], min_val=0, max_val=1)

            def slow_gathers(kind, p, hp, g):
                with pool.If(fast == 0):
                    a = arena(g)
                    n = p * NG + g
                    pool.wait_ge(sl_load, 32 * (n + 1))
                    pool.sem_inc(sl_seen, 1)
                    pool.iota(a["iota"], [[1, GN]], base=g * GN, channel_multiplier=0,
                              allow_small_or_imprecise_dtypes=True).then_inc(sl_iota, 1)
                    if kind[:3] != "deg":
                        m = hp * NG + g
                        pool.wait_ge(sl_rows, 16 * (hp + 1))
                        pool.sem_inc(sl_seen, 1)
                        with pool.Fori(0, SL // 2) as i:
                            for r in range(2):
                                pool.wait_ge(sl_used, n * SL + 2 * i + r + 1)
                                pool.tensor_copy(a["col"][:, r, 0:1], a["idx"][:, bass.ds(LEAD + 2 * i + r, 1)]).then_inc(sl_idx, 1)
                                pool.wait_ge(sl_idx, m * SL + 2 * i + r + 1)
                                pool.sem_inc(sl_seen, 1)
                                if kind == "gru":
                                    to, table = a["rows"][:, r, 0:2 * D].bitcast(F16), hrows16
                                else:
                                    to, table = a["rows"][:, r, :], hrows
                                pool.indirect_dma_start(out=to, out_offset=None, in_=table,
                                                        in_offset=bass.IndirectOffsetOnAxis(ap=a["col"][:, r, 0:1], axis=0)
                                                        ).then_inc(sl_g[g][r], 16)
                with pool.Else():
                    pool.nop()
                pool.nop()

            for g in range(NG):
                slow_gathers("deg_in", DEG_IN, 0, g)
            for p, hp in ((CONV0, 0), (CONV1, 1)):
                for g in range(NG):
                    slow_gathers("conv", p, hp, g)
            for g in range(NG):
                slow_gathers("deg_out", DEG_OUT, 0, g)
            with pool.Fori(0, STEPS) as s:
                for g in range(NG):
                    slow_gathers("gru", GRU0 + s, FEAT_GRU0 + s, g)
            for p, hp in ((CONV2, 7), (CONV3, 8)):
                for g in range(NG):
                    slow_gathers("conv", p, hp, g)
            for t in range(TYPES):
                for g in range(NG):
                    slow_gathers("type", TYPE0 + t, FEAT_TYPE0 + t, g)

        @block.tensor
        def _(pe):
            pe.sem_inc(s_blk, 2)
            pe.sem_inc(sl_used, 2)
            pe.wait_ge(s_const, 1)
            pe.wait_ge(s_rawf, 1)
            for k in range(3):
                for b in range(4):
                    mm = pe.transpose((D0, D0, D1)[k][:, 512 * (k % 2) + P * b:512 * (k % 2) + P * (b + 1)], rawf[:, k, b, :], identf[:])
                mm.then_inc(s_eT, 1)
            pe.wait_ge(s_M, NT)
            for b in range(4):
                cols = min(P, NCP - P * b)
                for sh in range(NT):
                    mm = pe.matmul(D1[0:cols, 512 + NT * b + sh:513 + NT * b + sh], M[:, sh, P * b:P * b + cols], ones[:, 0:1], start=True, stop=True)
            mm.then_inc(s_ctm, 1)
            pe.wait_ge(s_ct, 2)
            ring = [AG[:, 0:NCP], AG[:, 512:512 + NCP], D2[:, 0:NCP], D2[:, 512:512 + NCP]]

            def places_before(sh, r, wait):
                pe.wait_ge(s_gsel, wait)
                for b in range(4):
                    k = min(P, NCP - P * b)
                    pe.matmul(ring[r][:, P * b:NCP], ct[0:k, b, bass.ds(sh, 1)].to_broadcast([k, P]),
                              U[0:k, b, P * b:NCP], start=(b == 0), stop=False, skip_group_check=True)
                mm = pe.matmul(ring[r], tri, M[:, bass.ds(sh, 1), :], start=False, stop=True, skip_group_check=True)
                mm.then_inc(s_G, 1)

            with pe.Fori(0, NT // 4) as i:
                for r in range(4):
                    places_before(4 * i + r, r, 4 * i + r + 1)
            places_before(NT - 1, 0, NT)
            pe.wait_ge(s_V, 3)

            def records(b, r, w):
                pe.wait_ge(s_osl, b + 1)
                pe.wait_ge(s_rec, 2 * b + 2)
                for j in range(WIN):
                    mm = pe.matmul(D0[:, 512 * r:512 * r + 4 * NT], oslot[:, r, j, :], V[:, :, bass.ds(w + j, 1)],
                                   start=(j == 0), stop=(j == WIN - 1))
                mm.then_inc(s_rmm, 1)

            with pe.Fori(0, NT // 2) as i:
                for r in range(2):
                    records(2 * i + r, r, (i * 250 + 125 * r) // 8)
            records(NT - 1, 0, (NT - 1) * 125 // 8)
            pe.wait_ge(s_om, 1)
            pe.matmul(D1[:, 0:2], onesf, occs[:, 0:2], start=True, stop=True).then_inc(s_omm, 1)

            def ln_back(n):
                pe.wait_ge(s_norm, n + 1)
                if n:
                    pe.wait_ge(s_h, n)
                for i in range(GT):
                    mm = pe.transpose(D0[:, P * i:P * i + TN], tiles(C, TN)[:, i, :], identf[0:TN, 0:TN])
                mm.then_inc(s_hTm, 1)

            def ln_in(n):
                g = n % NG
                if n // NG == 2:
                    pe.wait_ge(s_hnew, STEPS * NG)
                else:
                    pe.wait_ge(s_act, n + 1)
                if n > NG:
                    pe.wait_ge(s_h, n)
                for i in range(GT):
                    mm = pe.transpose(D0[0:TN, P * i:P * (i + 1)], group(hT, g)[:, TN * i:TN * (i + 1)], identf[:])
                mm.then_inc(s_xT, 1)

            def dense(ps, w, act, start=True, stop=True):
                for h in range(2):
                    mm = pe.matmul(half(nodes(ps), h), W[:, w, :], half(act, h), start=start, stop=stop)
                return mm

            pe.wait_ge(s_w, 16)
            for n in range(NG):
                ln_back(n)
                pe.wait_ge(s_h, n + 1)
                if n:
                    pe.wait_ge(s_encr, n)
                dense(D2, 0, group(hT, n)).then_inc(s_enc, 1)

            pe.wait_ge(s_flag, 1)
            fast = pe.value_load(flag[0:1, 0:1], min_val=0, max_val=1)

            def step(q, g, j, r):
                t = g * NT + j
                pe.wait_ge(s_oh, q * BLD + t + 1)
                ps, free = blocks(q, g, r)
                pe.wait_ge(s_cnt, q * BLD + t + free)
                if isinstance(j, int) and j == 0:
                    pe.wait_ge(s_cnt, q * BLD + t + 2)
                oh = ohring(q, g, r)
                for i in range(GT):
                    mm = pe.matmul(ps[0:TN, P * i:P * i + TN], oh[:, i, 0:TN], oh[:, GT + i, 0:TN], start=True, stop=True)
                mm.then_inc(s_blk, 1)

            def agg(kind, p, hp, g, inserts=()):
                S = 2 if kind == "gru" else SPLITS
                n = p * NG + g
                what = along(kind, p, g)
                inserts = list(inserts)
                if kind[:3] != "deg" and g:
                    pe.wait_ge(s_feat, hp * NG + NG)
                Hs = H16 if kind == "gru" else H[:]

                def feature(j, k):
                    if kind[:3] == "deg":
                        return ones[0:TN, :]
                    if isinstance(j, int):
                        return Hs[0:TN, (j * S + k) * D:(j * S + k + 1) * D]
                    return Hs[0:TN, bass.ds((j * S + k) * D, D)]

                acc, ring = accumulator(kind, p, g)

                def free():
                    if not (kind == "deg_in" and g < 2):
                        pe.wait_ge(s_aggu, n if g == 0 or ring == 1 else n - 1)
                    if kind == "deg_out" and g == 1:
                        pe.wait_ge(s_h, 2 * NG)

                pe.wait_ge(s_cnt, cnt_of(kind, p, g))
                ks = 1 if kind[:3] == "deg" else S

                def tile(j):
                    if isinstance(j, int) and j == 0:
                        free()
                    for k in range(ks):
                        for h in range(2):
                            at, size = (0, H0) if h == 0 else (H0, H1)
                            mm = pe.matmul(half(nodes(acc), h), feature(j, k), adj[0:TN, bass.ds(g * GP + j * GN + at, size)],
                                           start=(isinstance(j, int) and j == 0 and k == 0), stop=(isinstance(j, int) and j == NT - 1 and k == ks - 1),
                                           skip_group_check=True)
                    if isinstance(j, int) and j == NT - 1:
                        mm.then_inc(s_aggf, 1)

                build = along_step(what, step)

                def tile_and_step(j, r):
                    tile(j)
                    if build:
                        build(j, r)

                with pe.If(fast == 1):
                    weave(pe, inserts, tile_and_step)
                with pe.Else():
                    weave(pe, inserts, build)
                    if kind[:3] != "deg":
                        pe.wait_ge(s_feat, hp * NG + NG)
                    free()
                    a = arena(g)
                    for h in range(2):
                        pe.matmul(half(nodes(acc), h), zeros[:], iota1[:, 0:1].to_broadcast([P, (H0, H1)[h]]), start=True, stop=False, skip_group_check=True)
                    with pe.Fori(0, SL // 2) as i:
                        for r in range(2):
                            pe.wait_ge(sl_oh, n * SL + 2 * i + r + 1)
                            if kind[:3] != "deg":
                                pe.wait_ge(sl_g[g][r], 16 * (hp * (SL // 2) + i + 1))
                            for k in range(1 if kind[:3] == "deg" else S):
                                rows = a["rows"][:, r, k * D:(k + 1) * D]
                                if kind == "gru":
                                    rows = rows.bitcast(F16)
                                for h in range(2):
                                    mm = pe.matmul(half(nodes(acc), h), ones[:] if kind[:3] == "deg" else rows, half(a["oh"][:, r, :], h),
                                                   start=False, stop=False, skip_group_check=True)
                            mm.then_inc(sl_used, 1)
                    for h in range(2):
                        mm = pe.matmul(half(nodes(acc), h), zeros[:], iota1[:, 0:1].to_broadcast([P, (H0, H1)[h]]), start=False, stop=True, skip_group_check=True)
                    mm.then_inc(s_aggf, 1)
                if kind == "conv" and isinstance(p, int) and p < DEG_OUT:
                    for i in range(GT):
                        for k in range(SPLITS):
                            mm = pe.matmul(nodes(acc)[:, TN * i:TN * (i + 1)], feature(g * GT + i, k), identb[0:TN, 0:TN],
                                           start=False, stop=(k == SPLITS - 1), skip_group_check=True)
                    mm.then_inc(s_agg, 1)
                else:
                    pe.wait_ge(s_aggf, n + 1)
                    pe.nop().then_inc(s_agg, 1)

            def nm(kind, hp, g, w=0, first=0, after=0):
                ps = D2 if kind == "gru" else D0
                m = hp * NG + g
                if kind == "conv":
                    pe.wait_ge(s_pre, first + g + 1)
                elif kind == "type":
                    pe.wait_ge(s_h, 4 * NG)
                if g == 0:
                    pe.wait_ge(s_aggu, after)
                elif kind == "gru":
                    pe.wait_ge(s_feat, m)
                else:
                    pe.wait_ge(s_r1, mid_of(hp, g - 1) + 1)
                if kind == "gru" and g == NG - 1 and after > GRU0 * NG:
                    pe.wait_ge(s_hnew, after - GRU0 * NG)
                for i in range(GT):
                    at = TN * i
                    if kind == "gru":
                        mm = pe.transpose(ps[0:TN, P * i:P * (i + 1)], group(hT, g)[:, at:at + TN], identf[:])
                    else:
                        mm = pe.matmul(ps[0:TN, P * i:P * (i + 1)], group(hT, g)[:, at:at + TN], W[:, w, :], start=True, stop=True)
                mm.then_inc(s_nm, 1)

            def sums(kind, p, hp, w=0, first=0, n=None):
                for g in range(NG):
                    ins = []
                    if g == 0 and kind[:3] != "deg":
                        at = NM_AT_GRU if kind == "gru" else NM_AT
                        ins = [(at[k], lambda k=k: nm(kind, hp, k, w, first, p * NG)) for k in range(NG)]
                        ins += [(GT * k, lambda k=k: pe.wait_ge(s_feat, hp * NG + k + 1)) for k in range(NG)]
                    if n is not None and (g or kind == "deg_out"):
                        m = n + g - 1
                        ins = [(1, lambda: ln_in(m)), (8, lambda: ln_back(m))]
                    if kind == "gru" and (g or not isinstance(p, int) or p > GRU0):
                        ins += gates(p * NG + g - 1 - GRU0 * NG, (g - 1) % NG)
                    agg(kind, p, hp, g, ins)

            pe.wait_ge(s_encr, NG)
            pe.wait_ge(s_h, NG)
            steps(pe, (0, 0), step)
            sums("deg_in", DEG_IN, 0)
            sums("conv", CONV0, 0, 1, 0)
            sums("conv", CONV1, 1, 2, NG, NG)
            agg("deg_out", DEG_OUT, 0, 0, [(1, lambda: ln_in(2 * NG - 1)), (8, lambda: ln_back(2 * NG - 1))])
            for g in range(1, NG):
                agg("deg_out", DEG_OUT, 0, g)
            pe.wait_ge(s_w, 32)
            pe.wait_ge(s_h, 2 * NG)

            def gates(n, g):
                h = group(hT, g)

                def message():
                    pe.wait_ge(s_aggu, GRU0 * NG + n + 1)
                    if not (isinstance(n, int) and n == 0):
                        pe.wait_ge(s_hnew, n)
                    dense(D0, 0, X).then_inc(s_pmsg, 1)

                def r_and_z():
                    pe.wait_ge(s_msg, n + 1)
                    dense(D1, 1, B, True, False)
                    dense(D1, 4, h, False, True)
                    dense(D0, 2, B, True, False)
                    dense(D0, 5, h, False, True).then_inc(s_prz, 1)

                def new():
                    pe.wait_ge(s_sig, 2 * n + 1)
                    dense(D1, 6, h)
                    pe.wait_ge(s_sig, 2 * n + 2)
                    dense(D0, 3, B).then_inc(s_pn, 1)
                return [(1, message), (4, r_and_z), (8, new)]

            def gru_pe(s):
                sums("gru", GRU0 + s, FEAT_GRU0 + s)

            gru_pe(0)
            with pe.Fori(1, STEPS - 1) as s:
                gru_pe(s)
            gru_pe(STEPS - 1)
            for _, f in gates(STEPS * NG - 1, NG - 1):
                f()
            for n in range(2 * NG, 3 * NG):
                ln_in(n)
                ln_back(n)
            pe.wait_ge(s_w, 48)
            pe.wait_ge(s_h, 3 * NG)
            sums("conv", CONV2, 7, 0, 2 * NG)
            sums("conv", CONV3, 8, 1, 3 * NG, 3 * NG)
            ln_in(4 * NG - 1)
            ln_back(4 * NG - 1)
            pe.wait_ge(s_w, 80)
            for t in range(TYPES):
                sums("type", TYPE0 + t, FEAT_TYPE0 + t, t)
            pe.wait_ge(s_lw, 48)
            banks = [D1[0:TN, 0:384], D1[0:TN, 512:896], D2[0:TN, 0:384], D2[0:TN, 512:896]]
            for g in range(NG):
                pe.wait_ge(s_lx, 64 * (g + 1))
                if g:
                    pe.wait_ge(s_ly, g)
                for i in range(GT):
                    n = g * GT + i
                    at = TN * i
                    h = group(hT, g)[:, at:at + TN]
                    pe.transpose(D0[0:TN, P * i:P * (i + 1)], h, identf[:])
                    if n >= 4:
                        pe.wait_ge(s_lt, n - 3)
                    pe.matmul(banks[n % 4], h, WN[:, 0, :], start=True, stop=False)
                    for t in range(TYPES):
                        mm = pe.matmul(banks[n % 4], part[:, t, at:at + TN], WN[:, 1 + t, :], start=False, stop=(t == TYPES - 1))
                    mm.then_inc(s_lo, 1)

        @block.vector
        def _(dve):
            own = [0]

            def mine(ins):
                own[0] += 1
                ins.then_inc(s_own, 1)
                dve.wait_ge(s_own, own[0])

            dve.sem_inc(s_gsel, 4)
            dve.memset(raw[:, :, 3, :], -1).then_inc(s_rawm, 1)
            dve.memset(ef[:, :, 0:LEAD], -1.0)
            dve.wait_ge(s_raw, 16 * 9)
            dve.wait_ge(s_rawm, 1)
            dve.tensor_copy(rawf.rearrange("p a b c -> p (a b c)"), raw.rearrange("p a b c -> p (a b c)")).then_inc(s_rawf, 1)
            for k in range(3):
                dve.wait_ge(s_eT, k + 1)
                dve.tensor_copy(ef[:, k, LEAD:NCP], (D0, D0, D1)[k][:, 512 * (k % 2):512 * (k % 2) + NCP - LEAD]).then_inc(s_ef, 1)
            dve.wait_ge(s_ef, 3)
            mine(dve.tensor_scalar(qi, ef[:, 0:2, :], 1.0 / TN, 0.5 / TN - 0.5, ALU.mult, ALU.add))
            mine(dve.tensor_copy(qf, qi))
            dve.tensor_copy(stile, qf[:, 0, :])
            mine(dve.scalar_tensor_tensor(out=qrem, in0=qf, scalar=-float(TN), in1=ef[:, 0:2, :], op0=ALU.mult, op1=ALU.add))
            for sh in range(NT):
                dve.tensor_scalar(M[:, sh, :], stile, float(sh), None, ALU.is_equal).then_inc(s_M, 1)
            dve.tensor_scalar(val[:, 0:2, :], qrem, 1.0, None, ALU.add)
            mine(dve.tensor_scalar(val[:, 2, :], ef[:, 2, :], 1.0, None, ALU.add))
            for k in range(3):
                dve.tensor_tensor(V[:, NT * k:NT * (k + 1), :], M, val[:, k:k + 1, :].to_broadcast([P, NT, NCP]), ALU.mult).then_inc(s_V, 1)

            def select(sh, r, v):
                dve.wait_ge(s_G, v)
                dve.scalar_tensor_tensor(out=gsel[:, bass.ds(sh, 1), :].rearrange("p a c -> p (a c)"), in0=stile, scalar=iotat[:, bass.ds(sh, 1)],
                                         in1=(AG, AG, D2, D2)[r][:, 512 * (r % 2):512 * (r % 2) + NCP],
                                         op0=ALU.is_equal, op1=ALU.mult).then_inc(s_gsel, 1)

            dve.wait_ge(s_const, 1)
            with dve.Fori(0, NT // 4) as i:
                for r in range(4):
                    select(4 * i + r, r, 4 * i + r + 1)
            select(NT - 1, 0, NT)
            dve.wait_ge(s_gsel, NT + 4)
            mine(dve.tensor_reduce(slot1, gsel.rearrange("p a c -> p c a"), AX, ALU.add))
            mine(dve.tensor_copy(gsum, slot1))
            mine(dve.tensor_scalar(gslot, gsum, P - 1, None, ALU.bitwise_and))
            mine(dve.tensor_scalar(slot1, gslot, 1.0, None, ALU.add))

            def slots(b, r, w):
                dve.wait_ge(s_rmm, b + 1)
                dve.scalar_tensor_tensor(out=slotb[:, r, :].rearrange("p (c d) -> p c d", d=4),
                                         in0=qf[:, 1, bass.ds(w, WIN)].unsqueeze(2).to_broadcast([P, WIN, 4]), scalar=iotat[:, bass.ds(b, 1)],
                                         in1=slot1[:, bass.ds(w, WIN)].unsqueeze(2).to_broadcast([P, WIN, 4]),
                                         op0=ALU.is_equal, op1=ALU.mult).then_inc(s_slotb, 1)
                dve.wait_ge(s_slotb, b + 1)
                dve.tensor_tensor(oslot[:, r, :, :].rearrange("p c (v d) -> p c v d", d=4),
                                  iota1[:].rearrange("p (v d) -> p v d", d=4).unsqueeze(1).to_broadcast([P, WIN, P // 4, 4]),
                                  slotb[:, r, :].rearrange("p (c d) -> p c d", d=4).unsqueeze(2).to_broadcast([P, WIN, P // 4, 4]),
                                  ALU.is_equal).then_inc(s_osl, 1)

            dve.sem_inc(s_rmm, 2)
            with dve.Fori(0, NT // 2) as i:
                for r in range(2):
                    slots(2 * i + r, r, (i * 250 + 125 * r) // 8)
            slots(NT - 1, 0, (NT - 1) * 125 // 8)
            dve.wait_ge(s_rec, 4 + 2 * NT)
            occ = B[:, 0:NT * NT]
            mine(dve.tensor_reduce(occs[:, 2:3], occ, AX, ALU.max))
            mine(dve.tensor_reduce(occs[:, 1:2], occ, AX, ALU.add))
            mine(dve.memset(onesf, 1.0))
            dve.tensor_scalar(occs[:, 0:1], occs[:, 2:3], 1.5, None, ALU.is_gt).then_inc(s_om, 1)
            dve.wait_ge(s_omm, 1)
            mine(dve.tensor_copy(occs[:, 2:4], D1[:, 0:2]))
            mine(dve.tensor_scalar(occs[:, 0:1], occs[:, 2:3], 0.5, None, ALU.is_lt))
            mine(dve.tensor_scalar(occs[:, 1:2], occs[:, 3:4], float(E), None, ALU.is_equal))
            dve.tensor_tensor(flag[:], occs[:, 0:1], occs[:, 1:2], ALU.mult).then_inc(s_flag, 1)

            dve.wait_ge(s_par, 16)
            dve.wait_ge(s_vstd, 1)
            v = lambda k: vec[:, k:k + 1]
            mine(dve.reciprocal(v(V_STD), v(V_STD)))
            mine(dve.tensor_tensor(v(V_SCALE), v(V_GAMMA), v(V_STD), ALU.mult))
            mine(dve.tensor_tensor(v(V_SHIFT), v(V_MEAN), v(V_SCALE), ALU.mult))
            mine(dve.tensor_tensor(v(V_SHIFT), v(V_BETA), v(V_SHIFT), ALU.subtract))
            dve.tensor_tensor(v(V_BR), v(V_BIR), v(V_BHR), ALU.add)
            dve.tensor_tensor(v(V_BZ), v(V_BIZ), v(V_BHZ), ALU.add).then_inc(s_vec, 1)

            def ln_parts(n):
                xt = tiles(X, TN)

                def sums():
                    dve.wait_ge(s_xl, 16 * (n + 1))
                    if n >= NG:
                        dve.wait_ge(s_xT, n - NG + 1)
                        dve.tensor_tensor(xt, xt, tiles(D0, TN), ALU.add).then_inc(s_xsum, 1)
                        dve.wait_ge(s_xsum, n - NG + 1)
                    for i in range(GT):
                        st = dve.bn_stats(stats[0:TN, i, :], xt[:, i, :])
                    st.then_inc(s_bn, 1)

                def moments():
                    dve.wait_ge(s_bn, n + 1)
                    for i in range(GT):
                        st = dve.bn_aggr(mv[0:TN, i, :], stats[0:TN, i, :])
                    st.then_inc(s_mv, 1)

                def scale():
                    dve.wait_ge(s_std, n + 1)
                    mine(dve.reciprocal(rstd[0:TN, :], rstd[0:TN, :]))
                    if n:
                        dve.wait_ge(s_hTm, n)
                    for i in range(GT):
                        st = dve.tensor_scalar(tiles(C, TN)[:, i, :], xt[:, i, :], mv[0:TN, i, 0:1], rstd[0:TN, i:i + 1], ALU.subtract, ALU.mult)
                    st.then_inc(s_norm, 1)
                return [(2, sums), (3, moments), (6, scale)]

            def ln(n):
                for _, f in ln_parts(n):
                    f()

            dve.wait_ge(s_vec, 1)
            for n in range(NG + 1):
                if n < NG:
                    ln(n)
                if n:
                    dve.wait_ge(s_encr, n)
                    dve.tensor_scalar(group(hT, n - 1), (A, B)[(n - 1) % 2][:, 0:GN], v(V_SCALE), v(V_SHIFT), ALU.mult, ALU.add).then_inc(s_bnh, 1)

            fast = dve.value_load(flag[0:1, 0:1], min_val=0, max_val=1)

            def prepare(q, g):
                dup = dup_of(q, g)
                n = q * BLD + g * NT
                if n:
                    dve.wait_ge(s_oh, n)
                if q > 2:
                    dve.wait_ge(s_blk, n + 1)
                    rect = ohring(q, g, parity(q, g, 0))[:, 0, 0:NT * GT].rearrange("p (i j) -> p i j", j=NT)
                    mine(dve.scalar_tensor_tensor(out=rect, in0=rec[:, 2, GT * g:GT * (g + 1), :], scalar=float(q - 2),
                                                  in1=rec[:, 1, GT * g:GT * (g + 1), :], op0=ALU.is_equal, op1=ALU.mult))
                for kind in range(2):
                    if q == 1:
                        r = rec[:, 1 - kind, :, GT * g:GT * (g + 1)]
                    elif q > 2 and kind == 1:
                        r = rect.rearrange("p i j -> p j i")
                    else:
                        r = rec[:, kind, GT * g:GT * (g + 1), :].rearrange("p i j -> p j i")
                    ins = dve.tensor_copy(dup[:, :, GT * kind:GT * (kind + 1), :], r.unsqueeze(3).to_broadcast([P, NT, GT, 4]))
                ins.then_inc(s_dup, 1)
                dve.wait_ge(s_dup, q * NG + g + 1)

            def step(q, g, j, r):
                dve.wait_ge(s_blk, q * BLD + g * NT + j + 1)
                dve.tensor_tensor(ohring(q, g, r).rearrange("p i (v d) -> p i v d", d=4),
                                  iota1[:].rearrange("p (v d) -> p v d", d=4).unsqueeze(1).to_broadcast([P, 2 * GT, P // 4, 4]),
                                  dup_of(q, g)[:, bass.ds(j, 1), :, :].rearrange("p a i d -> p (a i) d").unsqueeze(2).to_broadcast([P, 2 * GT, P // 4, 4]),
                                  ALU.is_equal).then_inc(s_oh, 1)

            def build_along(kind, p, g, inserts=()):
                what = along(kind, p, g)
                if what:
                    prepare(*what)
                weave(dve, inserts, along_step(what, step))

            def slow_hots(kind, p, g):
                with dve.If(fast == 0):
                    a = arena(g)
                    n = p * NG + g
                    dve.wait_ge(sl_load, 32 * (n + 1))
                    dve.wait_ge(sl_iota, n + 1)
                    dve.sem_inc(sl_seen, 1)
                    with dve.Fori(0, SL // 2) as i:
                        for r in range(2):
                            dve.wait_ge(sl_used, n * SL + 2 * i + r + 1)
                            dve.tensor_scalar(a["oh"][:, r, 0:GN], a["iota"], a["key"][:, bass.ds(LEAD + 2 * i + r, 1)], None, ALU.is_equal).then_inc(sl_oh, 1)
                with dve.Else():
                    dve.nop()
                dve.nop()

            def degrees(kind, p, d):
                for g in range(NG):
                    build_along(kind, p, g, ln_parts(2 * NG - 1) if d and g == 0 else ())
                    slow_hots(kind, p, g)
                    dve.wait_ge(s_agg, p * NG + g + 1)
                    if g:
                        dve.wait_ge(s_degst, 16 * (d * NG + g))
                    elif d:
                        dve.wait_ge(s_act, 2 * NG)
                    dve.tensor_copy(A[:, 0:GN], nodes(accumulator(kind, p, g)[0])).then_inc(s_aggu, 1)
                dve.wait_ge(s_degl, 16 * (d + 1))
                deg = A[0:TN, 0:NT]
                if d == 0:
                    mine(dve.tensor_scalar(A[0:TN, 128:128 + NT], deg, 1.0, None, ALU.add))
                dve.tensor_scalar(A[0:TN, 192:192 + NT], deg, 1.0, None, ALU.max).then_inc(s_degf, 1)
                dve.wait_ge(s_degs, d + 1)
                if d == 0:
                    mine(dve.reciprocal(A[0:TN, 128:128 + NT], A[0:TN, 128:128 + NT]))
                dve.reciprocal(A[0:TN, 192:192 + NT], A[0:TN, 192:192 + NT]).then_inc(s_norms, 1)

            def pre(j, g):
                p = {1: CONV0, 3: CONV2}.get(j)
                if p is None:
                    first, second = NB[f"pre{j}"], NB2[f"pre{j}"]
                    buf = (DB, C if j == 0 else B)[g % 2]
                    if g % 2 == 0:
                        dve.wait_ge(s_nb, 16 * (first + g // 2 + 1))
                    else:
                        dve.wait_ge(s_nb2, 16 * (second + g // 2 + 1))
                    if j == 2:
                        dve.wait_ge(s_h, 2 * NG + g + 1)
                else:
                    buf = C
                    dve.wait_ge(s_nb2, 16 * (NB2[p] + g + 1))
                    dve.wait_ge(s_act, conv_no(p) * NG + g + 1)
                dve.tensor_tensor(group(hT, g), group(hT, g), buf[:, 0:GN], ALU.mult).then_inc(s_pre, 1)

            def split3(hp, g, src, at):
                m = hp * NG + g
                Ht = H[0:TN, :].rearrange("p (t k d) -> p t k d", k=SPLITS, d=D)[:, GT * g:GT * (g + 1)]

                def rest1():
                    dve.wait_ge(s_hi, m + 1)
                    if m:
                        dve.wait_ge(s_feat, m)
                    dve.tensor_tensor(tiles(A, TN), src, Ht[:, :, 0, :], ALU.subtract).then_inc(s_r1, 1)

                def rest2():
                    dve.wait_ge(s_mid, mid_of(hp, g) + 1)
                    dve.tensor_tensor(Ht[:, :, 2, :], tiles(A, TN), Ht[:, :, 1, :], ALU.subtract).then_inc(s_feat, 1)
                return [(at + 2, rest1), (at + 4, rest2)]

            def splits3(hp):
                return [e for g in range(NG) for e in split3(hp, g, tiles(D0, TN), NM_AT[g])]

            def splits2(hp):
                def split2(g):
                    m = hp * NG + g
                    Ht = H16[0:TN].rearrange("p (t k d) -> p t k d", k=2, d=D)[:, GT * g:GT * (g + 1)]
                    dve.wait_ge(s_hi, m + 1)
                    dve.tensor_tensor(Ht[:, :, 1, :], tiles(D2, TN), Ht[:, :, 0, :], ALU.subtract).then_inc(s_feat, 1)
                return [(NM_AT_GRU[g] + 2, lambda g=g: split2(g)) for g in range(NG)]

            def splits_type(t):
                def bias(g):
                    dve.wait_ge(s_nm, (FEAT_TYPE0 + t) * NG + g + 1)
                    if t * NG + g:
                        dve.wait_ge(s_erelu, t * NG + g)
                    if t and g == 0:
                        dve.wait_ge(s_tst, 16 * t * NG)
                    dve.tensor_tensor(tiles(C, TN), tiles(D0, TN), beb[0:TN, t:t + 1, :].to_broadcast([TN, GT, D]), ALU.add).then_inc(s_ebias, 1)
                out = []
                for g in range(NG):
                    at = NM_AT[g]
                    out.append((at + 1, lambda g=g: bias(g)))
                    out += split3(FEAT_TYPE0 + t, g, tiles(B, TN), at + 1)
                return out

            def conv(p, g, inserts=(), n=None):
                if n is not None and g:
                    inserts = ln_parts(n + g - 1)
                build_along("conv", p, g, inserts)
                if p in (CONV0, CONV2) and g:
                    pre(1 if p == CONV0 else 3, g - 1)
                slow_hots("conv", p, g)
                dve.wait_ge(s_agg, p * NG + g + 1)
                dve.wait_ge(s_nb, 16 * (NB[p] + g + 1))
                if conv_no(p) * NG + g:
                    dve.wait_ge(s_act, conv_no(p) * NG + g)
                dve.tensor_tensor(A[:, 0:GN], nodes(accumulator("conv", p, g)[0]), DB[:, 0:GN], ALU.mult).then_inc(s_aggu, 1)

            dve.wait_ge(s_bnh, NG)
            prepare(0, 0)
            steps(dve, (0, 0), step)
            degrees("deg_in", DEG_IN, 0)
            for g in range(NG):
                pre(0, g)
            for g in range(NG):
                conv(CONV0, g, splits3(0) if g == 0 else ())
            pre(1, NG - 1)
            for g in range(NG):
                conv(CONV1, g, splits3(1) if g == 0 else (), NG)
            degrees("deg_out", DEG_OUT, 1)

            def gru(n, g):
                h = group(hT, g)
                b = B[:, 0:GN]
                a = A[:, 0:GN]

                def message():
                    dve.wait_ge(s_pmsg, n + 1)
                    dve.wait_ge(s_nb, 16 * (NB["gru"] + n + 1))
                    dve.scalar_tensor_tensor(out=b, in0=DB[:, 0:GN], scalar=v(V_BMSG), in1=nodes(D0), op0=ALU.mult, op1=ALU.add).then_inc(s_msg, 1)

                def new():
                    dve.wait_ge(s_pn, n + 1)
                    dve.wait_ge(s_sig, 2 * n + 2)
                    dve.scalar_tensor_tensor(out=a, in0=nodes(D1), scalar=v(V_BHN), in1=a, op0=ALU.add, op1=ALU.mult).then_inc(s_gown, 1)
                    dve.wait_ge(s_gown, 3 * n + 1)
                    dve.tensor_tensor(a, a, nodes(D0), ALU.add).then_inc(s_gpre, 1)

                def state1():
                    dve.wait_ge(s_gtanh, n + 1)
                    dve.tensor_tensor(b, h, a, ALU.subtract).then_inc(s_gown, 1)

                def state2():
                    dve.wait_ge(s_gown, 3 * n + 2)
                    dve.tensor_tensor(b, b, C[:, 0:GN], ALU.mult).then_inc(s_gown, 1)

                def state3():
                    dve.wait_ge(s_gown, 3 * n + 3)
                    dve.tensor_tensor(h, a, b, ALU.add).then_inc(s_hnew, 1)
                return [(2, message), (10, new), (13, state1), (14, state2), (15, state3)]

            def gru_dve(s):
                for g in range(NG):
                    ins = splits2(FEAT_GRU0 + s) if g == 0 else []
                    if g or not (isinstance(s, int) and s == 0):
                        ins += gru(s * NG + g - 1, (g - 1) % NG)
                    build_along("gru", GRU0 + s, g, ins)
                    slow_hots("gru", GRU0 + s, g)

            gru_dve(0)
            with dve.Fori(1, STEPS - 1) as s:
                gru_dve(s)
            gru_dve(STEPS - 1)
            for _, f in gru(STEPS * NG - 1, NG - 1):
                f()
            for n in range(2 * NG, 3 * NG):
                ln(n)
                if n > 2 * NG:
                    pre(2, n - 1 - 2 * NG)
            pre(2, NG - 1)
            dve.wait_ge(s_pre, 3 * NG)
            for g in range(NG):
                conv(CONV2, g, splits3(7) if g == 0 else ())
            pre(3, NG - 1)
            for g in range(NG):
                conv(CONV3, g, splits3(8) if g == 0 else (), 3 * NG)
            ln(4 * NG - 1)
            dve.wait_ge(s_xst, 16 * 3 * NG)
            dve.wait_ge(s_norm, 4 * NG)
            dve.wait_ge(s_w, 80)
            for t in range(TYPES):
                for g in range(NG):
                    build_along("type", TYPE0 + t, g, splits_type(t) if g == 0 else ())
                    slow_hots("type", TYPE0 + t, g)

            dve.wait_ge(s_lw, 48)
            mine(dve.tensor_copy(ntf[0:TN], nti[0:TN]))
            for t in range(TYPES):
                mine(dve.tensor_scalar(mask[0:TN, t, :], ntf[0:TN], float(t), None, ALU.is_equal))
            for g in range(NG):
                dve.wait_ge(s_lx, 64 * (g + 1))
                for i in range(GT):
                    n = g * GT + i
                    y = tmp[0:TN, n % 2, :]
                    xt = tiles(X, TN)[:, i, :]
                    dve.wait_ge(s_lo, n + 1)
                    dve.tensor_tensor(y, (D1, D1, D2, D2)[n % 4][0:TN, 512 * (n % 2):512 * (n % 2) + TYPES * D], bnb[0:TN], ALU.add).then_inc(s_lt, 1)
                    dve.wait_ge(s_lt, n + 1)
                    for t in range(TYPES):
                        mine(dve.scalar_tensor_tensor(out=xt, in0=y[:, D * t:D * (t + 1)], scalar=mask[0:TN, t, n:n + 1], in1=xt, op0=ALU.mult, op1=ALU.add))
                dve.tensor_tensor(tiles(X, TN), tiles(X, TN), tiles(D0, TN), ALU.add).then_inc(s_ly, 1)

        @block.scalar
        def _(act):
            act.sem_inc(s_rec, 4)
            act.sem_inc(s_cnt, 2)
            v = lambda k: vec[:, k:k + 1]
            act.wait_ge(s_par, 16)
            act.wait_ge(s_const, 1)
            act.activation(v(V_STD), v(V_VAR), ACT.Sqrt, bias=v(V_EPS)).then_inc(s_vstd, 1)
            act.wait_ge(s_ctm, 1)
            act.copy(ct[:, 0:3, :], D1[:, 512:512 + 3 * NT].rearrange("p (a b) -> p a b", a=3)).then_inc(s_ct, 1)
            act.copy(ct[0:NCP - 3 * P, 3, :], D1[0:NCP - 3 * P, 512 + 3 * NT:512 + 4 * NT]).then_inc(s_ct, 1)

            def take(b, r):
                act.wait_ge(s_rmm, b + 3)
                act.copy(rec[:, :, bass.ds(b, 1), :].rearrange("p k a s -> p k (a s)"), D0[:, 512 * r:512 * r + 3 * NT].rearrange("p (k s) -> p k s", k=3)).then_inc(s_rec, 1)
                act.copy(B[:, bass.ds(b * NT, NT)], D0[:, 512 * r + 3 * NT:512 * r + 4 * NT]).then_inc(s_rec, 1)

            with act.Fori(0, NT // 2) as i:
                for r in range(2):
                    take(2 * i + r, r)
            take(NT - 1, 0)

            def ln_std(n):
                act.wait_ge(s_mv, n + 1)
                act.activation(rstd[0:TN, :], mv[0:TN, :, 1], ACT.Sqrt, bias=vec[0:TN, V_EPS:V_EPS + 1]).then_inc(s_std, 1)

            def ln_h(n):
                act.wait_ge(s_hTm, n + 1)
                act.activation(group(hT, n % NG).rearrange("p (t n) -> p t n", t=GT), tiles(D0)[:, :, 0:TN], ACT.Relu).then_inc(s_h, 1)

            def ln_parts(n):
                return [(4, lambda: ln_std(n)), (9, lambda: ln_h(n))]

            act.wait_ge(s_flag, 1)
            for n in range(NG):
                ln_std(n)
                ln_h(n)
                act.wait_ge(s_enc, n + 1)
                if n > 1:
                    act.wait_ge(s_bnh, n - 1)
                act.activation((A, B)[n % 2][:, 0:GN], nodes(D2), ACT.Relu, bias=v(V_BENC)).then_inc(s_encr, 1)

            def step(q, g, j, r):
                act.wait_ge(s_blk, q * BLD + g * NT + j + 3)
                act.copy(adj[0:TN, bass.ds(g * GP + j * GN, GN)].rearrange("p (i n) -> p i n", i=GT), tiles(blocks(q, g, r)[0], TN)[:, :, 0:TN]).then_inc(s_cnt, 1)

            def build_along(kind, p, g, inserts=()):
                weave(act, inserts, along_step(along(kind, p, g), step))

            def part3(hp, g, src, at):
                m = hp * NG + g
                Ht = H[0:TN, :].rearrange("p (t k d) -> p t k d", k=SPLITS, d=D)[:, GT * g:GT * (g + 1)]

                def hi():
                    act.wait_ge(s_nm, m + 1)
                    act.copy(Ht[:, :, 0, :], src).then_inc(s_hi, 1)

                def mid():
                    act.wait_ge(s_r1, mid_of(hp, g) + 1)
                    act.copy(Ht[:, :, 1, :], tiles(A, TN)).then_inc(s_mid, 1)
                return [(at + 1, hi), (at + 3, mid)]

            def parts3(hp):
                return [e for g in range(NG) for e in part3(hp, g, tiles(D0, TN), NM_AT[g])]

            def parts2(hp):
                def hi(g):
                    act.wait_ge(s_nm, hp * NG + g + 1)
                    Ht = H16[0:TN].rearrange("p (t k d) -> p t k d", k=2, d=D)[:, GT * g:GT * (g + 1)]
                    act.copy(Ht[:, :, 0, :], tiles(D2, TN)).then_inc(s_hi, 1)
                return [(NM_AT_GRU[g] + 1, lambda g=g: hi(g)) for g in range(NG)]

            def parts_type(t):
                def relu(g):
                    act.wait_ge(s_ebias, t * NG + g + 1)
                    if t * NG + g:
                        act.wait_ge(s_r1, mid_of(FEAT_TYPE0 + t, g))
                    if t and g == 0:
                        act.wait_ge(s_tst, 16 * t * NG)
                    act.activation(tiles(B, TN), tiles(C, TN), ACT.Relu).then_inc(s_erelu, 1)
                    act.wait_ge(s_erelu, t * NG + g + 1)
                out = []
                for g in range(NG):
                    at = NM_AT[g]
                    out.append((at + 2, lambda g=g: relu(g)))
                    out += part3(FEAT_TYPE0 + t, g, tiles(B, TN), at + 1)
                return out

            def conv(p, g, bias, relu, inserts=(), n=None):
                if n is not None and g:
                    inserts = ln_parts(n + g - 1)
                build_along("conv", p, g, inserts)
                act.wait_ge(s_aggu, p * NG + g + 1)
                act.activation(group(hT, g), A[:, 0:GN], ACT.Relu if relu else ACT.Identity, bias=v(bias)).then_inc(s_act, 1)

            def norms(d):
                act.wait_ge(s_degf, d + 1)
                if d == 0:
                    act.activation(A[0:TN, 128:128 + NT], A[0:TN, 128:128 + NT], ACT.Sqrt)
                act.activation(A[0:TN, 192:192 + NT], A[0:TN, 192:192 + NT], ACT.Sqrt).then_inc(s_degs, 1)

            act.wait_ge(s_kp, 1)
            steps(act, (0, 0), step)
            for g in range(NG):
                build_along("deg_in", DEG_IN, g)
            norms(0)
            for g in range(NG):
                conv(CONV0, g, V_B01, True, parts3(0) if g == 0 else ())
            for g in range(NG):
                conv(CONV1, g, V_B02, False, parts3(1) if g == 0 else (), NG)
            build_along("deg_out", DEG_OUT, 0, ln_parts(2 * NG - 1))
            norms(1)

            def gru(n):
                def r():
                    act.wait_ge(s_prz, n + 1)
                    act.activation(A[:, 0:GN], nodes(D1), ACT.Sigmoid, bias=v(V_BR)).then_inc(s_sig, 1)

                def z():
                    act.activation(C[:, 0:GN], nodes(D0), ACT.Sigmoid, bias=v(V_BZ)).then_inc(s_sig, 1)

                def new():
                    act.wait_ge(s_gpre, n + 1)
                    act.activation(A[:, 0:GN], A[:, 0:GN], ACT.Tanh, bias=v(V_BIN)).then_inc(s_gtanh, 1)
                return [(6, r), (7, z), (12, new)]

            def gru_act(s):
                for g in range(NG):
                    p = GRU0 + s
                    ins = parts2(FEAT_GRU0 + s) if g == 0 else []
                    if g or not (isinstance(s, int) and s == 0):
                        ins += gru(s * NG + g - 1)
                    build_along("gru", p, g, ins)
                    act.wait_ge(s_agg, p * NG + g + 1)
                    if isinstance(s, int) and s == 0 and g == 0:
                        act.wait_ge(s_xst, 16 * NG)
                        act.wait_ge(s_norm, 2 * NG)
                    else:
                        act.wait_ge(s_pmsg, s * NG + g)
                    act.copy(X[:, 0:GN], nodes(accumulator("gru", p, g)[0])).then_inc(s_aggu, 1)

            gru_act(0)
            with act.Fori(1, STEPS - 1) as s:
                gru_act(s)
            gru_act(STEPS - 1)
            for _, f in gru(STEPS * NG - 1):
                f()
            for n in range(2 * NG, 3 * NG):
                ln_std(n)
                ln_h(n)
            for g in range(NG):
                conv(CONV2, g, V_B21, True, parts3(7) if g == 0 else ())
            for g in range(NG):
                conv(CONV3, g, V_B22, True, parts3(8) if g == 0 else (), 3 * NG)
            ln_std(4 * NG - 1)
            ln_h(4 * NG - 1)
            for t in range(TYPES):
                for g in range(NG):
                    p = TYPE0 + t
                    build_along("type", p, g, parts_type(t) if g == 0 else ())
                    act.wait_ge(s_agg, p * NG + g + 1)
                    k = t * NG + g
                    if k:
                        act.wait_ge(s_tst, 16 * k)
                    act.copy((A, B)[g % 2][:, 0:GN], nodes(accumulator("type", p, g)[0])).then_inc(s_aggu, 1)


_VECS = ("L0_gnn_b_enc", "L0_gnn_bn_gamma", "L0_gnn_bn_beta", "L0_gnn_bn_mean", "L0_gnn_bn_var", "L0_gnn_b1", "L0_gnn_b2", "L1_gnn_b_msg")


def kernel(**inputs):
    import numpy as np
    import concourse.bacc as bacc
    from concourse.bass_utils import run_bass_kernel_spmd

    a = {k: np.asarray(v) for k, v in inputs.items()}
    vecs = [a[k] for k in _VECS] + list(a["L1_gnn_b_ih"].reshape(3, D)) + list(a["L1_gnn_b_hh"].reshape(3, D)) + [a["L2_gnn_b1"], a["L2_gnn_b2"]]
    ih, hh = a["L1_gnn_W_ih"].reshape(3, D, D), a["L1_gnn_W_hh"].reshape(3, D, D)
    wts = [a["L0_gnn_W_enc"], a["L0_gnn_W1"], a["L0_gnn_W2"], a["L1_gnn_W_msg"].T, *(w.T for w in ih), *(w.T for w in hh),
           a["L2_gnn_W1"], a["L2_gnn_W2"], *(w.T for w in a["L3_gnn_W_e"])]
    wn = a["L3_gnn_W_n"].reshape(3, D, 4, D)
    wts += [wn[t, :, k, :].T for k in range(4) for t in range(3)]
    arrays = {
        "in_x": a["x"], "in_src": a["src"], "in_dst": a["dst"], "in_edge_type": a["edge_type_3"], "in_node_type": a["node_type_3"],
        "in_vecs": np.stack(vecs, 1), "in_weights": np.stack(wts, 1), "in_b_e": a["L3_gnn_b_e"], "in_b_n": a["L3_gnn_b_n"],
    }
    arrays = {k: np.ascontiguousarray(v) for k, v in arrays.items()}
    nc = bacc.Bacc("TRN2", target_bir_lowering=False, num_devices=1)
    args = [nc.dram_tensor(k, v.shape, mybir.dt.from_np(v.dtype), kind="ExternalInput").ap() for k, v in arrays.items()]
    args.append(nc.dram_tensor("out_x", (N, D), F32, kind="ExternalOutput").ap())
    gnn_kernel(nc, *args)
    r = run_bass_kernel_spmd(nc, [arrays], core_ids=[0])
    return r.results[0]["out_x"]
```

```python
from contextlib import ExitStack

import concourse.bass as bass
from concourse import mybir

F32 = mybir.dt.float32
BF16 = mybir.dt.bfloat16
F16 = mybir.dt.float16
I32 = mybir.dt.int32
ALU = mybir.AluOpType
ACT = mybir.ActivationFunctionType
AX = mybir.AxisListType.X

P = 128
N = 3125
E = 50000
D = 128
TN = 125
NT = N // TN
GT = 5
NG = NT // GT
GN = GT * TN
H0, H1 = 3 * TN, 2 * TN
AG0 = 512 - H0
NCH = -(-E // P)
LEAD = 4
NCP = 400
WIN = 25
GP = 15632
SPLITS = 3
EPS = 1e-5
STEPS = 5
TYPES = 3

DEG_IN, CONV0, CONV1, DEG_OUT, GRU0 = 0, 1, 2, 3, 4
CONV2 = GRU0 + STEPS
CONV3 = CONV2 + 1
TYPE0 = CONV3 + 1
FEAT = {CONV0: 0, CONV1: 1, CONV2: 2 + STEPS, CONV3: 3 + STEPS}
FEAT_GRU0 = 2
FEAT_TYPE0 = 4 + STEPS
(V_BENC, V_GAMMA, V_BETA, V_MEAN, V_VAR, V_B01, V_B02, V_BMSG, V_BIR, V_BIZ, V_BIN, V_BHR, V_BHZ, V_BHN,
 V_B21, V_B22, V_BR, V_BZ, V_SCALE, V_SHIFT, V_STD, V_EPS) = range(22)
NV = 16
W_ENC, W_01, W_02, W_MSG, W_IR, W_IZ, W_IN, W_HR, W_HZ, W_HN, W_21, W_22, W_E, W_N = 0, 1, 2, 3, 4, 5, 6, 7, 8, 9, 10, 11, 12, 15


def gnn_kernel(nc, x, src, dst, etype, ntype, vecs, wts, be, bn, out):
    with ExitStack() as ctx:
        def sb(name, shape, dt):
            return ctx.enter_context(nc.sbuf_tensor(name, shape, dt))

        def sem(name):
            return ctx.enter_context(nc.semaphore(name))

        xs = nc.dram_tensor("x_between", (N, D), F32, kind="Internal").ap()
        aggd = nc.dram_tensor("typed_sums", (TYPES, P, N), F32, kind="Internal").ap()
        degd = nc.dram_tensor("degrees", (2, N), F32, kind="Internal").ap()
        normd = nc.dram_tensor("norms", (3, N), F32, kind="Internal").ap()
        hrows = nc.dram_tensor("feature_rows", (N, SPLITS * D), BF16, kind="Internal").ap()
        hrows16 = nc.dram_tensor("feature_rows16", (N, 2 * D), F16, kind="Internal").ap()
        keyd = nc.dram_tensor("edge_keys", (5, P, NCP), F32, kind="Internal").ap()
        idxd = nc.dram_tensor("edge_rows", (2, P, NCP), I32, kind="Internal").ap()

        adj = sb("counts", [P, NG * GP], BF16)
        H = sb("H", [P, NT * SPLITS * D], BF16)
        hT = sb("hT", [P, N], F32)
        A, B, C, DB, F, X = (sb(f"buf{c}", [P, 640], F32) for c in "ABCDFX")
        W = sb("W", [P, 7, D], F32)
        rec = sb("rec", [P, 3, NT, NT], BF16)
        identf = sb("identf", [P, P], F32)
        identb = sb("identb", [P, P], BF16)
        ones = sb("ones", [P, P], BF16)
        zeros = sb("zeros", [P, P], BF16)
        iota1 = sb("iota1", [P, P], BF16)
        iotat = sb("iotat", [P, NT], F32)
        vec = sb("vec", [P, 22], F32)
        stats = sb("stats", [P, GT, 6], F32)
        mv = sb("mv", [P, GT, 2], F32)
        rstd = sb("rstd", [P, GT], F32)
        occs = sb("occs", [P, 4], F32)
        flag = sb("flag", [P, 1], I32)

        def place(base, at, shape, dt):
            size = 1
            for s in shape:
                size *= s
            elems = size * (2 if dt in (F32, I32) else 1)
            ap = base[:, at // 2:at // 2 + elems]
            if dt != BF16:
                ap = ap.bitcast(dt)
            if len(shape) == 2:
                ap = ap.rearrange("p (a b) -> p a b", b=shape[1])
            if len(shape) == 3:
                ap = ap.rearrange("p (a b c) -> p a b c", b=shape[1], c=shape[2])
            return ap

        raw = place(adj, 0, (3, 4, P), I32)
        rawf = place(adj, 6144, (3, 4, P), F32)
        ef = place(adj, 12288, (3, NCP), F32)
        qi = place(adj, 17088, (2, NCP), I32)
        qf = place(adj, 20288, (2, NCP), F32)
        val = place(adj, 26688, (3, NCP), BF16)
        stile = place(adj, 29088, (NCP,), BF16)
        V = place(adj, 29888, (4 * NT, NCP), BF16)
        M = place(adj, 29888 + 3 * NT * NCP * 2, (NT, NCP), BF16)
        U = place(adj, 109888, (4, NCP), BF16)
        tri = place(adj, 113088, (P,), BF16)
        ct = place(adj, 113344, (4, NT), BF16)
        gsel = place(adj, 113600, (NT, NCP), F32)
        oslot = place(adj, 113600, (2, WIN, P), BF16)
        gsum = place(adj, 0, (NCP,), I32)
        gslot = place(adj, 1600, (NCP,), I32)
        slot1 = place(adj, 3200, (NCP,), F32)
        slotb = place(adj, 6400, (2, WIN * 4), BF16)
        qrem = place(adj, 23488, (2, NCP), F32)
        onesf = place(adj, 130000, (P,), F32)
        keyf = place(H, 0, (5, NCP), F32)
        idxi = place(H, 8000, (2, NCP), I32)
        idxf = place(H, 11200, (NCP,), F32)
        dcol = place(H, 2 * NT * 2 * D + 4096, (3, NT), F32)
        H16 = place(H, 0, (NT * 2 * D,), F16)
        beb = W[:, 3:3 + TYPES, :]
        WN = place(adj, 0, (4, TYPES * D), F32)
        bnb = place(adj, 6144, (TYPES * D,), F32)
        parts = [place(adj, 2 * GP + 8192 * r, (TYPES, GN), F32) for r in range(2)]
        tmp = place(adj, 16384, (2, TYPES * D), F32)
        ntf = place(adj, 20480, (NT,), F32)
        nti = place(adj, 20608, (NT,), I32)
        mask = place(adj, 20736, (TYPES, NT), F32)

        AG, D0, D1, D2 = (ctx.enter_context(nc.psum_tensor(n, [P, 1024], F32)) for n in ("AG", "D0", "D1", "D2"))

        def nodes(ps):
            return ps[:, AG0:AG0 + GN]

        def half(ap, h):
            return ap[:, 0:H0] if h == 0 else ap[:, H0:GN]

        def tiles(ap, rows=P):
            return ap[0:rows, 0:640].rearrange("p (t n) -> p t n", t=GT)

        def group(ap, g):
            return ap[:, g * GN:(g + 1) * GN]

        def ohring(q, g, r):
            if r == 0 and q == 2 and g < NG - 1:
                return place(H, 2 * NT * 2 * D, (2 * GT, P), BF16)
            types = (q, g) >= (3, NG - 1)
            return (X if types and r == 0 else B if r == 0 else F)[:].bitcast(BF16).rearrange("p (i n) -> p i n", n=P)

        def dup_of(q, g):
            if q == 2 and g < NG - 1:
                return place(H, 2 * NT * 2 * D + 4 * 640, (NT, 2 * GT * 4), BF16).rearrange("p j (i d) -> p j i d", d=4)
            if q == 0 or (q, g) >= (3, NG - 1):
                flat = DB[:, 0:NT * GT * 4]
            else:
                flat = W[:, 3:7, :].rearrange("p a b -> p (a b)")[:, 0:NT * GT * 4]
            return flat.bitcast(BF16).rearrange("p (j i d) -> p j i d", j=NT, d=4)

        s_pown = sem("s_pown")
        sl_seen = sem("sl_seen")
        s_slotb = sem("s_slotb")
        s_aggf = sem("s_aggf")
        s_pmsg = sem("s_pmsg")
        s_msg = sem("s_msg")
        s_prz = sem("s_prz")
        s_sig = sem("s_sig")
        s_pn = sem("s_pn")
        s_const = sem("s_const")
        s_par = sem("s_par")
        s_w = sem("s_w")
        s_vec = sem("s_vec")
        s_vstd = sem("s_vstd")
        s_rawm = sem("s_rawm")
        s_raw = sem("s_raw")
        s_rawf = sem("s_rawf")
        s_eT = sem("s_eT")
        s_ef = sem("s_ef")
        s_own = sem("s_own")
        s_M = sem("s_M")
        s_ctm = sem("s_ctm")
        s_ct = sem("s_ct")
        s_G = sem("s_G")
        s_gsel = sem("s_gsel")
        s_V = sem("s_V")
        s_osl = sem("s_osl")
        s_rmm = sem("s_rmm")
        s_rec = sem("s_rec")
        s_om = sem("s_om")
        s_omm = sem("s_omm")
        s_flag = sem("s_flag")
        s_kp = sem("s_kp")
        s_key = sem("s_key")
        s_dup = sem("s_dup")
        s_oh = sem("s_oh")
        s_blk = sem("s_blk")
        s_cnt = sem("s_cnt")
        s_xl = sem("s_xl")
        s_xst = sem("s_xst")
        s_xT = sem("s_xT")
        s_xsum = sem("s_xsum")
        s_bn = sem("s_bn")
        s_mv = sem("s_mv")
        s_std = sem("s_std")
        s_norm = sem("s_norm")
        s_hTm = sem("s_hTm")
        s_h = sem("s_h")
        s_enc = sem("s_enc")
        s_encr = sem("s_encr")
        s_bnh = sem("s_bnh")
        s_nb = sem("s_nb")
        s_nb2 = sem("s_nb2")
        s_pre = sem("s_pre")
        s_nm = sem("s_nm")
        s_ebias = sem("s_ebias")
        s_hi = sem("s_hi")
        s_r1 = sem("s_r1")
        s_mid = sem("s_mid")
        s_feat = sem("s_feat")
        s_agg = sem("s_agg")
        s_aggu = sem("s_aggu")
        s_act = sem("s_act")
        s_degst = sem("s_degst")
        s_degl = sem("s_degl")
        s_degf = sem("s_degf")
        s_degs = sem("s_degs")
        s_norms = sem("s_norms")
        s_nst = sem("s_nst")
        s_gown = sem("s_gown")
        s_gpre = sem("s_gpre")
        s_gtanh = sem("s_gtanh")
        s_hnew = sem("s_hnew")
        s_tst = sem("s_tst")
        s_lw = sem("s_lw")
        s_lx = [sem("s_lx0"), sem("s_lx1")]
        s_lo = sem("s_lo")
        s_lt = sem("s_lt")
        s_ly = sem("s_ly")
        s_out = [sem("s_out0"), sem("s_out1")]
        sl_rows = sem("sl_rows")
        sl_load = sem("sl_load")
        sl_iota = sem("sl_iota")
        sl_idx = sem("sl_idx")
        sl_g = [[sem(f"sl_g{g}{r}") for r in range(2)] for g in range(NG)]
        sl_oh = sem("sl_oh")
        sl_used = sem("sl_used")

        block = ctx.enter_context(nc.Block())

        SL = NCH + 1
        BLD = NG * NT

        def arena(g):
            b = g * GP * 2
            return dict(key=place(adj, b, (NCP,), F32), idx=place(adj, b + 1600, (NCP,), I32),
                        iota=place(adj, b + 3200, (GN,), F32), oh=place(adj, b + 5728, (2, 640), BF16),
                        rows=place(adj, b + 8320, (2, SPLITS * D), BF16), col=place(adj, b + 10240, (2, 8), I32))

        def along(kind, p, g):
            if kind == "deg_in":
                return (0, g + 1) if g + 1 < NG else None
            if not isinstance(p, int) or kind == "conv" and p in (CONV0,):
                return None
            if g == 0:
                q = {DEG_OUT: 1, CONV2: 2, TYPE0: 3, TYPE0 + 1: 4, TYPE0 + 2: 5}.get(p)
                return None if q is None else (q, NG - 1)
            q = {CONV1: 1, GRU0 + STEPS - 1: 2, CONV3: 3, TYPE0: 4, TYPE0 + 1: 5}.get(p)
            return None if q is None else (q, g - 1)

        def parity(q, g, j):
            return (q * BLD + g * NT + j) % 2

        def blocks(q, g, j_parity):
            return (D2, 2) if q == 2 and g < NG - 1 else ((D2, D1)[j_parity], 1)

        def steps(eng, what, step, first=0, last=NT):
            q, g = what
            n = (last - first) // 2
            with eng.Fori(0, n) as i:
                for r in range(2):
                    step(q, g, first + 2 * i + r, parity(q, g, first + r))
            for j in range(first + 2 * n, last):
                step(q, g, j, parity(q, g, j))

        def weave(eng, todo, at_tile):
            todo = sorted(todo, key=lambda e: e[0])
            first = max([2] + [int(at) + 1 for at, _ in todo])
            first = min(first + first % 2, NT - 1)

            def before(j):
                while todo and todo[0][0] <= j:
                    todo.pop(0)[1]()
            for j in range(first):
                before(j)
                if at_tile:
                    at_tile(j, j % 2)
            if at_tile and first < NT - 1:
                with eng.Fori(0, (NT - 1 - first) // 2) as i:
                    for r in range(2):
                        at_tile(first + 2 * i + r, r)
            before(NT)
            if at_tile:
                at_tile(NT - 1, 0)

        def between(todo, tile):
            todo = sorted(todo, key=lambda e: e[0])
            for j in range(NT):
                while todo and todo[0][0] <= j:
                    todo.pop(0)[1]()
                tile(j)

        def along_step(what, step):
            return (lambda j, r: step(*what, j, parity(*what, r))) if what else None

        def accumulator(kind, p, g):
            if kind == "gru" and not (isinstance(p, int) and p == GRU0 + STEPS - 1):
                return ((AG, D2)[g % 2], 2)
            if kind[:3] == "deg" or kind == "type" or kind == "conv" and p in (CONV0, CONV2):
                return ((AG, D0)[g % 2], 2)
            return (AG, 1)

        EARLY = 8

        def is_early(kind, p):
            return (not isinstance(p, int) or p > GRU0) if kind == "gru" else kind != "gru" and p in (CONV1, CONV3, TYPE0 + 1, TYPE0 + 2)

        BY_DEGREES = {0: (), 1: (0, 1), 2: (2,), 3: (3,), 4: (4,)}

        def first_groups(kind, p):
            if kind == "gru" and isinstance(p, int) and p == GRU0:
                return ()
            return range(1 if is_early(kind, p) else 0, NG)

        def makes_early(kind, p):
            if kind == "gru":
                return not isinstance(p, int) or p < GRU0 + STEPS - 1
            return kind[:3] != "deg" and p in (CONV0, CONV2, TYPE0, TYPE0 + 1)

        def cnt_of(kind, p, g):
            return 2 + BLD * (builds_before(kind, p) - 1) + (g + 1) * NT

        NM_AT = (-12, -4, 1, 6, 11)
        NM_AT_GRU = (-9, 0, 5, 10, 18)

        def conv_no(p):
            return (CONV0, CONV1, CONV2, CONV3).index(p)

        def mid_of(hp, g):
            return (0, 1, 7, 8, 9, 10, 11).index(hp) * NG + g

        def key_of(kind, t):
            return {"deg_in": 0, "deg_out": 1, "conv": 0, "gru": 1, "type": 2 + t}[kind]

        def builds_before(kind, p):
            return {"deg_in": 1, "deg_out": 2, "gru": 2}.get(kind) or (1 if kind == "conv" and p < DEG_OUT else 3 if kind == "conv" else 4 + p - TYPE0)

        NB = {"pre0": 0, CONV0: 3, CONV1: 8, "gru": 13, "pre2": 38, CONV2: 41, CONV3: 46}
        NB2 = {"pre0": 0, CONV0: 2, "pre2": 7, CONV2: 9}

        @block.sync
        def _(sp):
            full = 3 * P * P
            sp.wait_ge(s_rawm, 1)
            for k, a in enumerate((src, dst, etype)):
                sp.dma_start(raw[:, k, 0:3, :], a[0:full].rearrange("(b c p) -> c b p", b=3, p=P)).then_inc(s_raw, 16)
                rows = (E - full) // P
                sp.dma_start(raw[0:rows, k, 3, :], a[full:full + rows * P].rearrange("(c p) -> c p", p=P)).then_inc(s_raw, 16)
                sp.dma_start(raw[rows:rows + 1, k, 3, 0:E - full - rows * P],
                             a[full + rows * P:E].rearrange("(c p) -> c p", c=1)).then_inc(s_raw, 16)
            sp.dma_start(vec[:, 0:NV], vecs).then_inc(s_par, 16)
            sp.dma_start(W[:, 0:3, :], wts[:, 0:3, :]).then_inc(s_w, 16)

            def load_x(n):
                q, g = divmod(n, NG)
                if n:
                    sp.wait_ge(s_norm, n)
                if n > NG:
                    sp.wait_ge(s_xst, 16 * (n - NG))
                srcx = x if q < 2 else xs
                sp.dma_start(tiles(X, TN), srcx[g * GN:(g + 1) * GN, :].rearrange("(t p) d -> p t d", p=TN)).then_inc(s_xl, 16)

            def store_x(n):
                g = n % NG
                sp.wait_ge(s_xsum, n - NG + 1)
                sp.dma_start(xs[g * GN:(g + 1) * GN, :].rearrange("(t p) d -> p t d", p=TN), tiles(X, TN)).then_inc(s_xst, 16)

            for n in range(NG):
                load_x(n)

            sp.wait_ge(s_kp, 1)
            sp.dma_start(keyd.rearrange("k p c -> p k c"), keyf).then_inc(s_key, 16)
            sp.dma_start(idxd.rearrange("k p c -> p k c"), idxi).then_inc(s_key, 16)
            sp.wait_ge(s_key, 32)

            sp.wait_ge(s_flag, 1)
            fast = sp.value_load(flag[0:1, 0:1], min_val=0, max_val=1)

            def slow_loads(kind, p, hp, g, t=0):
                with sp.If(fast == 0):
                    a = arena(g)
                    sp.wait_ge(s_cnt, cnt_of(kind, p, g))
                    if kind[:3] != "deg" and g == 0:
                        sp.wait_ge(s_feat, hp * NG + NG)
                        if kind == "gru":
                            sp.dma_start(hrows16.rearrange("(t p) d -> p t d", p=TN),
                                         H16[0:TN].rearrange("p (t d) -> p t d", t=NT)).then_inc(sl_rows, 16)
                        else:
                            sp.dma_start(hrows.rearrange("(t p) d -> p t d", p=TN),
                                         H[0:TN].rearrange("p (t d) -> p t d", t=NT)).then_inc(sl_rows, 16)
                    if not (kind == "deg_in" and g == 0):
                        sp.wait_ge(s_agg, p * NG + g)
                    sp.dma_start(a["key"], keyd[key_of(kind, t)]).then_inc(sl_load, 16)
                    sp.dma_start(a["idx"], idxd[1 if kind == "gru" else 0]).then_inc(sl_load, 16)
                with sp.Else():
                    sp.nop()
                sp.nop()

            def in_degrees():
                for g in range(NG):
                    slow_loads("deg_in", DEG_IN, 0, g)
                    sp.wait_ge(s_aggu, g + 1)
                    sp.dma_start(degd[0:1, g * GN:(g + 1) * GN], A[0:1, 0:GN]).then_inc(s_degst, 16)
                    sp.wait_ge(s_degst, 16 * (g + 1))
                    cols = slice(g * GT, (g + 1) * GT)
                    at = slice(g * GN, (g + 1) * GN)
                    sp.dma_start(dcol[0:TN, 0, cols], degd[0, at].rearrange("(t p) -> p t", p=TN), allow_slow_non_contiguous=True).then_inc(s_degl, 16)
                    sp.wait_ge(s_norms, g + 1)
                    for k in range(2):
                        sp.dma_start(normd[k, at].rearrange("(t p) -> p t", p=TN), dcol[0:TN, 1 + k, cols], allow_slow_non_contiguous=True).then_inc(s_nst, 16)
                    sp.wait_ge(s_nst, 32 * (g + 1))
                    if g > 1:
                        load_norm(0, g, (s_pre, g - 1), (X, C)[g % 2], (s_nb, s_nb2)[g % 2])
                    else:
                        load_norm(0, g, ((s_norm, NG), (s_h, NG))[g], (X, C)[g], (s_nb, s_nb2)[g])

            def degrees(kind, p, d):
                for g in range(NG):
                    slow_loads(kind, p, 0, g)
                    if g == 0:
                        store_x(2 * NG - 1)
                    if g == 1:
                        sp.wait_ge(s_oh, 2 * BLD)
                        sp.dma_start(W[:, 0:7, :], wts[:, W_MSG:W_MSG + 7, :]).then_inc(s_w, 16)
                    sp.wait_ge(s_aggu, p * NG + g + 1)
                    sp.dma_start(degd[d:d + 1, g * GN:(g + 1) * GN], A[0:1, 0:GN]).then_inc(s_degst, 16)
                    sp.wait_ge(s_degst, 16 * (d * NG + g + 1))
                sp.dma_start(A[0:TN, 0:NT], degd[d, :].rearrange("(t p) -> p t", p=TN), allow_slow_non_contiguous=True).then_inc(s_degl, 16)
                sp.wait_ge(s_norms, NG + 1)
                sp.dma_start(normd[1 + d, :].rearrange("(t p) -> p t", p=TN), A[0:TN, 192:192 + NT], allow_slow_non_contiguous=True).then_inc(s_nst, 16)
                sp.wait_ge(s_nst, 32 * NG + 16)

            def load_norm(row, g, after, buf=DB, sem=None):
                a = degd[1:2] if row == "deg" else normd[row:row + 1]
                sp.wait_ge(*after)
                sp.dma_start(buf[:, 0:GN], a[:, g * GN:(g + 1) * GN].to_broadcast([P, GN])).then_inc(sem or (s_nb if buf is DB else s_nb2), 16)

            def conv_norms(p, hp, done=None, row2=None, free2=None, n=None):
                for g in range(NG):
                    slow_loads("conv", p, hp, g)
                    load_norm(0 if p < DEG_OUT else 1, g, (s_pre, done) if g == 0 and done else (s_aggu, p * NG + g))
                    if row2 is not None:
                        load_norm(row2, g, (s_pre, done + g) if g or free2 is None else free2, C)
                    if n is not None and g:
                        store_x(n + g - 1)
                        load_x(n + g)

            in_degrees()
            conv_norms(CONV0, 0, NG, 0)
            load_x(NG)
            conv_norms(CONV1, 1, n=NG)
            degrees("deg_out", DEG_OUT, 1)

            def gru_sp(s):
                for g in range(NG):
                    slow_loads("gru", GRU0 + s, FEAT_GRU0 + s, g)
                    load_norm("deg", g, (s_msg, s * NG + g) if not (isinstance(s, int) and s == 0 and g == 0) else (s_aggu, CONV1 * NG + NG))

            gru_sp(0)
            with sp.Fori(1, STEPS - 1) as s:
                gru_sp(s)
            for g in range(NG + 1):
                if g < NG:
                    slow_loads("gru", GRU0 + STEPS - 1, FEAT_GRU0 + STEPS - 1, g)
                    load_norm("deg", g, (s_msg, (STEPS - 1) * NG + g))
                if g:
                    sp.wait_ge(s_pmsg, (STEPS - 1) * NG + g)
                    load_x(2 * NG + g - 1)
                    if g == NG:
                        load_norm(2, 0, (s_msg, STEPS * NG), DB)
                        load_norm(2, 1, (s_hnew, STEPS * NG), B)
                        sp.dma_start(W[:, 0:2, :], wts[:, W_21:W_21 + 2, :]).then_inc(s_w, 16)
                        for k in range(2, NG):
                            load_norm(2, k, (s_pre, 2 * NG + k - 1), (DB, B)[k % 2])
                    store_x(2 * NG + g - 1)
            conv_norms(CONV2, 7, 3 * NG, 2, (s_hTm, 3 * NG))
            load_x(3 * NG)
            conv_norms(CONV3, 8, n=3 * NG)
            store_x(4 * NG - 1)
            sp.wait_ge(s_feat, FEAT_TYPE0 * NG)
            sp.dma_start(W[:, 0:3, :], wts[:, W_E:W_E + 3, :]).then_inc(s_w, 16)
            sp.wait_ge(s_oh, 3 * BLD + (NG - 1) * NT)
            sp.dma_start(beb, be.rearrange("(a t) d -> a t d", a=1).to_broadcast([P, TYPES, D])).then_inc(s_w, 16)
            def load_last(g):
                if g > 1:
                    sp.wait_ge(s_lo, GT * (g - 1))
                    sp.wait_ge(s_out[g % 2], 16 * (g // 2))
                sp.wait_ge(s_tst, 16 * ((TYPES - 1) * NG + g + 1))
                for t in range(TYPES):
                    sp.dma_start(parts[g % 2][:, t, :], group(aggd[t], g)).then_inc(s_lx[g % 2], 16)
                sp.dma_start(tiles((X, F)[g % 2], TN), xs[g * GN:(g + 1) * GN, :].rearrange("(t p) d -> p t d", p=TN)).then_inc(s_lx[g % 2], 16)

            for t in range(TYPES):
                for g in range(NG):
                    slow_loads("type", TYPE0 + t, FEAT_TYPE0 + t, g, t)
                    buf = (B, A)[g % 2]
                    sp.wait_ge(s_aggu, (TYPE0 + t) * NG + g + 1)
                    sp.dma_start(group(aggd[t], g), buf[:, 0:GN]).then_inc(s_tst, 16)
                    if t == TYPES - 1 and g == 1:
                        sp.wait_ge(s_agg, (TYPE0 + t) * NG + 2)
                        sp.dma_start(WN, wts[:, W_N:W_N + 12, :].rearrange("p (a b) d -> p a (b d)", a=4)).then_inc(s_lw, 16)
                        sp.dma_start(bnb, bn.rearrange("(a t) d -> a (t d)", a=1).to_broadcast([P, TYPES * D])).then_inc(s_lw, 16)
                        sp.wait_ge(s_blk, 2 + 6 * BLD)
                        sp.dma_start(nti[0:TN], ntype.rearrange("(t p) -> p t", p=TN), allow_slow_non_contiguous=True).then_inc(s_lw, 16)
                    if t == TYPES - 1 and 1 < g < 4:
                        load_last(g - 2)

            for g in range(NG):
                sp.wait_ge(s_ly, g + 1)
                sp.dma_start(out[g * GN:(g + 1) * GN, :].rearrange("(t p) d -> p t d", p=TN), tiles((X, F)[g % 2], TN)).then_inc(s_out[g % 2], 16)
                if g + 2 < NG:
                    load_last(g + 2)
            sp.wait_ge(s_out[0], 16 * 3)
            sp.wait_ge(s_out[1], 16 * 2)

        @block.gpsimd
        def _(pool):
            pool.memset(identf[:], 0.0).then_inc(s_pown, 1)
            pool.memset(tri, 1.0).then_inc(s_pown, 1)
            pool.memset(U, 1.0).then_inc(s_pown, 1)
            pool.memset(ones[:], 1.0).then_inc(s_pown, 1)
            pool.memset(zeros[:], 0.0).then_inc(s_pown, 1)
            pool.wait_ge(s_pown, 5)
            pool.affine_select(out=identf[:], in_=identf[:], compare_op=ALU.not_equal, fill=1.0, base=0,
                               pattern=[[-1, P]], channel_multiplier=1).then_inc(s_pown, 1)
            pool.affine_select(out=tri, in_=tri, compare_op=ALU.is_gt, fill=0.0, base=0,
                               pattern=[[1, P]], channel_multiplier=-1).then_inc(s_pown, 1)
            pool.affine_select(out=U, in_=U, compare_op=ALU.is_gt, fill=0.0, base=0,
                               pattern=[[-P, 4], [1, NCP]], channel_multiplier=-1).then_inc(s_pown, 1)
            pool.iota(iota1[:], [[1, P]], base=1, channel_multiplier=0, allow_small_or_imprecise_dtypes=True).then_inc(s_pown, 1)
            pool.iota(iotat[:], [[1, NT]], base=0, channel_multiplier=0, allow_small_or_imprecise_dtypes=True).then_inc(s_pown, 1)
            pool.memset(vec[:, V_EPS:V_EPS + 1], EPS).then_inc(s_pown, 1)
            pool.wait_ge(s_pown, 11)
            pool.tensor_copy(identb[:], identf[:]).then_inc(s_const, 1)

            pool.wait_ge(s_ef, 3)
            pool.tensor_copy(keyf[:, 0, :], ef[:, 1, :]).then_inc(s_pown, 1)
            pool.tensor_copy(keyf[:, 1, :], ef[:, 0, :]).then_inc(s_pown, 1)
            for t in range(TYPES):
                pool.tensor_scalar(keyf[:, 2 + t, :], ef[:, 2, :], float(t), None, ALU.is_equal).then_inc(s_pown, 1)
            pool.tensor_scalar(idxf, ef[:, 1, :], 1.0, None, ALU.add).then_inc(s_pown, 1)
            pool.wait_ge(s_pown, 17)
            for t in range(TYPES):
                pool.tensor_tensor(keyf[:, 2 + t, :], keyf[:, 2 + t, :], idxf, ALU.mult).then_inc(s_pown, 1)
            pool.wait_ge(s_pown, 20)
            for t in range(TYPES):
                pool.tensor_scalar(keyf[:, 2 + t, :], keyf[:, 2 + t, :], -1.0, None, ALU.add).then_inc(s_pown, 1)
            for k in range(2):
                pool.tensor_scalar(idxi[:, k, :], ef[:, k, :], 0.0, None, ALU.max).then_inc(s_pown, 1)
            pool.wait_ge(s_pown, 25)
            pool.nop().then_inc(s_kp, 1)

            pool.wait_ge(s_flag, 1)
            fast = pool.value_load(flag[0:1, 0:1], min_val=0, max_val=1)

            def slow_gathers(kind, p, hp, g):
                with pool.If(fast == 0):
                    a = arena(g)
                    n = p * NG + g
                    pool.wait_ge(sl_load, 32 * (n + 1))
                    pool.sem_inc(sl_seen, 1)
                    pool.iota(a["iota"], [[1, GN]], base=g * GN, channel_multiplier=0,
                              allow_small_or_imprecise_dtypes=True).then_inc(sl_iota, 1)
                    if kind[:3] != "deg":
                        m = hp * NG + g
                        pool.wait_ge(sl_rows, 16 * (hp + 1))
                        pool.sem_inc(sl_seen, 1)
                        with pool.Fori(0, SL // 2) as i:
                            for r in range(2):
                                pool.wait_ge(sl_used, n * SL + 2 * i + r + 1)
                                pool.tensor_copy(a["col"][:, r, 0:1], a["idx"][:, bass.ds(LEAD + 2 * i + r, 1)]).then_inc(sl_idx, 1)
                                pool.wait_ge(sl_idx, m * SL + 2 * i + r + 1)
                                pool.sem_inc(sl_seen, 1)
                                if kind == "gru":
                                    to, table = a["rows"][:, r, 0:2 * D].bitcast(F16), hrows16
                                else:
                                    to, table = a["rows"][:, r, :], hrows
                                pool.indirect_dma_start(out=to, out_offset=None, in_=table,
                                                        in_offset=bass.IndirectOffsetOnAxis(ap=a["col"][:, r, 0:1], axis=0)
                                                        ).then_inc(sl_g[g][r], 16)
                with pool.Else():
                    pool.nop()
                pool.nop()

            for g in range(NG):
                slow_gathers("deg_in", DEG_IN, 0, g)
            for p, hp in ((CONV0, 0), (CONV1, 1)):
                for g in range(NG):
                    slow_gathers("conv", p, hp, g)
            for g in range(NG):
                slow_gathers("deg_out", DEG_OUT, 0, g)
            with pool.Fori(0, STEPS) as s:
                for g in range(NG):
                    slow_gathers("gru", GRU0 + s, FEAT_GRU0 + s, g)
            for p, hp in ((CONV2, 7), (CONV3, 8)):
                for g in range(NG):
                    slow_gathers("conv", p, hp, g)
            for t in range(TYPES):
                for g in range(NG):
                    slow_gathers("type", TYPE0 + t, FEAT_TYPE0 + t, g)

        @block.tensor
        def _(pe):
            pe.sem_inc(s_blk, 2)
            pe.sem_inc(sl_used, 2)
            pe.wait_ge(s_const, 1)
            pe.wait_ge(s_rawf, 1)
            for k in range(3):
                for b in range(4):
                    mm = pe.transpose((D0, D0, D1)[k][:, 512 * (k % 2) + P * b:512 * (k % 2) + P * (b + 1)], rawf[:, k, b, :], identf[:])
                mm.then_inc(s_eT, 1)
            pe.wait_ge(s_M, NT)
            for b in range(4):
                cols = min(P, NCP - P * b)
                for sh in range(NT):
                    mm = pe.matmul(D1[0:cols, 512 + NT * b + sh:513 + NT * b + sh], M[:, sh, P * b:P * b + cols], ones[:, 0:1], start=True, stop=True)
            mm.then_inc(s_ctm, 1)
            pe.wait_ge(s_ct, 2)
            ring = [AG[:, 0:NCP], AG[:, 512:512 + NCP], D2[:, 0:NCP], D2[:, 512:512 + NCP]]

            def places_before(sh, r, wait):
                pe.wait_ge(s_gsel, wait)
                for b in range(4):
                    k = min(P, NCP - P * b)
                    pe.matmul(ring[r][:, P * b:NCP], ct[0:k, b, bass.ds(sh, 1)].to_broadcast([k, P]),
                              U[0:k, b, P * b:NCP], start=(b == 0), stop=False, skip_group_check=True)
                mm = pe.matmul(ring[r], tri, M[:, bass.ds(sh, 1), :], start=False, stop=True, skip_group_check=True)
                mm.then_inc(s_G, 1)

            def ln_back(n):
                pe.wait_ge(s_norm, n + 1)
                if n:
                    pe.wait_ge(s_h, n)
                for i in range(GT):
                    mm = pe.transpose(D0[:, P * i:P * i + TN], tiles(C, TN)[:, i, :], identf[0:TN, 0:TN])
                mm.then_inc(s_hTm, 1)

            def dense(ps, w, act, start=True, stop=True):
                for h in range(2):
                    mm = pe.matmul(half(nodes(ps), h), W[:, w, :], half(act, h), start=start, stop=stop)
                return mm

            def encode(n):
                pe.wait_ge(s_h, n + 1)
                if n:
                    pe.wait_ge(s_encr, n)
                dense(D1, 0, group(hT, n)).then_inc(s_enc, 1)

            pe.wait_ge(s_w, 16)
            between([e for n in range(NG) for e in ((4 * n + 5, lambda n=n: ln_back(n)), (4 * n + 6, lambda n=n: encode(n)))],
                    lambda j: places_before(j, j % 4, j + 1))
            pe.wait_ge(s_h, NG)
            pe.wait_ge(s_encr, NG)
            pe.wait_ge(s_V, 3)

            def records(b, r, w):
                pe.wait_ge(s_osl, b + 1)
                pe.wait_ge(s_rec, 2 * b + 2)
                for j in range(WIN):
                    mm = pe.matmul(D0[:, 512 * r:512 * r + 4 * NT], oslot[:, r, j, :], V[:, :, bass.ds(w + j, 1)],
                                   start=(j == 0), stop=(j == WIN - 1))
                mm.then_inc(s_rmm, 1)

            for b in range(NT):
                records(b, b % 2, b * 125 // 8)
            pe.wait_ge(s_om, 1)
            pe.matmul(D1[:, 0:2], onesf, occs[:, 0:2], start=True, stop=True).then_inc(s_omm, 1)

            def ln_in(n):
                g = n % NG
                if n // NG == 2:
                    pe.wait_ge(s_hnew, (STEPS - 1) * NG + g + 1)
                else:
                    pe.wait_ge(s_act, n + 1)
                if n > NG:
                    pe.wait_ge(s_h, n)
                for i in range(GT):
                    mm = pe.transpose(D0[0:TN, P * i:P * (i + 1)], group(hT, g)[:, TN * i:TN * (i + 1)], identf[:])
                mm.then_inc(s_xT, 1)

            pe.wait_ge(s_flag, 1)
            fast = pe.value_load(flag[0:1, 0:1], min_val=0, max_val=1)

            def step(q, g, j, r):
                t = g * NT + j
                pe.wait_ge(s_oh, q * BLD + t + 1)
                ps, free = blocks(q, g, r)
                pe.wait_ge(s_cnt, q * BLD + t + free)
                if isinstance(j, int) and j == 0:
                    pe.wait_ge(s_cnt, q * BLD + t + 2)
                oh = ohring(q, g, r)
                for i in range(GT):
                    mm = pe.matmul(ps[0:TN, P * i:P * i + TN], oh[:, i, 0:TN], oh[:, GT + i, 0:TN], start=True, stop=True)
                mm.then_inc(s_blk, 1)

            def agg(kind, p, hp, g, inserts=()):
                S = 2 if kind == "gru" else SPLITS
                n = p * NG + g
                what = along(kind, p, g)
                inserts = list(inserts)
                if kind[:3] != "deg" and g:
                    pe.wait_ge(s_feat, hp * NG + NG)
                Hs = H16 if kind == "gru" else H[:]

                def feature(j, k):
                    if kind[:3] == "deg":
                        return ones[0:TN, :]
                    if isinstance(j, int):
                        return Hs[0:TN, (j * S + k) * D:(j * S + k + 1) * D]
                    return Hs[0:TN, bass.ds((j * S + k) * D, D)]

                acc, ring = accumulator(kind, p, g)

                def free():
                    if not (kind == "deg_in" and g < 2):
                        pe.wait_ge(s_aggu, n if g == 0 or ring == 1 else n - 1)
                    if kind == "deg_out" and g == 1:
                        pe.wait_ge(s_h, 2 * NG)

                pe.wait_ge(s_cnt, cnt_of(kind, p, g))
                ks = 1 if kind[:3] == "deg" else S

                def tile(j):
                    if isinstance(j, int) and j == 0:
                        free()
                    for k in range(ks):
                        for h in range(2):
                            at, size = (0, H0) if h == 0 else (H0, H1)
                            mm = pe.matmul(half(nodes(acc), h), feature(j, k), adj[0:TN, bass.ds(g * GP + j * GN + at, size)],
                                           start=(isinstance(j, int) and j == 0 and k == 0), stop=(isinstance(j, int) and j == NT - 1 and k == ks - 1),
                                           skip_group_check=True)
                    if isinstance(j, int) and j == NT - 1:
                        mm.then_inc(s_aggf, 1)

                build = along_step(what, step)

                def tile_and_step(j, r):
                    tile(j)
                    if build:
                        build(j, r)

                with pe.If(fast == 1):
                    weave(pe, inserts, tile_and_step)
                with pe.Else():
                    weave(pe, inserts, build)
                    if kind[:3] != "deg":
                        pe.wait_ge(s_feat, hp * NG + NG)
                    free()
                    a = arena(g)
                    for h in range(2):
                        pe.matmul(half(nodes(acc), h), zeros[:], iota1[:, 0:1].to_broadcast([P, (H0, H1)[h]]), start=True, stop=False, skip_group_check=True)
                    with pe.Fori(0, SL // 2) as i:
                        for r in range(2):
                            pe.wait_ge(sl_oh, n * SL + 2 * i + r + 1)
                            if kind[:3] != "deg":
                                pe.wait_ge(sl_g[g][r], 16 * (hp * (SL // 2) + i + 1))
                            for k in range(1 if kind[:3] == "deg" else S):
                                rows = a["rows"][:, r, k * D:(k + 1) * D]
                                if kind == "gru":
                                    rows = rows.bitcast(F16)
                                for h in range(2):
                                    mm = pe.matmul(half(nodes(acc), h), ones[:] if kind[:3] == "deg" else rows, half(a["oh"][:, r, :], h),
                                                   start=False, stop=False, skip_group_check=True)
                            mm.then_inc(sl_used, 1)
                    for h in range(2):
                        mm = pe.matmul(half(nodes(acc), h), zeros[:], iota1[:, 0:1].to_broadcast([P, (H0, H1)[h]]), start=False, stop=True, skip_group_check=True)
                    mm.then_inc(s_aggf, 1)
                if kind == "conv" and isinstance(p, int) and p < DEG_OUT:
                    for i in range(GT):
                        for k in range(SPLITS):
                            mm = pe.matmul(nodes(acc)[:, TN * i:TN * (i + 1)], feature(g * GT + i, k), identb[0:TN, 0:TN],
                                           start=False, stop=(k == SPLITS - 1), skip_group_check=True)
                    mm.then_inc(s_agg, 1)
                else:
                    pe.wait_ge(s_aggf, n + 1)
                    pe.nop().then_inc(s_agg, 1)

            def nm(kind, hp, g, w=0, first=0, after=0):
                ps = D2 if kind == "gru" else D0
                m = hp * NG + g
                if kind == "conv":
                    pe.wait_ge(s_pre, first + g + 1)
                elif kind == "type":
                    pe.wait_ge(s_h, 4 * NG)
                if g == 0:
                    pe.wait_ge(s_aggu, after)
                elif kind == "gru":
                    pe.wait_ge(s_feat, m)
                elif kind == "type":
                    pe.wait_ge(s_ebias, m - FEAT_TYPE0 * NG)
                else:
                    pe.wait_ge(s_r1, mid_of(hp, g - 1) + 1)
                if kind == "gru" and g == NG - 1 and (not isinstance(after, int) or after > GRU0 * NG):
                    pe.wait_ge(s_hnew, after - GRU0 * NG)
                for i in range(GT):
                    at = TN * i
                    if kind == "gru":
                        mm = pe.transpose(ps[0:TN, P * i:P * (i + 1)], group(hT, g)[:, at:at + TN], identf[:])
                    else:
                        mm = pe.matmul(ps[0:TN, P * i:P * (i + 1)], group(hT, g)[:, at:at + TN], W[:, w, :], start=True, stop=True)
                mm.then_inc(s_nm, 1)

            def sums(kind, p, hp, w=0, first=0, n=None):
                for g in range(NG):
                    ins = []
                    if g == 0 and kind[:3] != "deg":
                        at = NM_AT_GRU if kind == "gru" else NM_AT
                        ins = [(at[k], lambda k=k: nm(kind, hp, k, w, first, p * NG)) for k in first_groups(kind, p)]
                        ins += [(GT * k, lambda k=k: pe.wait_ge(s_feat, hp * NG + k + 1)) for k in range(NG)]
                    if n is not None and (g or kind == "deg_out"):
                        m = n + g - 1
                        ins = [(1, lambda: ln_in(m)), (11, lambda: ln_back(m))]
                    if kind == "gru" and (g or not isinstance(p, int) or p > GRU0):
                        ins += gates(p * NG + g - 1 - GRU0 * NG, (g - 1) % NG)
                    if kind == "gru" and isinstance(p, int) and p == GRU0 + STEPS - 1 and g:
                        m = 2 * NG + g - 1
                        ins += [(17, lambda: ln_in(m)), (24, lambda: ln_back(m))]
                    if g == NG - 1 and makes_early(kind, p):
                        ins.append((EARLY, lambda: nm(kind, hp + 1, 0, w + 1, first + NG, p * NG + NG - 1)))
                    agg(kind, p, hp, g, ins)

            steps(pe, (0, 0), step)
            sums("deg_in", DEG_IN, 0)
            sums("conv", CONV0, 0, 1, 0)
            sums("conv", CONV1, 1, 2, NG, NG)
            agg("deg_out", DEG_OUT, 0, 0, [(1, lambda: ln_in(2 * NG - 1)), (11, lambda: ln_back(2 * NG - 1))])
            pe.wait_ge(s_cnt, 2 + 2 * BLD)
            for g in range(1, NG):
                agg("deg_out", DEG_OUT, 0, g, [(8 * i, lambda k=k: nm("gru", FEAT_GRU0, k, after=DEG_OUT * NG)) for i, k in enumerate(BY_DEGREES[g])])
            pe.wait_ge(s_w, 32)
            pe.wait_ge(s_h, 2 * NG)

            def gates(n, g):
                h = group(hT, g)

                def message():
                    pe.wait_ge(s_aggu, GRU0 * NG + n + 1)
                    if not (isinstance(n, int) and n == 0):
                        pe.wait_ge(s_hnew, n)
                    dense(D0, 0, X).then_inc(s_pmsg, 1)

                def r_and_z():
                    pe.wait_ge(s_msg, n + 1)
                    dense(D1, 1, B, True, False)
                    dense(D1, 4, h, False, True)
                    dense(D0, 2, B, True, False)
                    dense(D0, 5, h, False, True).then_inc(s_prz, 1)

                def new():
                    pe.wait_ge(s_sig, 2 * n + 1)
                    dense(D1, 6, h)
                    pe.wait_ge(s_sig, 2 * n + 2)
                    dense(D0, 3, B).then_inc(s_pn, 1)
                return [(1, message), (5, r_and_z), (8, new)]

            def gru_pe(s):
                sums("gru", GRU0 + s, FEAT_GRU0 + s)

            gru_pe(0)
            with pe.Fori(1, STEPS - 1) as s:
                gru_pe(s)
            gru_pe(STEPS - 1)
            for _, f in gates(STEPS * NG - 1, NG - 1):
                f()
            ln_in(3 * NG - 1)
            ln_back(3 * NG - 1)
            pe.wait_ge(s_w, 48)
            pe.wait_ge(s_h, 3 * NG)
            sums("conv", CONV2, 7, 0, 2 * NG)
            sums("conv", CONV3, 8, 1, 3 * NG, 3 * NG)
            ln_in(4 * NG - 1)
            ln_back(4 * NG - 1)
            pe.wait_ge(s_w, 80)
            for t in range(TYPES):
                sums("type", TYPE0 + t, FEAT_TYPE0 + t, t)
            pe.wait_ge(s_lw, 48)
            pe.wait_ge(s_aggu, (TYPE0 + TYPES) * NG)
            banks = [D1[0:TN, 0:384], D1[0:TN, 512:896], D2[0:TN, 0:384], D2[0:TN, 512:896]]
            for g in range(NG):
                pe.wait_ge(s_lx[g % 2], 64 * (g // 2 + 1))
                if g > 1:
                    pe.wait_ge(s_ly, g - 1)
                for i in range(GT):
                    n = g * GT + i
                    at = TN * i
                    h = group(hT, g)[:, at:at + TN]
                    pe.transpose((D0, AG)[g % 2][0:TN, P * i:P * (i + 1)], h, identf[:])
                    if n >= 4:
                        pe.wait_ge(s_lt, n - 3)
                    pe.matmul(banks[n % 4], h, WN[:, 0, :], start=True, stop=False)
                    for t in range(TYPES):
                        mm = pe.matmul(banks[n % 4], parts[g % 2][:, t, at:at + TN], WN[:, 1 + t, :], start=False, stop=(t == TYPES - 1))
                    mm.then_inc(s_lo, 1)

        @block.vector
        def _(dve):
            own = [0]

            def mine(ins):
                own[0] += 1
                ins.then_inc(s_own, 1)
                dve.wait_ge(s_own, own[0])

            dve.sem_inc(s_gsel, 4)
            dve.memset(raw[:, :, 3, :], -1).then_inc(s_rawm, 1)
            dve.memset(ef[:, :, 0:LEAD], -1.0)
            dve.wait_ge(s_raw, 16 * 9)
            dve.wait_ge(s_rawm, 1)
            dve.tensor_copy(rawf.rearrange("p a b c -> p (a b c)"), raw.rearrange("p a b c -> p (a b c)")).then_inc(s_rawf, 1)
            for k in range(3):
                dve.wait_ge(s_eT, k + 1)
                dve.tensor_copy(ef[:, k, LEAD:NCP], (D0, D0, D1)[k][:, 512 * (k % 2):512 * (k % 2) + NCP - LEAD]).then_inc(s_ef, 1)
            dve.wait_ge(s_ef, 3)
            mine(dve.tensor_scalar(qi, ef[:, 0:2, :], 1.0 / TN, 0.5 / TN - 0.5, ALU.mult, ALU.add))
            mine(dve.tensor_copy(qf, qi))
            dve.tensor_copy(stile, qf[:, 0, :])
            mine(dve.scalar_tensor_tensor(out=qrem, in0=qf, scalar=-float(TN), in1=ef[:, 0:2, :], op0=ALU.mult, op1=ALU.add))
            for sh in range(NT):
                dve.tensor_scalar(M[:, sh, :], stile, float(sh), None, ALU.is_equal).then_inc(s_M, 1)
            dve.tensor_scalar(val[:, 0:2, :], qrem, 1.0, None, ALU.add)
            mine(dve.tensor_scalar(val[:, 2, :], ef[:, 2, :], 1.0, None, ALU.add))

            def values(k):
                dve.tensor_tensor(V[:, NT * k:NT * (k + 1), :], M, val[:, k:k + 1, :].to_broadcast([P, NT, NCP]), ALU.mult).then_inc(s_V, 1)

            def select(sh, r, v):
                dve.wait_ge(s_G, v)
                dve.scalar_tensor_tensor(out=gsel[:, bass.ds(sh, 1), :].rearrange("p a c -> p (a c)"), in0=stile, scalar=iotat[:, bass.ds(sh, 1)],
                                         in1=(AG, AG, D2, D2)[r][:, 512 * (r % 2):512 * (r % 2) + NCP],
                                         op0=ALU.is_equal, op1=ALU.mult).then_inc(s_gsel, 1)

            dve.wait_ge(s_const, 1)
            dve.wait_ge(s_par, 16)
            dve.wait_ge(s_vstd, 1)
            v = lambda k: vec[:, k:k + 1]
            mine(dve.reciprocal(v(V_STD), v(V_STD)))
            mine(dve.tensor_tensor(v(V_SCALE), v(V_GAMMA), v(V_STD), ALU.mult))
            mine(dve.tensor_tensor(v(V_SHIFT), v(V_MEAN), v(V_SCALE), ALU.mult))
            mine(dve.tensor_tensor(v(V_SHIFT), v(V_BETA), v(V_SHIFT), ALU.subtract))
            dve.tensor_tensor(v(V_BR), v(V_BIR), v(V_BHR), ALU.add)
            dve.tensor_tensor(v(V_BZ), v(V_BIZ), v(V_BHZ), ALU.add).then_inc(s_vec, 1)

            def ln_parts(n, at=1):
                xt = tiles(X, TN)

                def sums():
                    dve.wait_ge(s_xl, 16 * (n + 1))
                    if n >= NG:
                        dve.wait_ge(s_xT, n - NG + 1)
                        dve.tensor_tensor(xt, xt, tiles(D0, TN), ALU.add).then_inc(s_xsum, 1)
                        dve.wait_ge(s_xsum, n - NG + 1)
                    for i in range(GT):
                        st = dve.bn_stats(stats[0:TN, i, :], xt[:, i, :])
                    st.then_inc(s_bn, 1)

                def moments():
                    dve.wait_ge(s_bn, n + 1)
                    for i in range(GT):
                        st = dve.bn_aggr(mv[0:TN, i, :], stats[0:TN, i, :])
                    st.then_inc(s_mv, 1)

                def scale():
                    dve.wait_ge(s_std, n + 1)
                    mine(dve.reciprocal(rstd[0:TN, :], rstd[0:TN, :]))
                    if n:
                        dve.wait_ge(s_hTm, n)
                    for i in range(GT):
                        st = dve.tensor_scalar(tiles(C, TN)[:, i, :], xt[:, i, :], mv[0:TN, i, 0:1], rstd[0:TN, i:i + 1], ALU.subtract, ALU.mult)
                    st.then_inc(s_norm, 1)
                return [(at + 3, sums), (at + 4, moments), (at + (8 if at == 1 else 6), scale)]

            def ln(n):
                for _, f in ln_parts(n):
                    f()

            def batch_norm(n):
                dve.wait_ge(s_encr, n + 1)
                dve.tensor_scalar(group(hT, n), (A, B)[n % 2][:, 0:GN], v(V_SCALE), v(V_SHIFT), ALU.mult, ALU.add).then_inc(s_bnh, 1)

            dve.wait_ge(s_vec, 1)
            between([e for n in range(NG) for e in ln_parts(n, 4 * n - 2) + [(4 * n + 8, lambda n=n: batch_norm(n))]]
                    + [(7 * k + 4.5, lambda k=k: values(k)) for k in range(3)],
                    lambda j: select(j, j % 4, j + 1))
            dve.wait_ge(s_gsel, NT + 4)
            mine(dve.tensor_reduce(slot1, gsel.rearrange("p a c -> p c a"), AX, ALU.add))
            mine(dve.tensor_copy(gsum, slot1))
            mine(dve.tensor_scalar(gslot, gsum, P - 1, None, ALU.bitwise_and))
            mine(dve.tensor_scalar(slot1, gslot, 1.0, None, ALU.add))

            def slots(b, r, w):
                dve.wait_ge(s_rmm, b + 1)
                dve.scalar_tensor_tensor(out=slotb[:, r, :].rearrange("p (c d) -> p c d", d=4),
                                         in0=qf[:, 1, bass.ds(w, WIN)].unsqueeze(2).to_broadcast([P, WIN, 4]), scalar=iotat[:, bass.ds(b, 1)],
                                         in1=slot1[:, bass.ds(w, WIN)].unsqueeze(2).to_broadcast([P, WIN, 4]),
                                         op0=ALU.is_equal, op1=ALU.mult).then_inc(s_slotb, 1)
                dve.wait_ge(s_slotb, b + 1)
                dve.tensor_tensor(oslot[:, r, :, :].rearrange("p c (v d) -> p c v d", d=4),
                                  iota1[:].rearrange("p (v d) -> p v d", d=4).unsqueeze(1).to_broadcast([P, WIN, P // 4, 4]),
                                  slotb[:, r, :].rearrange("p (c d) -> p c d", d=4).unsqueeze(2).to_broadcast([P, WIN, P // 4, 4]),
                                  ALU.is_equal).then_inc(s_osl, 1)

            dve.sem_inc(s_rmm, 2)
            for b in range(NT):
                slots(b, b % 2, b * 125 // 8)
            dve.wait_ge(s_rec, 4 + 2 * NT)
            occ = B[:, 0:NT * NT]
            mine(dve.tensor_reduce(occs[:, 2:3], occ, AX, ALU.max))
            mine(dve.tensor_reduce(occs[:, 1:2], occ, AX, ALU.add))
            mine(dve.memset(onesf, 1.0))
            dve.tensor_scalar(occs[:, 0:1], occs[:, 2:3], 1.5, None, ALU.is_gt).then_inc(s_om, 1)
            dve.wait_ge(s_omm, 1)
            mine(dve.tensor_copy(occs[:, 2:4], D1[:, 0:2]))
            mine(dve.tensor_scalar(occs[:, 0:1], occs[:, 2:3], 0.5, None, ALU.is_lt))
            mine(dve.tensor_scalar(occs[:, 1:2], occs[:, 3:4], float(E), None, ALU.is_equal))
            dve.tensor_tensor(flag[:], occs[:, 0:1], occs[:, 1:2], ALU.mult).then_inc(s_flag, 1)

            dve.wait_ge(s_flag, 1)
            fast = dve.value_load(flag[0:1, 0:1], min_val=0, max_val=1)

            def prepare(q, g):
                dup = dup_of(q, g)
                n = q * BLD + g * NT
                if n:
                    dve.wait_ge(s_oh, n)
                if q > 2:
                    dve.wait_ge(s_blk, n + 1)
                    rect = ohring(q, g, parity(q, g, 0))[:, 0, 0:NT * GT].rearrange("p (i j) -> p i j", j=NT)
                    mine(dve.scalar_tensor_tensor(out=rect, in0=rec[:, 2, GT * g:GT * (g + 1), :], scalar=float(q - 2),
                                                  in1=rec[:, 1, GT * g:GT * (g + 1), :], op0=ALU.is_equal, op1=ALU.mult))
                for kind in range(2):
                    if q == 1:
                        r = rec[:, 1 - kind, :, GT * g:GT * (g + 1)]
                    elif q > 2 and kind == 1:
                        r = rect.rearrange("p i j -> p j i")
                    else:
                        r = rec[:, kind, GT * g:GT * (g + 1), :].rearrange("p i j -> p j i")
                    ins = dve.tensor_copy(dup[:, :, GT * kind:GT * (kind + 1), :], r.unsqueeze(3).to_broadcast([P, NT, GT, 4]))
                ins.then_inc(s_dup, 1)
                dve.wait_ge(s_dup, q * NG + g + 1)

            def step(q, g, j, r):
                dve.wait_ge(s_blk, q * BLD + g * NT + j + 1)
                dve.tensor_tensor(ohring(q, g, r).rearrange("p i (v d) -> p i v d", d=4),
                                  iota1[:].rearrange("p (v d) -> p v d", d=4).unsqueeze(1).to_broadcast([P, 2 * GT, P // 4, 4]),
                                  dup_of(q, g)[:, bass.ds(j, 1), :, :].rearrange("p a i d -> p (a i) d").unsqueeze(2).to_broadcast([P, 2 * GT, P // 4, 4]),
                                  ALU.is_equal).then_inc(s_oh, 1)

            def shifted(todo, by):
                return [(at + by, f) for at, f in todo]

            def build_along(kind, p, g, inserts=()):
                if g == NG - 1 and makes_early(kind, p):
                    if kind == "gru":
                        more = splits2(p + 1 - GRU0 + FEAT_GRU0, [0])
                        by = EARLY - NM_AT_GRU[0]
                    else:
                        more = splits_type(p + 1 - TYPE0, [0]) if kind == "type" else splits3(1 if p == CONV0 else 8, [0])
                        by = EARLY - NM_AT[0]
                    inserts = list(inserts) + shifted(more, by)
                what = along(kind, p, g)
                if what in ((0, 1), (2, NG - 1), (3, NG - 1)):
                    prepare(*what)
                weave(dve, inserts, along_step(what, step))
                if kind == "type" and g == NG - 1 and p < TYPE0 + TYPES - 1:
                    following = (3 + p + 1 - TYPE0, NG - 1)
                elif kind == "conv" and g == NG - 1 and p == CONV1:
                    following = (1, NG - 1)
                else:
                    following = along(kind, p, g + 1) if g + 1 < NG else None
                if following:
                    prepare(*following)

            def slow_hots(kind, p, g):
                with dve.If(fast == 0):
                    a = arena(g)
                    n = p * NG + g
                    dve.wait_ge(sl_load, 32 * (n + 1))
                    dve.wait_ge(sl_iota, n + 1)
                    dve.sem_inc(sl_seen, 1)
                    with dve.Fori(0, SL // 2) as i:
                        for r in range(2):
                            dve.wait_ge(sl_used, n * SL + 2 * i + r + 1)
                            dve.tensor_scalar(a["oh"][:, r, 0:GN], a["iota"], a["key"][:, bass.ds(LEAD + 2 * i + r, 1)], None, ALU.is_equal).then_inc(sl_oh, 1)
                with dve.Else():
                    dve.nop()
                dve.nop()

            def norm_parts(g):
                cols = slice(g * GT, (g + 1) * GT)

                def clip():
                    dve.wait_ge(s_degl, 16 * (g + 1))
                    dve.tensor_scalar(dcol[0:TN, 1, cols], dcol[0:TN, 0, cols], 1.0, None, ALU.add)
                    dve.tensor_scalar(dcol[0:TN, 2, cols], dcol[0:TN, 0, cols], 1.0, None, ALU.max).then_inc(s_degf, 1)

                def invert():
                    dve.wait_ge(s_degs, g + 1)
                    dve.reciprocal(dcol[0:TN, 1:3, cols], dcol[0:TN, 1:3, cols]).then_inc(s_norms, 1)
                return [(7, clip), (9, invert), (19, lambda: pre(0, g))]

            def in_degrees():
                for g in range(NG):
                    build_along("deg_in", DEG_IN, g, norm_parts(g - 1) if g else ())
                    slow_hots("deg_in", DEG_IN, g)
                    dve.wait_ge(s_agg, g + 1)
                    if g:
                        dve.wait_ge(s_degst, 16 * g)
                    dve.tensor_copy(A[:, 0:GN], nodes(accumulator("deg_in", DEG_IN, g)[0])).then_inc(s_aggu, 1)

            def degrees(kind, p, d):
                for g in range(NG):
                    build_along(kind, p, g, ln_parts(2 * NG - 1) if g == 0 else splits2(FEAT_GRU0, BY_DEGREES[g]))
                    slow_hots(kind, p, g)
                    dve.wait_ge(s_agg, p * NG + g + 1)
                    if g:
                        dve.wait_ge(s_degst, 16 * (d * NG + g))
                    else:
                        dve.wait_ge(s_act, 2 * NG)
                    dve.tensor_copy(A[:, 0:GN], nodes(accumulator(kind, p, g)[0])).then_inc(s_aggu, 1)
                dve.wait_ge(s_degl, 16 * (NG + 1))
                deg = A[0:TN, 0:NT]
                dve.tensor_scalar(A[0:TN, 192:192 + NT], deg, 1.0, None, ALU.max).then_inc(s_degf, 1)
                dve.wait_ge(s_degs, NG + 1)
                dve.reciprocal(A[0:TN, 192:192 + NT], A[0:TN, 192:192 + NT]).then_inc(s_norms, 1)

            def pre(j, g):
                p = {1: CONV0, 3: CONV2}.get(j)
                if p is None:
                    first, second = NB[f"pre{j}"], NB2[f"pre{j}"]
                    buf = ((X, C) if j == 0 else (DB, B))[g % 2]
                    if g % 2 == 0:
                        dve.wait_ge(s_nb, 16 * (first + g // 2 + 1))
                    else:
                        dve.wait_ge(s_nb2, 16 * (second + g // 2 + 1))
                    if j == 2:
                        dve.wait_ge(s_h, 2 * NG + g + 1)
                else:
                    buf = C
                    dve.wait_ge(s_nb2, 16 * (NB2[p] + g + 1))
                    dve.wait_ge(s_act, conv_no(p) * NG + g + 1)
                dve.tensor_tensor(group(hT, g), group(hT, g), buf[:, 0:GN], ALU.mult).then_inc(s_pre, 1)

            def split3(hp, g, src, at, t=None):
                m = hp * NG + g
                Ht = H[0:TN, :].rearrange("p (t k d) -> p t k d", k=SPLITS, d=D)[:, GT * g:GT * (g + 1)]

                def rest1():
                    dve.wait_ge(s_hi, m + 1)
                    if m:
                        dve.wait_ge(s_feat, m)
                    if t is None and g == 0 and hp in (1, 8):
                        dve.wait_ge(s_act, conv_no(CONV1 if hp == 1 else CONV3) * NG - 1)
                    if t is None:
                        dve.tensor_tensor(tiles(A, TN), src, Ht[:, :, 0, :], ALU.subtract).then_inc(s_r1, 1)
                        return
                    if t and g == 0:
                        dve.wait_ge(s_tst, 16 * (t * NG - 1))
                    for i in range(GT):
                        ins = dve.scalar_tensor_tensor(out=tiles(A, TN)[:, i, :], in0=src[:, i, :], scalar=0.0, in1=Ht[:, i, 0, :], op0=ALU.max, op1=ALU.subtract)
                    ins.then_inc(s_r1, 1)

                def rest2():
                    dve.wait_ge(s_mid, mid_of(hp, g) + 1)
                    dve.tensor_tensor(Ht[:, :, 2, :], tiles(A, TN), Ht[:, :, 1, :], ALU.subtract).then_inc(s_feat, 1)
                return [(at + 4, rest1), (at + 7, rest2)]

            def splits3(hp, groups=range(NG)):
                return [e for g in groups for e in split3(hp, g, tiles(D0, TN), NM_AT[g])]

            def splits2(hp, groups=range(NG)):
                def split2(g):
                    m = hp * NG + g
                    Ht = H16[0:TN].rearrange("p (t k d) -> p t k d", k=2, d=D)[:, GT * g:GT * (g + 1)]
                    dve.wait_ge(s_hi, m + 1)
                    dve.tensor_tensor(Ht[:, :, 1, :], tiles(D2, TN), Ht[:, :, 0, :], ALU.subtract).then_inc(s_feat, 1)
                return [(NM_AT_GRU[g] + 2, lambda g=g: split2(g)) for g in groups]

            def splits_type(t, groups=range(NG)):
                def bias(g):
                    dve.wait_ge(s_nm, (FEAT_TYPE0 + t) * NG + g + 1)
                    if t * NG + g:
                        dve.wait_ge(s_r1, mid_of(FEAT_TYPE0 + t, g))
                        dve.wait_ge(s_hi, (FEAT_TYPE0 + t) * NG + g)
                    dve.tensor_tensor(tiles(C, TN), tiles(D0, TN), beb[0:TN, t:t + 1, :].to_broadcast([TN, GT, D]), ALU.add).then_inc(s_ebias, 1)

                out = []
                for g in groups:
                    out.append((NM_AT[g] + 3, lambda g=g: bias(g)))
                    out += split3(FEAT_TYPE0 + t, g, tiles(C, TN), NM_AT[g] + 2, t)
                return out

            def conv(p, g, inserts=(), n=None):
                if n is not None and g:
                    inserts = ln_parts(n + g - 1)
                build_along("conv", p, g, inserts)
                if p in (CONV0, CONV2) and g:
                    pre(1 if p == CONV0 else 3, g - 1)
                slow_hots("conv", p, g)
                dve.wait_ge(s_agg, p * NG + g + 1)
                dve.wait_ge(s_nb, 16 * (NB[p] + g + 1))
                if g == NG - 1 and makes_early("conv", p):
                    dve.wait_ge(s_feat, (1 if p == CONV0 else 8) * NG + 1)
                if conv_no(p) * NG + g:
                    dve.wait_ge(s_act, conv_no(p) * NG + g)
                dve.tensor_tensor(A[:, 0:GN], nodes(accumulator("conv", p, g)[0]), DB[:, 0:GN], ALU.mult).then_inc(s_aggu, 1)

            dve.wait_ge(s_bnh, NG)
            prepare(0, 0)
            steps(dve, (0, 0), step)
            in_degrees()
            dve.wait_ge(s_degst, 16 * NG)
            for g in range(NG):
                conv(CONV0, g, splits3(0) + [(3.5 + i, f) for i, (_, f) in enumerate(norm_parts(NG - 1))] if g == 0 else ())
            pre(1, NG - 1)
            for g in range(NG):
                conv(CONV1, g, splits3(1, range(1, NG)) if g == 0 else (), NG)
            degrees("deg_out", DEG_OUT, 1)

            def gru(n, g):
                h = group(hT, g)
                b = B[:, 0:GN]
                a = A[:, 0:GN]

                def message():
                    dve.wait_ge(s_pmsg, n + 1)
                    dve.wait_ge(s_nb, 16 * (NB["gru"] + n + 1))
                    dve.scalar_tensor_tensor(out=b, in0=DB[:, 0:GN], scalar=v(V_BMSG), in1=nodes(D0), op0=ALU.mult, op1=ALU.add).then_inc(s_msg, 1)

                def new():
                    dve.wait_ge(s_pn, n + 1)
                    dve.wait_ge(s_sig, 2 * n + 2)
                    dve.scalar_tensor_tensor(out=a, in0=nodes(D1), scalar=v(V_BHN), in1=a, op0=ALU.add, op1=ALU.mult).then_inc(s_gown, 1)
                    dve.wait_ge(s_gown, 3 * n + 1)
                    dve.tensor_tensor(a, a, nodes(D0), ALU.add).then_inc(s_gpre, 1)

                def state1():
                    dve.wait_ge(s_gtanh, n + 1)
                    dve.tensor_tensor(b, h, a, ALU.subtract).then_inc(s_gown, 1)

                def state2():
                    dve.wait_ge(s_gown, 3 * n + 2)
                    dve.tensor_tensor(b, b, C[:, 0:GN], ALU.mult).then_inc(s_gown, 1)

                def state3():
                    dve.wait_ge(s_gown, 3 * n + 3)
                    dve.tensor_tensor(h, a, b, ALU.add).then_inc(s_hnew, 1)
                return [(4, message), (11, new), (15, state1), (16, state2), (17, state3)]

            def gru_dve(s):
                for g in range(NG):
                    ins = splits2(FEAT_GRU0 + s, first_groups("gru", GRU0 + s)) if g == 0 else []
                    if g or not (isinstance(s, int) and s == 0):
                        ins += gru(s * NG + g - 1, (g - 1) % NG)
                    if isinstance(s, int) and s == STEPS - 1 and g:
                        ins += ln_parts(2 * NG + g - 1, 17)
                    build_along("gru", GRU0 + s, g, ins)
                    slow_hots("gru", GRU0 + s, g)

            gru_dve(0)
            with dve.Fori(1, STEPS - 1) as s:
                gru_dve(s)
            gru_dve(STEPS - 1)
            for _, f in gru(STEPS * NG - 1, NG - 1):
                f()
            (_, sums_last), (_, moments_last), (_, scale_last) = ln_parts(3 * NG - 1)
            pre(2, 0)
            sums_last()
            moments_last()
            pre(2, 1)
            scale_last()
            for g in range(2, NG):
                pre(2, g)
            dve.wait_ge(s_pre, 3 * NG)
            for g in range(NG):
                conv(CONV2, g, splits3(7) if g == 0 else ())
            pre(3, NG - 1)
            for g in range(NG):
                conv(CONV3, g, splits3(8, range(1, NG)) if g == 0 else (), 3 * NG)
            ln(4 * NG - 1)
            dve.wait_ge(s_xst, 16 * 3 * NG)
            dve.wait_ge(s_norm, 4 * NG)
            dve.wait_ge(s_w, 80)
            for t in range(TYPES):
                for g in range(NG):
                    build_along("type", TYPE0 + t, g, splits_type(t, range(1 if t else 0, NG)) if g == 0 else ())
                    slow_hots("type", TYPE0 + t, g)

            dve.wait_ge(s_lw, 48)
            mine(dve.tensor_copy(ntf[0:TN], nti[0:TN]))
            for t in range(TYPES):
                mine(dve.tensor_scalar(mask[0:TN, t, :], ntf[0:TN], float(t), None, ALU.is_equal))
            for g in range(NG):
                xb = tiles((X, F)[g % 2], TN)
                dve.wait_ge(s_lx[g % 2], 64 * (g // 2 + 1))
                for i in range(GT):
                    n = g * GT + i
                    y = tmp[0:TN, n % 2, :]
                    xt = xb[:, i, :]
                    dve.wait_ge(s_lo, n + 1)
                    dve.tensor_tensor(y, (D1, D1, D2, D2)[n % 4][0:TN, 512 * (n % 2):512 * (n % 2) + TYPES * D], bnb[0:TN], ALU.add).then_inc(s_lt, 1)
                    dve.wait_ge(s_lt, n + 1)
                    for t in range(TYPES):
                        mine(dve.scalar_tensor_tensor(out=xt, in0=y[:, D * t:D * (t + 1)], scalar=mask[0:TN, t, n:n + 1], in1=xt, op0=ALU.mult, op1=ALU.add))
                dve.tensor_tensor(xb, xb, tiles((D0, AG)[g % 2], TN), ALU.add).then_inc(s_ly, 1)

        @block.scalar
        def _(act):
            act.sem_inc(s_rec, 4)
            act.sem_inc(s_cnt, 2)
            v = lambda k: vec[:, k:k + 1]
            act.wait_ge(s_par, 16)
            act.wait_ge(s_const, 1)
            act.activation(v(V_STD), v(V_VAR), ACT.Sqrt, bias=v(V_EPS)).then_inc(s_vstd, 1)
            act.wait_ge(s_ctm, 1)
            act.copy(ct[:, 0:3, :], D1[:, 512:512 + 3 * NT].rearrange("p (a b) -> p a b", a=3)).then_inc(s_ct, 1)
            act.copy(ct[0:NCP - 3 * P, 3, :], D1[0:NCP - 3 * P, 512 + 3 * NT:512 + 4 * NT]).then_inc(s_ct, 1)

            def ln_std(n):
                act.wait_ge(s_mv, n + 1)
                act.activation(rstd[0:TN, :], mv[0:TN, :, 1], ACT.Sqrt, bias=vec[0:TN, V_EPS:V_EPS + 1]).then_inc(s_std, 1)

            def ln_h(n):
                act.wait_ge(s_hTm, n + 1)
                act.activation(group(hT, n % NG).rearrange("p (t n) -> p t n", t=GT), tiles(D0)[:, :, 0:TN], ACT.Relu).then_inc(s_h, 1)

            def ln_parts(n, at=1):
                return [(at + 4, lambda: ln_std(n)), (at + (10 if at == 1 else 7), lambda: ln_h(n))]

            def encoded(n):
                act.wait_ge(s_enc, n + 1)
                if n > 1:
                    act.wait_ge(s_bnh, n - 1)
                act.activation((A, B)[n % 2][:, 0:GN], nodes(D1), ACT.Relu, bias=v(V_BENC)).then_inc(s_encr, 1)

            between([e for n in range(NG) for e in ((4 * n + 2, lambda n=n: ln_std(n)), (4 * n + 5, lambda n=n: ln_h(n)), (4 * n + 6, lambda n=n: encoded(n)))],
                    lambda j: None)
            act.wait_ge(s_bnh, NG)

            def take(b, r):
                act.wait_ge(s_rmm, b + 3)
                act.copy(rec[:, :, bass.ds(b, 1), :].rearrange("p k a s -> p k (a s)"), D0[:, 512 * r:512 * r + 3 * NT].rearrange("p (k s) -> p k s", k=3)).then_inc(s_rec, 1)
                act.copy(B[:, bass.ds(b * NT, NT)], D0[:, 512 * r + 3 * NT:512 * r + 4 * NT]).then_inc(s_rec, 1)

            with act.Fori(0, NT // 2) as i:
                for r in range(2):
                    take(2 * i + r, r)
            take(NT - 1, 0)

            def step(q, g, j, r):
                act.wait_ge(s_blk, q * BLD + g * NT + j + 3)
                act.copy(adj[0:TN, bass.ds(g * GP + j * GN, GN)].rearrange("p (i n) -> p i n", i=GT), tiles(blocks(q, g, r)[0], TN)[:, :, 0:TN]).then_inc(s_cnt, 1)

            def build_along(kind, p, g, inserts=()):
                if g == NG - 1 and makes_early(kind, p):
                    if kind == "gru":
                        more = parts2(p + 1 - GRU0 + FEAT_GRU0, [0])
                        by = EARLY - NM_AT_GRU[0]
                    else:
                        more = parts_type(p + 1 - TYPE0, [0]) if kind == "type" else parts3(1 if p == CONV0 else 8, [0])
                        by = EARLY - NM_AT[0]
                    inserts = list(inserts) + [(at + by, f) for at, f in more]
                weave(act, inserts, along_step(along(kind, p, g), step))

            def part3(hp, g, src, at, relu=False):
                m = hp * NG + g
                Ht = H[0:TN, :].rearrange("p (t k d) -> p t k d", k=SPLITS, d=D)[:, GT * g:GT * (g + 1)]

                def hi():
                    if relu:
                        act.wait_ge(s_ebias, m - FEAT_TYPE0 * NG + 1)
                        act.activation(Ht[:, :, 0, :], src, ACT.Relu).then_inc(s_hi, 1)
                    else:
                        act.wait_ge(s_nm, m + 1)
                        act.copy(Ht[:, :, 0, :], src).then_inc(s_hi, 1)

                def mid():
                    act.wait_ge(s_r1, mid_of(hp, g) + 1)
                    act.copy(Ht[:, :, 1, :], tiles(A, TN)).then_inc(s_mid, 1)
                return [(at + 1, hi), (at + 4, mid)]

            def parts3(hp, groups=range(NG)):
                return [e for g in groups for e in part3(hp, g, tiles(D0, TN), NM_AT[g])]

            def parts2(hp, groups=range(NG)):
                def hi(g):
                    act.wait_ge(s_nm, hp * NG + g + 1)
                    Ht = H16[0:TN].rearrange("p (t k d) -> p t k d", k=2, d=D)[:, GT * g:GT * (g + 1)]
                    act.copy(Ht[:, :, 0, :], tiles(D2, TN)).then_inc(s_hi, 1)
                return [(NM_AT_GRU[g] + 1, lambda g=g: hi(g)) for g in groups]

            def parts_type(t, groups=range(NG)):
                return [e for g in groups for e in part3(FEAT_TYPE0 + t, g, tiles(C, TN), NM_AT[g] + 2, True)]

            def conv(p, g, bias, relu, inserts=(), n=None):
                if n is not None and g:
                    inserts = ln_parts(n + g - 1)
                build_along("conv", p, g, inserts)
                act.wait_ge(s_aggu, p * NG + g + 1)
                act.activation(group(hT, g), A[:, 0:GN], ACT.Relu if relu else ACT.Identity, bias=v(bias)).then_inc(s_act, 1)

            def in_norms(g):
                cols = slice(g * GT, (g + 1) * GT)
                act.wait_ge(s_degf, g + 1)
                act.activation(dcol[0:TN, 1:3, cols], dcol[0:TN, 1:3, cols], ACT.Sqrt).then_inc(s_degs, 1)

            def norms():
                act.wait_ge(s_degf, NG + 1)
                act.activation(A[0:TN, 192:192 + NT], A[0:TN, 192:192 + NT], ACT.Sqrt).then_inc(s_degs, 1)

            act.wait_ge(s_kp, 1)
            steps(act, (0, 0), step)
            for g in range(NG):
                build_along("deg_in", DEG_IN, g, [(8, lambda g=g: in_norms(g - 1))] if g else ())
            for g in range(NG):
                conv(CONV0, g, V_B01, True, parts3(0) + [(4, lambda: in_norms(NG - 1))] if g == 0 else ())
            for g in range(NG):
                conv(CONV1, g, V_B02, False, parts3(1, range(1, NG)) if g == 0 else (), NG)
            build_along("deg_out", DEG_OUT, 0, ln_parts(2 * NG - 1))
            for g in range(1, NG):
                build_along("deg_out", DEG_OUT, g, parts2(FEAT_GRU0, BY_DEGREES[g]))
            norms()

            def gru(n):
                def r():
                    act.wait_ge(s_prz, n + 1)
                    act.activation(A[:, 0:GN], nodes(D1), ACT.Sigmoid, bias=v(V_BR)).then_inc(s_sig, 1)

                def z():
                    act.activation(C[:, 0:GN], nodes(D0), ACT.Sigmoid, bias=v(V_BZ)).then_inc(s_sig, 1)

                def new():
                    act.wait_ge(s_gpre, n + 1)
                    act.activation(A[:, 0:GN], A[:, 0:GN], ACT.Tanh, bias=v(V_BIN)).then_inc(s_gtanh, 1)
                return [(6, r), (7, z), (11, new)]

            def gru_act(s):
                for g in range(NG):
                    p = GRU0 + s
                    ins = parts2(FEAT_GRU0 + s, first_groups("gru", GRU0 + s)) if g == 0 else []
                    if g or not (isinstance(s, int) and s == 0):
                        ins += gru(s * NG + g - 1)
                    if isinstance(s, int) and s == STEPS - 1 and g:
                        ins += ln_parts(2 * NG + g - 1, 17)
                    build_along("gru", p, g, ins)
                    act.wait_ge(s_agg, p * NG + g + 1)
                    if isinstance(s, int) and s == 0 and g == 0:
                        act.wait_ge(s_xst, 16 * NG)
                        act.wait_ge(s_norm, 2 * NG)
                    else:
                        act.wait_ge(s_pmsg, s * NG + g)
                    if isinstance(s, int) and s == STEPS - 1:
                        act.wait_ge(s_xst, 16 * (NG + g))
                        act.wait_ge(s_norm, 2 * NG + g)
                    act.copy(X[:, 0:GN], nodes(accumulator("gru", p, g)[0])).then_inc(s_aggu, 1)

            gru_act(0)
            with act.Fori(1, STEPS - 1) as s:
                gru_act(s)
            gru_act(STEPS - 1)
            for _, f in gru(STEPS * NG - 1):
                f()
            ln_std(3 * NG - 1)
            ln_h(3 * NG - 1)
            for g in range(NG):
                conv(CONV2, g, V_B21, True, parts3(7) if g == 0 else ())
            for g in range(NG):
                conv(CONV3, g, V_B22, True, parts3(8, range(1, NG)) if g == 0 else (), 3 * NG)
            ln_std(4 * NG - 1)
            ln_h(4 * NG - 1)
            for t in range(TYPES):
                for g in range(NG):
                    p = TYPE0 + t
                    build_along("type", p, g, parts_type(t, range(1 if t else 0, NG)) if g == 0 else ())
                    act.wait_ge(s_agg, p * NG + g + 1)
                    k = t * NG + g
                    if k:
                        act.wait_ge(s_tst, 16 * k)
                    act.copy((B, A)[g % 2][:, 0:GN], nodes(accumulator("type", p, g)[0])).then_inc(s_aggu, 1)


_VECS = ("L0_gnn_b_enc", "L0_gnn_bn_gamma", "L0_gnn_bn_beta", "L0_gnn_bn_mean", "L0_gnn_bn_var", "L0_gnn_b1", "L0_gnn_b2", "L1_gnn_b_msg")


def kernel(**inputs):
    import numpy as np
    import concourse.bacc as bacc
    from concourse.bass_utils import run_bass_kernel_spmd

    a = {k: np.asarray(v) for k, v in inputs.items()}
    vecs = [a[k] for k in _VECS] + list(a["L1_gnn_b_ih"].reshape(3, D)) + list(a["L1_gnn_b_hh"].reshape(3, D)) + [a["L2_gnn_b1"], a["L2_gnn_b2"]]
    ih, hh = a["L1_gnn_W_ih"].reshape(3, D, D), a["L1_gnn_W_hh"].reshape(3, D, D)
    wts = [a["L0_gnn_W_enc"], a["L0_gnn_W1"], a["L0_gnn_W2"], a["L1_gnn_W_msg"].T, *(w.T for w in ih), *(w.T for w in hh),
           a["L2_gnn_W1"], a["L2_gnn_W2"], *(w.T for w in a["L3_gnn_W_e"])]
    wn = a["L3_gnn_W_n"].reshape(3, D, 4, D)
    wts += [wn[t, :, k, :].T for k in range(4) for t in range(3)]
    arrays = {
        "in_x": a["x"], "in_src": a["src"], "in_dst": a["dst"], "in_edge_type": a["edge_type_3"], "in_node_type": a["node_type_3"],
        "in_vecs": np.stack(vecs, 1), "in_weights": np.stack(wts, 1), "in_b_e": a["L3_gnn_b_e"], "in_b_n": a["L3_gnn_b_n"],
    }
    arrays = {k: np.ascontiguousarray(v) for k, v in arrays.items()}
    nc = bacc.Bacc("TRN2", target_bir_lowering=False, num_devices=1)
    args = [nc.dram_tensor(k, v.shape, mybir.dt.from_np(v.dtype), kind="ExternalInput").ap() for k, v in arrays.items()]
    args.append(nc.dram_tensor("out_x", (N, D), F32, kind="ExternalOutput").ap())
    gnn_kernel(nc, *args)
    r = run_bass_kernel_spmd(nc, [arrays], core_ids=[0])
    return r.results[0]["out_x"]
```
